# Optimizing a Trainium2 kernel written in Bass

```python
import numpy as np
import jax
import jax.numpy as jnp

def _softmax(x, axis=-1):
    return jax.nn.softmax(x, axis=axis)

def _gelu(x):
    return jax.nn.gelu(x, approximate=True)

def _silu(x):
    return jax.nn.silu(x)

def _sigmoid(x):
    return jax.nn.sigmoid(x)

def _layernorm(x, axis=-1, eps=1e-05):
    m = jnp.mean(x, axis=axis, keepdims=True)
    v = jnp.var(x, axis=axis, keepdims=True)
    return (x - m) / jnp.sqrt(v + eps)

def _scatter_add(tgt, idx, src, axis=0):
    return tgt.at[idx].add(src)

def _segment_sum(src, seg, n):
    return jax.ops.segment_sum(src, seg, n)
kernel_name = 'mk_xattn_ffn_d4_seqx_r8_dc57b5'

def setup_inputs(seed: int=0):
    np.random.seed(seed)
    _w = jnp.asarray

    def _rec_inputs():
        import jax
        import jax.numpy as jnp
        _rk = jax.random.key(seed)
        x = -0.0002928 + 1 * jax.random.normal(jax.random.fold_in(_rk, 1), (32, 64, 128), jnp.float32)
        _lenS = 64 - jax.random.randint(jax.random.fold_in(_rk, 7), (32,), 0, max(1, 64 // 4) + 1, jnp.int32)
        _lenS2 = 64 - jax.random.randint(jax.random.fold_in(_rk, 8), (32,), 0, max(1, 64 // 4) + 1, jnp.int32)
        _ctx_1024P = jax.random.normal(jax.random.fold_in(_rk, 11), (32, 16, 128), jnp.float32)
        _ctx_1024c = jax.random.dirichlet(jax.random.fold_in(_rk, 511), 0.3 * jnp.ones((16,), jnp.float32), (32, 64))
        _ctx_1024t = jnp.einsum('bsk,bkd->bsd', _ctx_1024c, _ctx_1024P)
        _ctx_1024t = _ctx_1024t * jax.lax.rsqrt(jnp.mean(jnp.square(_ctx_1024t)) + 1e-12) * 0.953939
        ctx_1024 = -1.39393e-06 + 0.999914 * (_ctx_1024t + 0.3 * jax.random.normal(jax.random.fold_in(_rk, 611), (32, 64, 128), jnp.float32))
        _validS = jnp.arange(64)[None, :] < _lenS[:, None]
        _validS2 = jnp.arange(64)[None, :] < _lenS2[:, None]
        _causal = jnp.tril(jnp.ones((64, 64), dtype=bool))
        mask_BxS2_ik0 = jnp.where(jnp.broadcast_to(_validS2[:, :], (32, 64)), 0, 1).astype(jnp.int32)
        mask_Bx1xSxS2_if1 = jnp.where(jnp.ones((32, 1, 64, 64), dtype=bool), 1, 0).astype(jnp.int32)
        mask_BxS2_bk0 = jnp.logical_not(jnp.broadcast_to(_validS2[:, :], (32, 64)))
        return (x, ctx_1024, mask_BxS2_ik0, mask_Bx1xSxS2_if1, mask_BxS2_bk0)
    x, ctx_1024, mask_BxS2_ik0, mask_Bx1xSxS2_if1, mask_BxS2_bk0 = _rec_inputs()

    def _L0_xattn_setup():
        import jax, jax.numpy as jnp
        import numpy as np
        B, S, D, H = (2, 256, 128, 16)
        DK = D // H
        SQRT_DK = DK ** 0.5
        NEG = -1000000000.0
        key = jax.random.key(seed)
        ks = jax.random.split(key, 7)
        scale = 1.0 / np.sqrt(D)
        return {'x': jax.random.normal(ks[0], (B, S, D), jnp.float32), 'encoder_output': jax.random.normal(ks[1], (B, S, D), jnp.float32), 'mask': jax.random.randint(ks[2], (B, S), 0, 2, jnp.int32), 'WQ': jax.random.normal(ks[3], (D, D), jnp.float32) * scale, 'WK': jax.random.normal(ks[4], (D, D), jnp.float32) * scale, 'WV': jax.random.normal(ks[5], (D, D), jnp.float32) * scale, 'WO': jax.random.normal(ks[6], (D, D), jnp.float32) * scale}
    _L0_xattn_all = _L0_xattn_setup()
    _L0_xattn_in = {k: v for k, v in _L0_xattn_all.items() if k in ('WQ', 'WK', 'WV', 'WO')}
    del _L0_xattn_all

    def _L0_ffn_setup():
        import jax, jax.numpy as jnp
        import numpy as np
        D_MODEL, D_FF, RANK = (128, 512, 32)
        B, S = (4, 512)
        key = jax.random.key(seed)
        ks = jax.random.split(key, 7)
        return {'x': jax.random.normal(ks[0], (B, S, D_MODEL), dtype=jnp.float32), 'U1': jax.random.normal(ks[1], (D_MODEL, RANK), dtype=jnp.float32) * 0.02, 'V1': jax.random.normal(ks[2], (RANK, D_FF), dtype=jnp.float32) * 0.02, 'b1': jnp.zeros((D_FF,), dtype=jnp.float32), 'U2': jax.random.normal(ks[3], (D_FF, RANK), dtype=jnp.float32) * 0.02, 'V2': jax.random.normal(ks[4], (RANK, D_MODEL), dtype=jnp.float32) * 0.02, 'b2': jnp.zeros((D_MODEL,), dtype=jnp.float32)}
    _L0_ffn_all = _L0_ffn_setup()
    _L0_ffn_in = {k: v for k, v in _L0_ffn_all.items() if k in ('U1', 'V1', 'b1', 'U2', 'V2', 'b2')}
    del _L0_ffn_all

    def _L1_xattn_setup():
        import jax, jax.numpy as jnp
        import numpy as np
        EMBED = 128
        HEADS = 16
        RANK = 16
        ALPHA = 32
        SCALING = ALPHA / RANK

        def _lora_params(key, d_in, d_out, rank):
            k1, k2, k3 = jax.random.split(key, 3)
            W = jax.random.normal(k1, (d_in, d_out), jnp.float32) * (1.0 / np.sqrt(d_in))
            b = jnp.zeros((d_out,), jnp.float32)
            A = jax.random.normal(k2, (d_in, rank), jnp.float32) * (1.0 / np.sqrt(d_in))
            B = jax.random.normal(k3, (rank, d_out), jnp.float32) * 0.01
            return (W, b, A, B)

        def _lora_linear(x, W, b, A, Bm):
            return x @ W + b + SCALING * (x @ A @ Bm)

        def _attention(q, k, v):
            d = q.shape[-1]
            scale = 1.0 / np.sqrt(d).astype(np.float32)
            scores = jnp.einsum('bhqd,bhkd->bhqk', q, k) * scale
            scores = scores - scores.max(axis=-1, keepdims=True)
            attn = jax.nn.softmax(scores, axis=-1)
            return jnp.einsum('bhqk,bhkd->bhqd', attn, v)
        key = jax.random.key(seed)
        ks = jax.random.split(key, 8)
        B_, L, C = (4, 256, EMBED)
        q_in = jax.random.normal(ks[0], (B_, L, C), jnp.float32)
        k_in = jax.random.normal(ks[1], (B_, L, C), jnp.float32)
        v_in = jax.random.normal(ks[2], (B_, L, C), jnp.float32)
        Wq, bq, Aq, Bq = _lora_params(ks[3], C, EMBED, RANK)
        Wk, bk, Ak, Bk = _lora_params(ks[4], C, EMBED, RANK)
        Wv, bv, Av, Bv = _lora_params(ks[5], C, EMBED, RANK)
        Wo, bo, Ao, Bo = _lora_params(ks[6], EMBED, EMBED, RANK)
        return dict(q_in=q_in, k_in=k_in, v_in=v_in, Wq=Wq, bq=bq, Aq=Aq, Bq=Bq, Wk=Wk, bk=bk, Ak=Ak, Bk=Bk, Wv=Wv, bv=bv, Av=Av, Bv=Bv, Wo=Wo, bo=bo, Ao=Ao, Bo=Bo)
    _L1_xattn_all = _L1_xattn_setup()
    _L1_xattn_in = {k: v for k, v in _L1_xattn_all.items() if k in ('Wq', 'bq', 'Aq', 'Bq', 'Wk', 'bk', 'Ak', 'Bk', 'Wv', 'bv', 'Av', 'Bv', 'Wo', 'bo', 'Ao', 'Bo')}
    del _L1_xattn_all

    def _L1_ffn_setup():
        import jax, jax.numpy as jnp
        import numpy as np
        LORA_DIM = 16
        LORA_TOKEN_INDEX = 1
        B, S, D, H = (4, 256, 128, 512)
        key = jax.random.key(seed)
        ks = jax.random.split(key, 6)
        x = jax.random.normal(ks[0], (B, S, D), dtype=jnp.float32)
        W1 = jax.random.normal(ks[1], (H, D), dtype=jnp.float32) * 0.02
        b1 = jnp.zeros((H,), dtype=jnp.float32)
        W2 = jax.random.normal(ks[2], (D, H), dtype=jnp.float32) * 0.02
        b2 = jnp.zeros((D,), dtype=jnp.float32)
        scale = jnp.asarray(0.001, dtype=jnp.float32)
        return {'x': x, 'W1': W1, 'b1': b1, 'W2': W2, 'b2': b2, 'scale': scale}
    _L1_ffn_all = _L1_ffn_setup()
    _L1_ffn_in = {k: v for k, v in _L1_ffn_all.items() if k in ('W1', 'b1', 'W2', 'b2', 'scale')}
    del _L1_ffn_all

    def _L2_xattn_setup():
        import jax, jax.numpy as jnp
        import numpy as np
        HEADS = 16
        key = jax.random.key(seed)
        ks = jax.random.split(key, 8)
        N, S, E = (2, 256, 128)
        D = E // HEADS
        return {'values': jax.random.normal(ks[0], (N, S, E), jnp.float32), 'keys': jax.random.normal(ks[1], (N, S, E), jnp.float32), 'queries': jax.random.normal(ks[2], (N, S, E), jnp.float32), 'mask': jnp.ones((N, 1, S, S), jnp.int32), 'Wv': jax.random.normal(ks[3], (D, D), jnp.float32) * D ** (-0.5), 'Wk': jax.random.normal(ks[4], (D, D), jnp.float32) * D ** (-0.5), 'Wq': jax.random.normal(ks[5], (D, D), jnp.float32) * D ** (-0.5), 'Wo': jax.random.normal(ks[6], (E, E), jnp.float32) * E ** (-0.5), 'bo': jnp.zeros((E,), jnp.float32)}
    _L2_xattn_all = _L2_xattn_setup()
    _L2_xattn_in = {k: v for k, v in _L2_xattn_all.items() if k in ('Wv', 'Wk', 'Wq', 'Wo', 'bo')}
    del _L2_xattn_all

    def _L2_ffn_setup():
        import jax, jax.numpy as jnp
        import numpy as np
        DIM = 128
        HEADS = 16
        HD = DIM // HEADS
        M = 32
        E = 4
        K = 2
        HID = 256
        MID = 256
        LB = 0.01
        EPS = 1.1920929e-07

        def _rms(x, w):
            return x * jax.lax.rsqrt(jnp.mean(x * x, axis=-1, keepdims=True) + EPS) * w

        def _gelu(x):
            return jax.nn.gelu(x, approximate=False)
        key = jax.random.key(seed)
        ks = jax.random.split(key, 20)
        d = DIM
        w = lambda k, s: jax.random.normal(k, s, jnp.float32) * 0.02
        return {'x': jax.random.normal(ks[0], (4, 128, d), jnp.float32), 'n1_w': jnp.ones((d,), jnp.float32), 'n2_w': jnp.ones((d,), jnp.float32), 'wq': w(ks[1], (d, d)), 'wk': w(ks[2], (d, d)), 'wv': w(ks[3], (d, d)), 'wo': w(ks[4], (d, d)), 'qn_w': jnp.ones((HD,), jnp.float32), 'kn_w': jnp.ones((HD,), jnp.float32), 'gate_w': w(ks[5], (E, d)), 'e0_up': w(ks[6], (HID, d)), 'e0_down': w(ks[7], (d, HID)), 'e1_w1': w(ks[8], (HID, d)), 'e1_w2': w(ks[9], (HID, d)), 'e1_down': w(ks[10], (d, HID)), 'e2_l1': w(ks[11], (MID, d)), 'e2_l2': w(ks[12], (HID, MID)), 'e2_l3': w(ks[13], (MID, HID)), 'e2_l4': w(ks[14], (d, MID)), 'e3_down': w(ks[15], (d, d)), 'e3_up': w(ks[16], (HID, d)), 'e3_out': w(ks[17], (d, HID))}
    _L2_ffn_all = _L2_ffn_setup()
    _L2_ffn_in = {k: v for k, v in _L2_ffn_all.items() if k in ('n1_w', 'n2_w', 'wq', 'wk', 'wv', 'wo', 'qn_w', 'kn_w', 'gate_w', 'e0_up', 'e0_down', 'e1_w1', 'e1_w2', 'e1_down', 'e2_l1', 'e2_l2', 'e2_l3', 'e2_l4', 'e3_down', 'e3_up', 'e3_out')}
    del _L2_ffn_all

    def _L3_xattn_setup():
        import jax, jax.numpy as jnp
        import numpy as np
        DIM = 128
        DIM_LATENT = 128
        DIM_HEAD = 64
        INNER = max(DIM, DIM_LATENT)
        HEADS = INNER // DIM_HEAD
        SCALE = DIM_HEAD ** (-0.5)
        LN_EPS = 1e-05
        RMS_EPS = 1e-08

        def layernorm(x, g, b):
            mu = jnp.mean(x, axis=-1, keepdims=True)
            var = jnp.mean(jnp.square(x - mu), axis=-1, keepdims=True)
            return (x - mu) * jax.lax.rsqrt(var + LN_EPS) * g + b

        def rmsnorm(x, gamma):
            n = jnp.linalg.norm(x, axis=-1, keepdims=True) * x.shape[-1] ** (-0.5)
            return x / jnp.maximum(n, RMS_EPS) * gamma
        key = jax.random.key(seed)
        ks = jax.random.split(key, 8)
        b, n, nl = (8, 256, 64)
        x = jax.random.normal(ks[0], (b, n, DIM), dtype=jnp.float32)
        latents = jax.random.normal(ks[1], (b, nl, DIM_LATENT), dtype=jnp.float32)
        mask = jax.random.randint(ks[2], (b, n), 0, 2).astype(bool)
        init = lambda k, shape, fan_in: jax.random.normal(k, shape, jnp.float32) * fan_in ** (-0.5)
        return {'x': x, 'latents': latents, 'mask': mask, 'ln_x_g': jnp.ones((DIM,), jnp.float32), 'ln_x_b': jnp.zeros((DIM,), jnp.float32), 'ln_l_g': jnp.ones((DIM_LATENT,), jnp.float32), 'ln_l_b': jnp.zeros((DIM_LATENT,), jnp.float32), 'q_gamma': jnp.ones((DIM_HEAD,), jnp.float32), 'k_gamma': jnp.ones((DIM_HEAD,), jnp.float32), 'W_q': init(ks[3], (DIM_LATENT, INNER), DIM_LATENT), 'W_kv': init(ks[4], (DIM, 2 * INNER), DIM), 'W_out': init(ks[5], (INNER, DIM_LATENT), INNER), 'b_out': jnp.zeros((DIM_LATENT,), jnp.float32)}
    _L3_xattn_all = _L3_xattn_setup()
    _L3_xattn_in = {k: v for k, v in _L3_xattn_all.items() if k in ('ln_x_g', 'ln_x_b', 'ln_l_g', 'ln_l_b', 'q_gamma', 'k_gamma', 'W_q', 'W_kv', 'W_out', 'b_out')}
    del _L3_xattn_all

    def _L3_ffn_setup():
        import jax, jax.numpy as jnp
        import numpy as np
        NUM_EXPERTS = 8
        HIDDEN = 128
        FFN = 512
        BATCH = 2
        SEQ = 256
        key = jax.random.key(seed)
        k_x, k_g, k_u, k_d = jax.random.split(key, 4)
        scale_in = 1.0 / np.sqrt(HIDDEN)
        scale_mid = 1.0 / np.sqrt(FFN)
        return {'hidden_states': jax.random.normal(k_x, (BATCH, SEQ, HIDDEN), dtype=jnp.float32), 'Wg': jax.random.normal(k_g, (NUM_EXPERTS, HIDDEN, FFN), dtype=jnp.float32) * scale_in, 'Wu': jax.random.normal(k_u, (NUM_EXPERTS, HIDDEN, FFN), dtype=jnp.float32) * scale_in, 'Wd': jax.random.normal(k_d, (NUM_EXPERTS, FFN, HIDDEN), dtype=jnp.float32) * scale_mid}
    _L3_ffn_all = _L3_ffn_setup()
    _L3_ffn_in = {k: v for k, v in _L3_ffn_all.items() if k in ('Wg', 'Wu', 'Wd')}
    del _L3_ffn_all
    return {'x': x, 'ctx_1024': ctx_1024, 'mask_BxS2_ik0': mask_BxS2_ik0, 'mask_Bx1xSxS2_if1': mask_Bx1xSxS2_if1, 'mask_BxS2_bk0': mask_BxS2_bk0, 'L0_xattn_WQ': _L0_xattn_in['WQ'], 'L0_xattn_WK': _L0_xattn_in['WK'], 'L0_xattn_WV': _L0_xattn_in['WV'], 'L0_xattn_WO': _L0_xattn_in['WO'], 'L0_ffn_U1': _L0_ffn_in['U1'], 'L0_ffn_V1': _L0_ffn_in['V1'], 'L0_ffn_b1': _L0_ffn_in['b1'], 'L0_ffn_U2': _L0_ffn_in['U2'], 'L0_ffn_V2': _L0_ffn_in['V2'], 'L0_ffn_b2': _L0_ffn_in['b2'], 'L1_xattn_Wq': _L1_xattn_in['Wq'], 'L1_xattn_bq': _L1_xattn_in['bq'], 'L1_xattn_Aq': _L1_xattn_in['Aq'], 'L1_xattn_Bq': _L1_xattn_in['Bq'], 'L1_xattn_Wk': _L1_xattn_in['Wk'], 'L1_xattn_bk': _L1_xattn_in['bk'], 'L1_xattn_Ak': _L1_xattn_in['Ak'], 'L1_xattn_Bk': _L1_xattn_in['Bk'], 'L1_xattn_Wv': _L1_xattn_in['Wv'], 'L1_xattn_bv': _L1_xattn_in['bv'], 'L1_xattn_Av': _L1_xattn_in['Av'], 'L1_xattn_Bv': _L1_xattn_in['Bv'], 'L1_xattn_Wo': _L1_xattn_in['Wo'], 'L1_xattn_bo': _L1_xattn_in['bo'], 'L1_xattn_Ao': _L1_xattn_in['Ao'], 'L1_xattn_Bo': _L1_xattn_in['Bo'], 'L1_ffn_W1': _L1_ffn_in['W1'], 'L1_ffn_b1': _L1_ffn_in['b1'], 'L1_ffn_W2': _L1_ffn_in['W2'], 'L1_ffn_b2': _L1_ffn_in['b2'], 'L1_ffn_scale': _L1_ffn_in['scale'], 'L2_xattn_Wv': _L2_xattn_in['Wv'], 'L2_xattn_Wk': _L2_xattn_in['Wk'], 'L2_xattn_Wq': _L2_xattn_in['Wq'], 'L2_xattn_Wo': _L2_xattn_in['Wo'], 'L2_xattn_bo': _L2_xattn_in['bo'], 'L2_ffn_n1_w': _L2_ffn_in['n1_w'], 'L2_ffn_n2_w': _L2_ffn_in['n2_w'], 'L2_ffn_wq': _L2_ffn_in['wq'], 'L2_ffn_wk': _L2_ffn_in['wk'], 'L2_ffn_wv': _L2_ffn_in['wv'], 'L2_ffn_wo': _L2_ffn_in['wo'], 'L2_ffn_qn_w': _L2_ffn_in['qn_w'], 'L2_ffn_kn_w': _L2_ffn_in['kn_w'], 'L2_ffn_gate_w': _L2_ffn_in['gate_w'], 'L2_ffn_e0_up': _L2_ffn_in['e0_up'], 'L2_ffn_e0_down': _L2_ffn_in['e0_down'], 'L2_ffn_e1_w1': _L2_ffn_in['e1_w1'], 'L2_ffn_e1_w2': _L2_ffn_in['e1_w2'], 'L2_ffn_e1_down': _L2_ffn_in['e1_down'], 'L2_ffn_e2_l1': _L2_ffn_in['e2_l1'], 'L2_ffn_e2_l2': _L2_ffn_in['e2_l2'], 'L2_ffn_e2_l3': _L2_ffn_in['e2_l3'], 'L2_ffn_e2_l4': _L2_ffn_in['e2_l4'], 'L2_ffn_e3_down': _L2_ffn_in['e3_down'], 'L2_ffn_e3_up': _L2_ffn_in['e3_up'], 'L2_ffn_e3_out': _L2_ffn_in['e3_out'], 'L3_xattn_ln_x_g': _L3_xattn_in['ln_x_g'], 'L3_xattn_ln_x_b': _L3_xattn_in['ln_x_b'], 'L3_xattn_ln_l_g': _L3_xattn_in['ln_l_g'], 'L3_xattn_ln_l_b': _L3_xattn_in['ln_l_b'], 'L3_xattn_q_gamma': _L3_xattn_in['q_gamma'], 'L3_xattn_k_gamma': _L3_xattn_in['k_gamma'], 'L3_xattn_W_q': _L3_xattn_in['W_q'], 'L3_xattn_W_kv': _L3_xattn_in['W_kv'], 'L3_xattn_W_out': _L3_xattn_in['W_out'], 'L3_xattn_b_out': _L3_xattn_in['b_out'], 'L3_ffn_Wg': _L3_ffn_in['Wg'], 'L3_ffn_Wu': _L3_ffn_in['Wu'], 'L3_ffn_Wd': _L3_ffn_in['Wd']}

def reference(x, ctx_1024, mask_BxS2_ik0, mask_Bx1xSxS2_if1, mask_BxS2_bk0, L0_xattn_WQ, L0_xattn_WK, L0_xattn_WV, L0_xattn_WO, L0_ffn_U1, L0_ffn_V1, L0_ffn_b1, L0_ffn_U2, L0_ffn_V2, L0_ffn_b2, L1_xattn_Wq, L1_xattn_bq, L1_xattn_Aq, L1_xattn_Bq, L1_xattn_Wk, L1_xattn_bk, L1_xattn_Ak, L1_xattn_Bk, L1_xattn_Wv, L1_xattn_bv, L1_xattn_Av, L1_xattn_Bv, L1_xattn_Wo, L1_xattn_bo, L1_xattn_Ao, L1_xattn_Bo, L1_ffn_W1, L1_ffn_b1, L1_ffn_W2, L1_ffn_b2, L1_ffn_scale, L2_xattn_Wv, L2_xattn_Wk, L2_xattn_Wq, L2_xattn_Wo, L2_xattn_bo, L2_ffn_n1_w, L2_ffn_n2_w, L2_ffn_wq, L2_ffn_wk, L2_ffn_wv, L2_ffn_wo, L2_ffn_qn_w, L2_ffn_kn_w, L2_ffn_gate_w, L2_ffn_e0_up, L2_ffn_e0_down, L2_ffn_e1_w1, L2_ffn_e1_w2, L2_ffn_e1_down, L2_ffn_e2_l1, L2_ffn_e2_l2, L2_ffn_e2_l3, L2_ffn_e2_l4, L2_ffn_e3_down, L2_ffn_e3_up, L2_ffn_e3_out, L3_xattn_ln_x_g, L3_xattn_ln_x_b, L3_xattn_ln_l_g, L3_xattn_ln_l_b, L3_xattn_q_gamma, L3_xattn_k_gamma, L3_xattn_W_q, L3_xattn_W_kv, L3_xattn_W_out, L3_xattn_b_out, L3_ffn_Wg, L3_ffn_Wu, L3_ffn_Wd):
    import jax
    import jax.numpy as jnp

    def _L0_xattn_ref(x, encoder_output, mask, WQ, WK, WV, WO):
        import jax, jax.numpy as jnp
        import numpy as np
        B, S, D, H = (2, 256, 128, 16)
        DK = D // H
        SQRT_DK = DK ** 0.5
        NEG = -1000000000.0
        b, s, d = x.shape
        q = (x @ WQ).reshape(b, s, H, DK).transpose(0, 2, 1, 3)
        k = (encoder_output @ WK).reshape(b, s, H, DK).transpose(0, 2, 1, 3)
        v = (encoder_output @ WV).reshape(b, s, H, DK).transpose(0, 2, 1, 3)
        scores = jnp.einsum('bhqd,bhkd->bhqk', q, k) / SQRT_DK
        future = jnp.triu(jnp.ones((s, s), jnp.int32), 1)
        m = mask[:, None, :, None] + future[None, None, :, :]
        scores = jnp.where(m != 0, NEG, scores)
        attn = jax.nn.softmax(scores, axis=-1)
        ctx = jnp.einsum('bhqk,bhkd->bqhd', attn, v).reshape(b, s, d)
        return ctx @ WO

    def _L0_ffn_ref(x, U1, V1, b1, U2, V2, b2):
        import jax, jax.numpy as jnp
        import numpy as np
        D_MODEL, D_FF, RANK = (128, 512, 32)
        B, S = (4, 512)
        P = jnp.einsum('bsd,dr->bsr', x, U1)
        H = jax.nn.gelu(jnp.einsum('bsr,rf->bsf', P, V1) + b1)
        Q = jnp.einsum('bsf,fr->bsr', H, U2)
        return jnp.einsum('bsr,rd->bsd', Q, V2) + b2

    def _L1_xattn_ref(q_in, k_in, v_in, Wq, bq, Aq, Bq, Wk, bk, Ak, Bk, Wv, bv, Av, Bv, Wo, bo, Ao, Bo):
        import jax, jax.numpy as jnp
        import numpy as np
        EMBED = 128
        HEADS = 16
        RANK = 16
        ALPHA = 32
        SCALING = ALPHA / RANK

        def _lora_params(key, d_in, d_out, rank):
            k1, k2, k3 = jax.random.split(key, 3)
            W = jax.random.normal(k1, (d_in, d_out), jnp.float32) * (1.0 / np.sqrt(d_in))
            b = jnp.zeros((d_out,), jnp.float32)
            A = jax.random.normal(k2, (d_in, rank), jnp.float32) * (1.0 / np.sqrt(d_in))
            B = jax.random.normal(k3, (rank, d_out), jnp.float32) * 0.01
            return (W, b, A, B)

        def _lora_linear(x, W, b, A, Bm):
            return x @ W + b + SCALING * (x @ A @ Bm)

        def _attention(q, k, v):
            d = q.shape[-1]
            scale = 1.0 / np.sqrt(d).astype(np.float32)
            scores = jnp.einsum('bhqd,bhkd->bhqk', q, k) * scale
            scores = scores - scores.max(axis=-1, keepdims=True)
            attn = jax.nn.softmax(scores, axis=-1)
            return jnp.einsum('bhqk,bhkd->bhqd', attn, v)
        B_, L, C = q_in.shape
        hd = EMBED // HEADS
        q = _lora_linear(q_in, Wq, bq, Aq, Bq).reshape(B_, L, HEADS, hd).transpose(0, 2, 1, 3)
        k = _lora_linear(k_in, Wk, bk, Ak, Bk).reshape(B_, L, HEADS, hd).transpose(0, 2, 1, 3)
        v = _lora_linear(v_in, Wv, bv, Av, Bv).reshape(B_, L, HEADS, hd).transpose(0, 2, 1, 3)
        y = _attention(q, k, v)
        y = y.transpose(0, 2, 1, 3).reshape(B_, L, C)
        return _lora_linear(y, Wo, bo, Ao, Bo)

    def _L1_ffn_ref(x, W1, b1, W2, b2, scale):
        import jax, jax.numpy as jnp
        import numpy as np
        LORA_DIM = 16
        LORA_TOKEN_INDEX = 1
        B, S, D, H = (4, 256, 128, 512)
        Bx, Sx, Dx = x.shape
        Hx = W1.shape[0]
        lt = jax.lax.dynamic_slice_in_dim(x, LORA_TOKEN_INDEX, LORA_DIM, axis=1)
        even = lt[:, ::2, :]
        odd = lt[:, 1::2, :]
        m1 = (even[:, :4, :, None] * odd[:, :4, None, :]).reshape(Bx, Hx, Dx)
        m2 = (even[:, 4:, :, None] * odd[:, 4:, None, :]).reshape(Bx, Dx, Hx)
        h = jnp.einsum('bsd,hd->bsh', x, W1) + scale * jnp.einsum('bsd,bhd->bsh', x, m1) + b1
        h = jax.nn.gelu(h, approximate=False)
        out = jnp.einsum('bsh,oh->bso', h, W2) + scale * jnp.einsum('bsh,boh->bso', h, m2) + b2
        return out

    def _L2_xattn_ref(values, keys, queries, mask, Wv, Wk, Wq, Wo, bo):
        import jax, jax.numpy as jnp
        import numpy as np
        HEADS = 16
        N, Sq, E = queries.shape
        H = HEADS
        D = E // H
        v = values.reshape(N, -1, H, D)
        k = keys.reshape(N, -1, H, D)
        q = queries.reshape(N, Sq, H, D)
        v = jnp.einsum('nlhd,od->nlho', v, Wv)
        k = jnp.einsum('nlhd,od->nlho', k, Wk)
        q = jnp.einsum('nqhd,od->nqho', q, Wq)
        energy = jnp.einsum('nqhd,nkhd->nhqk', q, k)
        energy = jnp.where(mask == 0, jnp.float32(-1e+20), energy)
        attn = jax.nn.softmax(energy * (1.0 / E ** 0.5), axis=3)
        out = jnp.einsum('nhqk,nkhd->nqhd', attn, v).reshape(N, Sq, E)
        return out @ Wo.T + bo

    def _L2_ffn_ref(x, n1_w, n2_w, wq, wk, wv, wo, qn_w, kn_w, gate_w, e0_up, e0_down, e1_w1, e1_w2, e1_down, e2_l1, e2_l2, e2_l3, e2_l4, e3_down, e3_up, e3_out):
        import jax, jax.numpy as jnp
        import numpy as np
        DIM = 128
        HEADS = 16
        HD = DIM // HEADS
        M = 32
        E = 4
        K = 2
        HID = 256
        MID = 256
        LB = 0.01
        EPS = 1.1920929e-07

        def _rms(x, w):
            return x * jax.lax.rsqrt(jnp.mean(x * x, axis=-1, keepdims=True) + EPS) * w

        def _gelu(x):
            return jax.nn.gelu(x, approximate=False)
        B, T, C = x.shape
        h = _rms(x, n1_w)
        heads = lambda w_: (h @ w_.T).reshape(B, T, HEADS, HD).transpose(0, 2, 1, 3)
        q = _rms(heads(wq), qn_w)
        k = _rms(heads(wk), kn_w)
        v = heads(wv)
        scores = jnp.einsum('bhqd,bhkd->bhqk', q, k) * HD ** (-0.5)
        causal = jnp.tril(jnp.ones((T, T), bool))
        scores = jnp.where(causal[None, None], scores, -jnp.inf)
        attn = jax.nn.softmax(scores, axis=-1)
        ao = jnp.einsum('bhqk,bhkd->bhqd', attn, v).transpose(0, 2, 1, 3).reshape(B, T, C) @ wo.T
        ao = ao.at[:, :, :M].set(0.0)
        x = x + ao
        xf = _rms(x, n2_w).reshape(-1, C)
        N = xf.shape[0]
        logits = jnp.nan_to_num(xf @ gate_w.T)
        probs = jax.nn.softmax(logits, axis=-1)
        topv, topi = jax.lax.top_k(probs, K)
        topv = topv / (topv.sum(-1, keepdims=True) + 1e-08)
        wts = jnp.zeros((N, E), x.dtype).at[jnp.arange(N)[:, None], topi].add(topv)
        o0 = _gelu(xf @ e0_up.T) @ e0_down.T
        o1 = jax.nn.silu(xf @ e1_w1.T) * (xf @ e1_w2.T) @ e1_down.T
        o2 = _gelu(_gelu(_gelu(xf @ e2_l1.T) @ e2_l2.T) @ e2_l3.T) @ e2_l4.T
        o3 = _gelu(_gelu(xf @ e3_down.T) @ e3_up.T) @ e3_out.T
        moe = wts[:, 0:1] * o0 + wts[:, 1:2] * o1 + wts[:, 2:3] * o2 + wts[:, 3:4] * o3
        moe = moe.reshape(B, T, C).at[:, :, :M].set(0.0)
        return x + moe

    def _L3_xattn_ref(x, latents, mask, ln_x_g, ln_x_b, ln_l_g, ln_l_b, q_gamma, k_gamma, W_q, W_kv, W_out, b_out):
        import jax, jax.numpy as jnp
        import numpy as np
        DIM = 128
        DIM_LATENT = 128
        DIM_HEAD = 64
        INNER = max(DIM, DIM_LATENT)
        HEADS = INNER // DIM_HEAD
        SCALE = DIM_HEAD ** (-0.5)
        LN_EPS = 1e-05
        RMS_EPS = 1e-08

        def layernorm(x, g, b):
            mu = jnp.mean(x, axis=-1, keepdims=True)
            var = jnp.mean(jnp.square(x - mu), axis=-1, keepdims=True)
            return (x - mu) * jax.lax.rsqrt(var + LN_EPS) * g + b

        def rmsnorm(x, gamma):
            n = jnp.linalg.norm(x, axis=-1, keepdims=True) * x.shape[-1] ** (-0.5)
            return x / jnp.maximum(n, RMS_EPS) * gamma
        b, n, _ = x.shape
        nl = latents.shape[1]
        xn = layernorm(x, ln_x_g, ln_x_b)
        ln = layernorm(latents, ln_l_g, ln_l_b)
        q = ln @ W_q
        kv = jnp.concatenate([xn @ W_kv, ln @ W_kv], axis=1)
        k, v = (kv[..., :INNER], kv[..., INNER:])
        to_heads = lambda t: t.reshape(t.shape[0], t.shape[1], HEADS, DIM_HEAD).transpose(0, 2, 1, 3)
        q, k, v = (to_heads(q), to_heads(k), to_heads(v))
        qn = rmsnorm(q, q_gamma) * SCALE
        kn = rmsnorm(k, k_gamma)
        sim = jnp.einsum('bhid,bhjd->bhij', qn, kn)
        full_mask = jnp.pad(mask, ((0, 0), (0, nl)), constant_values=True)
        neg = -jnp.finfo(sim.dtype).max
        sim = jnp.where(full_mask[:, None, None, :], sim, neg)
        attn = jax.nn.softmax(sim.astype(jnp.float32), axis=-1).astype(sim.dtype)
        out = jnp.einsum('bhij,bhjd->bhid', attn, v)
        out = out.transpose(0, 2, 1, 3).reshape(b, nl, INNER)
        return out @ W_out + b_out

    def _L3_ffn_ref(hidden_states, Wg, Wu, Wd):
        import jax, jax.numpy as jnp
        import numpy as np
        NUM_EXPERTS = 8
        HIDDEN = 128
        FFN = 512
        BATCH = 2
        SEQ = 256
        B, S, H = hidden_states.shape
        x = hidden_states.reshape(-1, H)

        def expert_step(acc, w):
            wg, wu, wd = w
            h = jax.nn.silu(x @ wg) * (x @ wu)
            return (acc + h @ wd, None)
        acc, _ = jax.lax.scan(expert_step, jnp.zeros_like(x), (Wg, Wu, Wd))
        return acc.reshape(B, S, H)
    x = x + _L0_xattn_ref(_layernorm(x, axis=-1), ctx_1024, mask_BxS2_ik0, L0_xattn_WQ, L0_xattn_WK, L0_xattn_WV, L0_xattn_WO)
    x = x + _L0_ffn_ref(_layernorm(x, axis=-1), L0_ffn_U1, L0_ffn_V1, L0_ffn_b1, L0_ffn_U2, L0_ffn_V2, L0_ffn_b2)
    x = x + _L1_xattn_ref(_layernorm(x, axis=-1), ctx_1024, ctx_1024, L1_xattn_Wq, L1_xattn_bq, L1_xattn_Aq, L1_xattn_Bq, L1_xattn_Wk, L1_xattn_bk, L1_xattn_Ak, L1_xattn_Bk, L1_xattn_Wv, L1_xattn_bv, L1_xattn_Av, L1_xattn_Bv, L1_xattn_Wo, L1_xattn_bo, L1_xattn_Ao, L1_xattn_Bo)
    x = x + _L1_ffn_ref(_layernorm(x, axis=-1), L1_ffn_W1, L1_ffn_b1, L1_ffn_W2, L1_ffn_b2, L1_ffn_scale)
    x = x + _L2_xattn_ref(ctx_1024, ctx_1024, _layernorm(x, axis=-1), mask_Bx1xSxS2_if1, L2_xattn_Wv, L2_xattn_Wk, L2_xattn_Wq, L2_xattn_Wo, L2_xattn_bo)
    x = x + _L2_ffn_ref(_layernorm(x, axis=-1), L2_ffn_n1_w, L2_ffn_n2_w, L2_ffn_wq, L2_ffn_wk, L2_ffn_wv, L2_ffn_wo, L2_ffn_qn_w, L2_ffn_kn_w, L2_ffn_gate_w, L2_ffn_e0_up, L2_ffn_e0_down, L2_ffn_e1_w1, L2_ffn_e1_w2, L2_ffn_e1_down, L2_ffn_e2_l1, L2_ffn_e2_l2, L2_ffn_e2_l3, L2_ffn_e2_l4, L2_ffn_e3_down, L2_ffn_e3_up, L2_ffn_e3_out)
    x = x + _L3_xattn_ref(ctx_1024, _layernorm(x, axis=-1), mask_BxS2_bk0, L3_xattn_ln_x_g, L3_xattn_ln_x_b, L3_xattn_ln_l_g, L3_xattn_ln_l_b, L3_xattn_q_gamma, L3_xattn_k_gamma, L3_xattn_W_q, L3_xattn_W_kv, L3_xattn_W_out, L3_xattn_b_out)
    x = x + _L3_ffn_ref(_layernorm(x, axis=-1), L3_ffn_Wg, L3_ffn_Wu, L3_ffn_Wd)
    return x

_drawn_inputs = setup_inputs


def setup_inputs(seed=0):
    import zlib

    import numpy as np

    out = dict(_drawn_inputs(seed))
    spreads = {'L0_ffn_b1': (0.0, 0.8),
     'L0_ffn_b2': (0.0, 0.1),
     'L1_xattn_bq': (0.0, 0.382),
     'L1_xattn_bk': (0.0, 2.0),
     'L1_xattn_bv': (0.0, 0.1),
     'L1_xattn_bo': (0.0, 0.1),
     'L1_ffn_b1': (0.0, 0.397),
     'L1_ffn_b2': (0.0, 0.1),
     'L2_xattn_bo': (0.0, 0.1),
     'L2_ffn_n1_w': (1.0, 0.6),
     'L2_ffn_n2_w': (1.0, 0.6),
     'L2_ffn_qn_w': (1.0, 0.6),
     'L2_ffn_kn_w': (1.0, 0.6),
     'L3_xattn_ln_x_g': (1.0, 0.6),
     'L3_xattn_ln_x_b': (0.0, 2.0),
     'L3_xattn_ln_l_g': (1.0, 0.6),
     'L3_xattn_ln_l_b': (0.0, 0.8),
     'L3_xattn_q_gamma': (1.0, 0.6),
     'L3_xattn_k_gamma': (1.0, 0.6),
     'L3_xattn_b_out': (0.0, 0.745)}
    factors = {'L0_ffn_U1': 8.0,
     'L0_ffn_V1': 8.0,
     'L0_ffn_U2': 8.0,
     'L0_ffn_V2': 8.0,
     'L1_xattn_Aq': 3.509,
     'L1_xattn_Bq': 3.512,
     'L1_xattn_Ak': 3.284,
     'L1_xattn_Bk': 3.315,
     'L2_ffn_wq': 8.0,
     'L2_ffn_wk': 8.0,
     'L2_ffn_wv': 3.312,
     'L2_ffn_wo': 3.401,
     'L2_ffn_gate_w': 8.0,
     'L2_ffn_e0_up': 8.0,
     'L2_ffn_e0_down': 8.0,
     'L2_ffn_e1_w1': 8.0,
     'L2_ffn_e1_w2': 8.0,
     'L2_ffn_e1_down': 8.0,
     'L2_ffn_e2_l1': 8.0,
     'L2_ffn_e2_l2': 8.0,
     'L2_ffn_e2_l3': 8.0,
     'L2_ffn_e2_l4': 8.0,
     'L2_ffn_e3_down': 8.0,
     'L2_ffn_e3_up': 8.0,
     'L2_ffn_e3_out': 8.0}
    for name, (base, spread) in spreads.items():
        noise = np.random.default_rng([zlib.crc32(name.encode()), seed]).standard_normal(out[name].shape)
        drawn = base * np.exp(spread * noise) if base else spread * noise
        out[name] = jnp.asarray(drawn.astype(out[name].dtype))
    for name, factor in factors.items():
        out[name] = (out[name] * factor).astype(out[name].dtype)
    return out
```

```python
from contextlib import ExitStack

import concourse.bass as bass
from concourse import mybir

P = 128
B, S, D = 32, 64, 128
NPAIR = B * S // P
NG = 4
PPG = NPAIR // NG
BPG = B // NG
GT = PPG * P
F32 = mybir.dt.float32
BF16 = mybir.dt.bfloat16
ALU = mybir.AluOpType
ACT = mybir.ActivationFunctionType
AX = mybir.AxisListType.X

LN_EPS, RMS_EPS, RMS3_EPS = 1e-5, 1.1920929e-07, 1e-8
FLT_MAX = 3.4028234e38

L0A, L0F, L1A, L1F, L2A, L2F, L2M, L3A, L3F = range(9)
ATT = {L0A: 0, L1A: 1, L2A: 2, L2F: 3, L3A: 4}
NORMS = [1, 1, 1, 1, 1, 2, 1, 3, 1]
TURNS = [1, 1, 1, 1, 1, 1, 1, 2, 1]


def before(counts, k):
    return NG * sum(counts[:k])


X_UPS = [NPAIR if k in ATT else NG for k in range(9)]


def x_after(k):
    return sum(X_UPS[:k + 1])


PACK = [("L0_WQ", 128), ("L0_WK", 128), ("L0_WV", 128), ("L0_WO", 128),
        ("U1", 32), ("V1", 512), ("U2", 128), ("V2", 128),
        ("L1_Wq", 128), ("L1_Wk", 128), ("L1_Wv", 128), ("L1_Wo", 128),
        ("W1T", 512), ("W2T", 512),
        ("L2_q", 8), ("L2_k", 8), ("L2_v", 8), ("L2_WoT", 128),
        ("wqkT", 256), ("wvT", 128), ("woT", 128), ("gateT", 4),
        ("e0_up", 256), ("e0_down", 256), ("e1_w1", 256), ("e1_w2", 256), ("e1_down", 256),
        ("e2_l1", 256), ("e2_l2", 512), ("e2_l3", 512), ("e2_l4", 256),
        ("e3_down", 128), ("e3_up", 256), ("e3_out", 256),
        ("L3_Wq", 128), ("L3_Wkv", 256), ("L3_Wout", 128),
        ("c_L0b1", 4), ("c_L0b2", 1), ("c_bq", 1), ("c_bk", 1), ("c_bv", 1),
        ("c_L1b1", 4), ("c_L1b2", 1), ("c_n1", 1), ("c_n2", 1), ("c_qn", 1), ("c_kn", 1),
        ("c_lxg", 1), ("c_lxb", 1), ("c_llg", 1), ("c_llb", 1), ("c_qg", 1), ("c_kg", 1),
        ("c_scale", 1)]
OFF = {}
_at = 0
for _n, _w in PACK:
    OFF[_n] = (_at, _w)
    _at += _w
NPACK = _at


MOE_CHUNKS = [("e2_l1", 0, 0), ("e2_l1", 1, 1), ("e3_down", 0, 2), ("e0_up", 0, 8), ("e0_up", 1, 9),
              ("e2_l2", 0, 6), ("e2_l2", 1, 7), ("e3_up", 0, 10), ("e3_up", 1, 11),
              ("e2_l3", 0, 0), ("e2_l3", 1, 1),
              ("e1_w1", 0, 4), ("e1_w2", 0, None), ("e1_w1", 1, 5), ("e1_w2", 1, None)]
MOE_IN = {"e2_l2": ([0, 1], 1), "e2_l3": ([6, 7], 6), "e3_up": ([2], 2)}
MOE_OUTS = [(6, 0, "e0_down", (8, 9), 4), (12, 3, "e3_out", (10, 11), 8),
            (14, 2, "e2_l4", (0, 1), 10), (14, 1, "e1_down", (4, 5), 13)]
NCH = len(MOE_CHUNKS)


def acts_through(n):
    return sum(dst is not None for _, _, dst in MOE_CHUNKS[:n + 1])


NACT = acts_through(NCH - 1)
H_PS = {L0F: 0, L1F: NG * 6, L2M: NG * 10, L3F: NG * (10 + NCH)}
H_SB = {L0F: 0, L1F: NG * 6, L2M: NG * 10, L3F: NG * (10 + NACT)}
H_MUL = {L2M: 0, L3F: NG * 2}
NCHUNK3 = 32


def groups(eng, body):
    body(0)
    with eng.Fori(1, NG) as g:
        body(g)


def wait(eng, sem, value):
    if isinstance(value, int) and value <= 0:
        return
    eng.wait_ge(sem, value)


def pipelined(eng, steps, unit=2):
    lo = min(lag for lag, _ in steps)
    hi = max(lag for lag, _ in steps)
    first = hi + hi % 2 + 2
    last = NPAIR + min(lo, 0)
    last -= (last - first) % 2

    def turn(t, static):
        for lag, step in steps:
            p = t - lag
            if static and not 0 <= p < NPAIR:
                continue
            step(p, None)

    for t in range(lo, first):
        turn(t, True)
    with eng.Fori(0, (last - first) // 2) as j:
        for half in range(2):
            for lag, step in steps:
                step(2 * j + (first + half - lag), (first + half - lag) % 2)
    for t in range(last, NPAIR + hi):
        turn(t, True)


def build_program(nc, x, ctx_tok, ctx_T2, mask_q, mask_qk, mask_key, pack, rows, lora_A, lora_B,
                  gate_up, down, out):
    es = ExitStack()
    with es:
        def sb(name, shape, dt=F32):
            return es.enter_context(nc.sbuf_tensor(name, shape, dt))

        def sem(name):
            return es.enter_context(nc.semaphore(name))

        X = sb("X", [P, NPAIR, D])
        Zr = sb("Zr", [P, NPAIR, D])
        CTX = Zr
        arena = sb("arena", [P, 12 * GT])
        W = sb("W", [P, NPACK])
        ROWS = sb("ROWS", [1, 3 * D])
        WGU = sb("WGU", [P, 8, 2, 512])
        WD = sb("WD", [P, 8, 4, D])
        QT = sb("QT", [P, NPAIR, P])
        KT = sb("KT", [P, B, P])
        KT64 = KT[:, 0:B // 2, :].rearrange("p a (b k) -> p (a b) k", k=S)
        V = sb("V", [P, B, D])
        ctx2 = sb("ctx2", [P, BPG, 2, S])
        yT2 = CL = ctx2
        LA = arena[0:16, 0:512].rearrange("p (n d) -> p n d", n=4)
        LB = arena[0:16, 512:1024].rearrange("p (n d) -> p n d", n=4)
        Kx = arena[:, 0:4096].rearrange("p (r b c) -> p r b c", r=2, b=2)
        Qs = sb("Qs", [P, 2, P])
        PR = arena[:, 4096:6144].rearrange("p (r c) -> p r c", r=2)
        arena2 = sb("arena2", [P, 4 * GT])
        PT = arena2[:, :].rearrange("p (r n q) -> p r n q", r=2, n=8)
        Vz = sb("Vz", [P, 2, 2, 384])
        cT = sb("cT", [P, 2, P])
        mx = sb("mx", [P, 2, 16])
        sm = sb("sm", [P, 2, 16])
        rc = sb("rc", [P, 2, 16])
        kd = sb("kd", [P, 2, P], BF16)
        st = sb("st", [P, PPG, 6])
        spare = sb("spare", [P, 2])
        mv = sb("mv", [P, PPG, 2])
        ve = sb("ve", [P, PPG])
        rstd = sb("rstd", [P, PPG])
        y = arena2[:, 0:GT].rearrange("p (j d) -> p j d", d=D)
        yy = arena2[:, GT:2 * GT].rearrange("p (j d) -> p j d", d=D)
        yT = arena2[:, 2 * GT:3 * GT]
        Hs = arena[:, :].rearrange("p (n t) -> p n t", n=12)
        oT = arena2[:, 3 * GT:4 * GT]
        sq = arena[:, 2048:3584]
        ss = sb("ss", [P, 128])
        rs = sb("rs", [P, 128])
        rt = sb("rt", [P, 128])
        qkn = arena[:, 0:1536]
        oddT = sb("oddT", [P, 2, BPG, 4])
        Er = sb("Er", [32, 4, D])
        E2 = sb("E2", [P, 4, 32])
        XO = sb("XO", [32, BPG, S])
        GM = sb("GM", [P, BPG, S])
        lg = sb("lg", [P, PPG, 4])
        fin = sb("fin", [P, PPG, 4], mybir.dt.uint32)
        lgz = sb("lgz", [P, PPG, 4])
        gmx = sb("gmx", [P, PPG])
        gs = sb("gs", [P, PPG])
        cmp = sb("cmp", [P, PPG, 4, 4])
        tie = sb("tie", [P, PPG, 4, 4])
        rank = sb("rank", [P, PPG, 4])
        moe = sb("moe", [P, PPG, D])
        zero = arena2[:, 0:512]
        ident = sb("ident", [P, P])
        identb = sb("identb", [P, P], BF16)
        hm16a = sb("hm16a", [P, 16])
        hm16 = sb("hm16", [P, 16])
        hm2 = sb("hm2", [P, 2])
        causal = sb("causal", [P, S], BF16)
        causalf = sb("causalf", [P, S])
        ones_row = sb("ones_row", [1, P])
        sel2f = sb("sel2f", [2, 2, S])
        sel2 = sb("sel2", [2, P], BF16)
        low4 = sb("low4", [P, 4, 4])
        eps_c = sb("eps_c", [P, 3])
        mhalf = sb("mhalf", [P, 128])
        Sel1 = sb("Sel1", [P, PPG, BPG, 4])
        Sel2 = sb("Sel2", [P, PPG, 4, 32])
        mB = sb("mB", [P, 4, BPG])
        dB = sb("dB", [P, BPG])
        mR = sb("mR", [P, 32, 4])
        dR = sb("dR", [P, 4])
        mq_i = sb("mq_i", [P, NPAIR], mybir.dt.int32)
        keep = sb("keep", [P, NPAIR])
        mqk_i = arena[:, 4096:5120].bitcast(mybir.dt.int32).rearrange("p (n k) -> p n k", k=S)
        mqk = sb("mqk", [P, NPAIR, S], BF16)
        mk_i = arena[0:2, 5120:6144].bitcast(mybir.dt.int32).rearrange("p (n k) -> p n k", k=S)
        mk = sb("mk", [2, NPAIR, S], BF16)
        W1m = sb("W1m", [P, 4, D])
        BD = sb("BD", [P, 3, 16, 8])

        PS = es.enter_context(nc.psum_tensor("PS", [P, 8, 512], F32))
        PSf = PS[:, :, :].rearrange("p a b -> p (a b)")

        def w(name, i=None, n=128, rows_=P):
            o, size = OFF[name]
            if i is None:
                return W[0:rows_, o:o + size]
            return W[0:rows_, o + i * n:o + (i + 1) * n]

        def col(name, i=0):
            o = OFF[name][0] + i
            return W[:, o:o + 1]

        dma_x, dma_ctx, dma_pack, dma_small, dma_moe, dma_ctx2, dma_out = (
            sem(n) for n in ("dma_x", "dma_ctx", "dma_pack", "dma_small", "dma_moe", "dma_ctx2", "dma_out"))
        consts, consts_v, lora_ps, x_ready = (sem(n) for n in ("consts", "consts_v", "lora_ps", "x_ready"))
        n_stats, n_aggr, n_ve, n_rstd, n_done = (sem("n_" + n) for n in ("stats", "aggr", "ve", "rstd", "done"))
        t_ps, t_sb, z_copied = (sem(n) for n in ("t_ps", "t_sb", "z_copied"))
        kv_ps, q_ps, k_sb, v_sb, q_sb = (sem("p_" + n) for n in ("kv_ps", "q_ps", "k_sb", "v_sb", "q_sb"))
        sq_sb, ss_sb, rs_sb, qkn_sb, qk_turned = (sem("r_" + n) for n in ("sq", "ss", "rs", "qkn", "turned"))
        kx_v, kx_p, qs_sb, sc_ps, mx_sb, sub_sb, exp_sb, sum_sb, rc_sb, pn_sb = (
            sem("a_" + n) for n in ("kx_v", "kx_p", "qs", "sc", "mx", "sub", "exp", "sum", "rc", "pn"))
        pt_ps, pt_sb, vz_sb, pv_ps, ct_sb, o_ps, kd_sb = (
            sem("a_" + n) for n in ("pt_ps", "pt_sb", "vz", "pv", "ct", "o", "kd"))
        h_ps, h_sb, h_mul, acc_ps, o_sb, ot_ps = (sem("f_" + n) for n in ("h_ps", "h_sb", "h_mul", "acc", "o_sb", "ot"))
        e_ps, e_sb, odd_sb, xo_ps, xo_sb, g_ps, g_sb = (
            sem("l_" + n) for n in ("e_ps", "e_sb", "odd", "xo_ps", "xo_sb", "g_ps", "g_sb"))
        lg_ps, gate_v, gate_e, wt_sb, oe_ps, derived = (
            sem("m_" + n) for n in ("lg", "gate_v", "gate_e", "wt", "oe", "derived"))
        sums_sb, root_sb, n_gate, w_done, moe_sb, x_part, d_ps, n_ms, n_kp = (
            sem(n) for n in ("r_sums", "r_root", "m_gate2", "m_w", "m_sum", "m_x", "f_down", "n_ms", "n_kp"))

        SMALL = 16 * 6
        TOK = [L0A, L1A, L2A]

        block = es.enter_context(nc.Block())

        @block.sync
        def _(sp):
            sp.dma_start(X[:, :, :], x).then_inc(dma_x, 16)
            sp.dma_start(W[:, 0:NPACK // 2], pack[:, 0:NPACK // 2]).then_inc(dma_pack, 16)
            sp.dma_start(W[:, NPACK // 2:NPACK], pack[:, NPACK // 2:NPACK]).then_inc(dma_pack, 16)
            sp.dma_start(ctx2[:, :, :, :], ctx_T2[:, 0, :, :, :]).then_inc(dma_ctx2, 16)
            for a in range(3):
                with sp.Fori(int(a == 0), NG) as g:
                    sp.wait_ge(kv_ps, NG * a + g)
                    sp.dma_start(ctx2[:, :, :, :], ctx_T2[:, g, :, :, :]).then_inc(dma_ctx2, 16)
            sp.wait_ge(x_ready, x_after(L2M))
            sp.dma_start(CTX[:, :, :], ctx_tok).then_inc(dma_ctx, 16)
            sp.wait_ge(x_ready, x_after(L3F))
            sp.dma_start(out, X[:, :, :]).then_inc(dma_out, 16)
            sp.wait_ge(dma_out, 16)

        @block.gpsimd
        def _(pool):
            pool.memset(zero[:, :], 0.0).then_inc(consts, 1)
            pool.memset(ones_row[:, :], 1.0).then_inc(consts, 1)
            pool.memset(mhalf[:, :], -0.5).then_inc(consts, 1)
            pool.memset(eps_c[:, 0:1], LN_EPS).then_inc(consts, 1)
            pool.memset(eps_c[:, 1:2], RMS_EPS).then_inc(consts, 1)
            pool.memset(eps_c[:, 2:3], 0.0).then_inc(consts, 1)
            pool.memset(causalf[:, :], 0.0).then_inc(consts, 1)
            pool.memset(Vz[:, :, :, :], 0.0).then_inc(consts, 1)
            pool.wait_ge(consts, 8)

            def pick(o, src, pattern, base, cm, op=ALU.not_equal, fill=1.0):
                pool.affine_select(out=o, in_=src, compare_op=op, fill=fill, base=base, pattern=pattern,
                                   channel_multiplier=cm).then_inc(consts, 1)

            pick(ident[:, :], zero[:, 0:P], [[-1, P]], 0, 1)
            pick(hm16a[:, :], mhalf[:, 0:16], [[-8, 16]], 0, 1, ALU.is_ge, 0.0)
            pick(mB[:, :, :], mhalf[:, 0:32].rearrange("p (c b) -> p c b", c=4), [[-32, 4], [-4, 8]], 0, 1, ALU.is_ge, 0.0)
            pick(mR[:, :, :], zero[:, 0:128].rearrange("p (m r) -> p m r", r=4), [[-4, 32], [-1, 4]], 0, 1)
            pick(Sel1[:, :, :, :], zero[:, 0:128].rearrange("p (j b r) -> p j b r", j=4, b=8),
                 [[128, 4], [-64, 8], [-2, 4]], -1, 1)
            pick(Sel2[:, :, :, :].rearrange("p j c (b r) -> p j c b r", b=8),
                 zero[:, 0:512].rearrange("p (j c b r) -> p j c b r", j=4, c=4, b=8),
                 [[128, 4], [0, 4], [-64, 8], [-2, 4]], -9, 1)
            pool.wait_ge(consts, 14)
            pick(hm16[:, :], hm16a[:, :], [[8, 16]], 7, -1, ALU.is_ge, 0.0)
            pick(mB[:, :, :], mB[:, :, :], [[32, 4], [4, 8]], 3, -1, ALU.is_ge, 0.0)
            pick(hm2[:, :], mhalf[:, 0:2], [[-64, 2]], 0, 1, ALU.is_ge, 0.0)
            pick(low4[:, :, :], zero[:, 0:16].rearrange("p (e j) -> p e j", e=4), [[-1, 4], [1, 4]], 0, 0, ALU.is_ge, 1.0)
            pool.wait_ge(consts, 18)
            pick(hm2[:, :], hm2[:, :], [[64, 2]], 63, -1, ALU.is_ge, 0.0)
            pool.wait_ge(consts, 19)
            pick(sel2f[:, :, :], zero[0:2, 0:P].rearrange("p (b q) -> p b q", b=2), [[-1, 2], [0, S]], 0, 1)
            pool.wait_ge(consts, 20)
            pick(causalf[0:64, :], causalf[0:64, :], [[-1, S]], 0, 1, ALU.is_ge, -1e9)
            pool.wait_ge(consts, 21)
            pick(causalf[64:128, :], causalf[64:128, :], [[-1, S]], 0, 1, ALU.is_ge, -1e9)

            def rstd_of(v, eps, ms=None, kp=None):
                pool.wait_ge(n_aggr, v)
                var, mu = mv[:, :, 1], mv[:, :, 0]
                if ms is not None:
                    pool.tensor_tensor(rstd[:, :], mu, mu, ALU.mult).then_inc(n_ms, 1)
                    pool.wait_ge(n_ms, 2 * ms + 1)
                    pool.tensor_tensor(rstd[:, :], var, rstd[:, :], ALU.add).then_inc(n_ms, 1)
                    pool.wait_ge(n_ms, 2 * ms + 2)
                    var = rstd[:, :]
                pool.tensor_tensor(ve[:, :], var, eps_c[:, eps:eps + 1].to_broadcast([P, PPG]), ALU.add).then_inc(n_ve, 1)
                pool.wait_ge(n_ve, v)
                if kp is None:
                    pool.tensor_tensor(rstd[:, :], ve[:, :], mhalf[:, 0:PPG], ALU.pow).then_inc(n_rstd, 1)
                else:
                    pool.tensor_tensor(ve[:, :], ve[:, :], mhalf[:, 0:PPG], ALU.pow).then_inc(n_kp, 1)
                    pool.wait_ge(n_kp, v)
                    pool.tensor_tensor(rstd[:, :], ve[:, :], kp, ALU.mult).then_inc(n_rstd, 1)

            def norms(k, g, t=0):
                return before(NORMS, k) + NORMS[k] * g + t + 1

            def pairs(a, nh, nk):
                hm = hm16 if nh == 16 else hm2
                nc_ = nh * nk
                kt = KT64 if nk == S else KT[:, :, :]

                def spread(p, par):
                    par = p % 2 if par is None else par
                    wait(pool, sc_ps, NPAIR * a + p - 1)
                    pool.tensor_tensor(Kx[:, par, 1, 0:nc_].rearrange("p (h k) -> p h k", h=nh),
                                       kt[:, 2 * p + 1, :].unsqueeze(1).to_broadcast([P, nh, nk]),
                                       hm[:, :].unsqueeze(2).to_broadcast([P, nh, nk]),
                                       ALU.mult).then_inc(kx_p, 1)

                def normalise(p, par):
                    par = p % 2 if par is None else par
                    pool.wait_ge(rc_sb, NPAIR * a + p + 1)
                    pr = PR[:, par, 0:nc_].rearrange("p (h k) -> p h k", h=nh)
                    pool.tensor_tensor(pr, pr, rc[:, par, 0:nh].unsqueeze(2).to_broadcast([P, nh, nk]),
                                       ALU.mult).then_inc(pn_sb, 1)

                pool.wait_ge(k_sb, NG * (a + 1))
                pipelined(pool, [(-2, spread), (0, normalise)])

            pool.wait_ge(consts_v, 1)
            def group_norms(k, g):
                if k == L0A:
                    rstd_of(norms(k, g), 0, kp=keep[:, :].rearrange("p (g j) -> p g j", j=PPG)[:, g, :])
                elif k == L2M:
                    rstd_of(norms(k, g), 1, ms=NG + g)
                else:
                    rstd_of(norms(k, g), 0)
                if k == L2F:
                    pool.wait_ge(n_done, norms(k, g))
                    pool.tensor_copy(Zr[:, :, :].rearrange("p (g j) d -> p g j d", j=PPG)[:, g], y[:, :, :])\
                        .then_inc(z_copied, 1)
                    rstd_of(norms(k, g, 1), 1, ms=g)
                if k == L3A:
                    rstd_of(norms(k, g, 1), 0)
                    rstd_of(norms(k, g, 2), 0)
            for k in range(9):
                groups(pool, lambda g, k=k: group_norms(k, g))
                if k in ATT:
                    pairs(ATT[k], *((2, 128) if k == L3A else (16, 64)))

        @block.scalar
        def _(act):
            act.dma_start(ROWS[:, :], rows).then_inc(dma_small, 16)
            act.dma_start(LA[:, :, :], lora_A).then_inc(dma_small, 16)
            act.dma_start(LB[:, :, :], lora_B).then_inc(dma_small, 16)
            act.dma_start(mq_i[:, :], mask_q).then_inc(dma_small, 16)
            act.dma_start(mqk_i[:, :, :], mask_qk).then_inc(dma_small, 16)
            act.dma_start(mk_i[:, :, :], mask_key).then_inc(dma_small, 16)
            act.dma_start(WGU[:, :, :, :], gate_up).then_inc(dma_moe, 16)
            act.dma_start(WD[:, :, :, :], down).then_inc(dma_moe, 16)
            act.wait_ge(consts_v, 1)

            def turned(k, g, t=0):
                return before(TURNS, k) + TURNS[k] * g + t + 1

            def turn_out(k, g, t, outs, scale=None, bias=None):
                act.wait_ge(t_ps, turned(k, g, t))
                for n, o in enumerate(outs):
                    src = PS[:, 7, :]
                    if len(o.shape) == 3:
                        src = src.rearrange("p (b s) -> p b s", s=S)
                    if scale is None:
                        ins = act.activation(o, src, ACT.Copy)
                    else:
                        ins = act.activation(o, src, ACT.Identity, bias=bias if bias is not None else 0.0, scale=scale)
                ins.then_inc(t_sb, 1)

            def pairs(k):
                a = ATT[k]
                L3 = k == L3A
                nc_ = 256 if L3 else 1024
                scale = {L0A: 8 ** -0.5, L1A: 8 ** -0.5, L2A: 128 ** -0.5, L2F: 8 ** -0.5, L3A: 64 ** -0.5}[k]

                def exps(p, par):
                    par = p % 2 if par is None else par
                    act.wait_ge(sub_sb, NPAIR * a + p + 1)
                    act.activation(PR[:, par, 0:nc_], PR[:, par, 0:nc_], ACT.Exp, scale=scale).then_inc(exp_sb, 1)

                def query(p, par):
                    par = p % 2 if par is None else par
                    wait(act, sc_ps, NPAIR * a + p - 1)
                    act.activation(Qs[:, par, :], QT[:, p, :], ACT.Copy).then_inc(qs_sb, 1)

                def values(p, par):
                    par = p % 2 if par is None else par
                    wait(act, pv_ps, NPAIR * a + p - 1)
                    if L3:
                        ins = act.activation(Vz[:, par, :, 0:P], V3p(p), ACT.Copy)
                    else:
                        for h in range(2):
                            dst = Vz[64 * h:64 * h + 64, par, :, :].rearrange("p b (n c) -> p b n c", c=48)[:, :, :, 8 * h:8 * h + 8]
                            src = V3p(p)[64 * h:64 * h + 64].rearrange("p b (n c) -> p b n c", c=16)[:, :, :, 8 * h:8 * h + 8]
                            ins = act.activation(dst, src, ACT.Copy)
                    ins.then_inc(vz_sb, 1)

                def V3p(p):
                    return V[:, :, :].rearrange("p (a b) d -> p a b d", b=2)[:, p]

                def probs_out(p, par):
                    par = p % 2 if par is None else par
                    n = nc_ // P // 2
                    wait(act, pv_ps, NPAIR * a + p - 1)
                    for half in range(2):
                        act.wait_ge(pt_ps, 2 * (NPAIR * a + p) + half + 1)
                        act.activation(PT[:, par, n * half:n * (half + 1), :],
                                       PS[:, 4 + half, 0:n * P].rearrange("p (n q) -> p n q", n=n),
                                       ACT.Copy).then_inc(pt_sb, 1)

                def context_out(p, par):
                    par = p % 2 if par is None else par
                    act.wait_ge(pv_ps, NPAIR * a + p + 1)
                    wait(act, o_ps, NPAIR * a + p - 1)
                    src = PS[:, 6, P * par:P * par + P]
                    if k == L1A:
                        act.activation(cT[:, par, :], src, ACT.Identity, bias=col("c_bv")).then_inc(ct_sb, 1)
                    else:
                        act.activation(cT[:, par, :], src, ACT.Copy).then_inc(ct_sb, 1)

                pipelined(act, [(1, probs_out), (2, context_out), (0, exps), (-2, query), (0, values)])

            def half_root(u, n):
                act.wait_ge(ss_sb, u + 1)
                act.activation(rt[:, 0:n], ss[:, 0:n], ACT.Sqrt, scale=0.25).then_inc(root_sb, 1)

            def group_work(k, g):
                if k in TOK:
                    a = ATT[k]
                    act.wait_ge(kv_ps, NG * a + g + 1)
                    kdst = KT64.rearrange("p (g b) s -> p g (b s)", b=BPG)[:, g]
                    if k == L1A:
                        act.activation(kdst, PS[:, 1, :], ACT.Identity, bias=col("c_bk")).then_inc(k_sb, 1)
                    else:
                        act.activation(kdst, PS[:, 1, :], ACT.Copy).then_inc(k_sb, 1)
                    turn_out(k, g, 0, [yT[:, :]])
                    act.wait_ge(q_ps, NG * a + g + 1)
                    qdst = QT[:, :, :].rearrange("p (g j) q -> p g (j q)", j=PPG)[:, g]
                    if k == L1A:
                        act.activation(qdst, PS[:, 0, :], ACT.Identity, bias=col("c_bq")).then_inc(q_sb, 1)
                    else:
                        act.activation(qdst, PS[:, 0, :], ACT.Copy).then_inc(q_sb, 1)
                elif k == L2F:
                    turn_out(k, g, 0, [yT2[:, :, 0, :], yT2[:, :, 1, :], yT[:, :]], scale=col("c_n1"))
                    act.wait_ge(q_ps, NG * 3 + g + 1)
                    act.activation(sq[:, 0:1024], PSf[:, 0:1024], ACT.Square).then_inc(sq_sb, 1)
                    half_root(g, 128)
                    act.wait_ge(qk_turned, g + 1)
                    act.activation(QT[:, :, :].rearrange("p (g j) q -> p g (j q)", j=PPG)[:, g], PS[:, 5, :],
                                   ACT.Identity, scale=col("c_qn")).then_inc(q_sb, 1)
                    act.activation(KT64.rearrange("p (g b) s -> p g (b s)", b=BPG)[:, g], PS[:, 6, :],
                                   ACT.Identity, scale=col("c_kn")).then_inc(k_sb, 1)
                elif k == L3A:
                    turn_out(k, g, 0, [CL[:, :, 1, :], yT[:, :]], scale=col("c_llg"), bias=col("c_llb"))
                    turn_out(k, g, 1, [CL[:, :, 0, :]], scale=col("c_lxg"), bias=col("c_lxb"))
                    act.wait_ge(q_ps, NG * 4 + g + 1)
                    kps = PSf[:, 0:2048].rearrange("p (b c) -> p b c", c=256)
                    act.activation(sq[:, 0:1024].rearrange("p (b c) -> p b c", c=P), kps[:, :, 0:P], ACT.Square)
                    act.activation(sq[:, 1024:1536], PS[:, 4, :], ACT.Square).then_inc(sq_sb, 1)
                    act.activation(V[:, :, :].rearrange("p (g b) d -> p g b d", b=BPG)[:, g], kps[:, :, P:256],
                                   ACT.Copy).then_inc(v_sb, 1)
                    half_root(NG + g, 24)
                    act.wait_ge(qk_turned, NG + g + 1)
                    act.activation(KT[:, :, :].rearrange("p (g b) s -> p g (b s)", b=BPG)[:, g], PSf[:, 2560:3584],
                                   ACT.Identity, scale=col("c_kg")).then_inc(k_sb, 1)
                    act.activation(QT[:, :, :].rearrange("p (g j) q -> p g (j q)", j=PPG)[:, g], PS[:, 7, :],
                                   ACT.Identity, scale=col("c_qg")).then_inc(q_sb, 1)
                elif k == L0F:
                    turn_out(k, g, 0, [yT[:, :]])
                    u = H_PS[L0F] + 6 * g
                    act.wait_ge(h_ps, u + 1)
                    act.activation(Hs[0:32, 0, :], PS[0:32, 0, :], ACT.Copy).then_inc(h_sb, 1)
                    for c in range(4):
                        act.wait_ge(h_ps, u + 2 + c)
                        act.activation(Hs[:, 1 + c, :], PS[:, (1 + c) % 4, :], ACT.Gelu_apprx_tanh,
                                       bias=col("c_L0b1", c)).then_inc(h_sb, 1)
                    act.wait_ge(h_ps, u + 6)
                    act.activation(Hs[0:32, 5, :], PS[0:32, 5, :], ACT.Copy).then_inc(h_sb, 1)
                    act.wait_ge(acc_ps, g + 1)
                    act.activation(oT[:, :], PS[:, 4, :], ACT.Identity, bias=col("c_L0b2")).then_inc(o_sb, 1)
                elif k == L1F:
                    turn_out(k, g, 0, [yT[:, :]])
                    u = H_PS[L1F] + 4 * g
                    for c in range(4):
                        act.wait_ge(h_ps, u + 1 + c)
                        act.activation(Hs[:, c, :], PS[:, c, :], ACT.Gelu, bias=col("c_L1b1", c)).then_inc(h_sb, 1)
                    act.wait_ge(acc_ps, NG + g + 1)
                    act.activation(oT[:, :], PS[:, 4, :], ACT.Identity, bias=col("c_L1b2")).then_inc(o_sb, 1)
                elif k == L2M:
                    turn_out(k, g, 0, [yT[:, :]], scale=col("c_n2"))
                    act.wait_ge(gate_v, 7 * g + 5)
                    act.activation(lgz[:, :, :], lgz[:, :, :], ACT.Exp).then_inc(gate_e, 1)
                    for n, (name, c, dst) in enumerate(MOE_CHUNKS):
                        if dst is None:
                            continue
                        act.wait_ge(h_ps, H_PS[L2M] + NCH * g + n + 1)
                        act.activation(Hs[:, dst, :], PS[:, n % 4, :],
                                       ACT.Silu if name == "e1_w1" else ACT.Gelu).then_inc(h_sb, 1)
                else:
                    turn_out(k, g, 0, [yT[:, :]])
                    for n in range(NCHUNK3):
                        act.wait_ge(h_ps, H_PS[L3F] + NCHUNK3 * g + n + 1)
                        if n >= 2:
                            act.wait_ge(h_mul, H_MUL[L3F] + NCHUNK3 * g + n - 1)
                        act.activation(Hs[:, n % 2, :], PS[:, n % 2, :], ACT.Silu).then_inc(h_sb, 1)
                    act.wait_ge(d_ps, NCHUNK3 * (g + 1))
                    act.activation(oT[:, :], PS[:, 4, :], ACT.Copy).then_inc(o_sb, 1)

            for k in range(9):
                if k > 0:
                    act.wait_ge(x_ready, x_after(k - 1))
                groups(act, lambda g, k=k: group_work(k, g))
                if k in ATT:
                    pairs(k)

        @block.vector
        def _(dve):
            dve.wait_ge(consts, 22)
            dve.wait_ge(dma_small, SMALL)
            dve.wait_ge(dma_pack, 32)
            cv = [0]

            def made(ins):
                cv[0] += 1
                ins.then_inc(derived, 1)

            def settle():
                dve.wait_ge(derived, cv[0])

            made(dve.tensor_copy(identb[:, :], ident[:, :]))
            made(dve.tensor_scalar(hm16[:, :], hm16[:, :], -2.0, None, ALU.mult))
            made(dve.tensor_scalar(hm2[:, :], hm2[:, :], -2.0, None, ALU.mult))
            made(dve.tensor_copy(causal[:, :], causalf[:, :]))
            made(dve.tensor_copy(sel2[:, :], sel2f[:, :, :].rearrange("p b q -> p (b q)")))
            made(dve.tensor_scalar(keep[:, :], mq_i[:, :], 0.0, None, ALU.is_equal))
            made(dve.tensor_scalar(mqk[:, :, :], mqk_i[:, :, :], 0.0, -1e20, ALU.is_equal, ALU.mult))
            made(dve.tensor_scalar(mk[:, :, :], mk_i[:, :, :], 0.0, -1e30, ALU.is_equal, ALU.mult))
            made(dve.tensor_reduce(dB[:, :], mB[:, :, :].rearrange("p c b -> p b c"), AX, ALU.add))
            made(dve.tensor_reduce(dR[:, :], mR[:, :, :].rearrange("p m r -> p r m"), AX, ALU.add))
            settle()
            made(dve.tensor_scalar(dB[:, :], dB[:, :], -2.0, col("c_scale"), ALU.mult, ALU.mult))
            for n, name in enumerate(("L2_q", "L2_k", "L2_v")):
                made(dve.tensor_tensor(BD[:, n, :, :], w(name).unsqueeze(1).to_broadcast([P, 16, 8]),
                                       hm16[:, :].unsqueeze(2).to_broadcast([P, 16, 8]), ALU.mult))
            dve.wait_ge(lora_ps, 1)
            settle()
            for n, name in enumerate(("L1_Wq", "L1_Wk", "L1_Wv", "L1_Wo")):
                ins = dve.scalar_tensor_tensor(W1m[:, n, :], PS[:, 0, P * n:P * n + P], 2.0, w(name), ALU.mult, ALU.add)
            ins.then_inc(consts_v, 1)
            dve.wait_ge(dma_x, 16)

            def norm_no(k, g, t=0):
                return before(NORMS, k) + NORMS[k] * g + t + 1

            def turned(k, g, t=0):
                return before(TURNS, k) + TURNS[k] * g + t + 1

            def normalise(v, src, dst, mean=True, free=None):
                for j in range(PPG):
                    ins = dve.bn_stats(st[:, j, :], src(j))
                ins.then_inc(n_stats, 1)
                dve.wait_ge(n_stats, v)
                dve.memset(spare[:, 0:1], 0.0)
                for j in range(PPG):
                    ins = dve.bn_aggr(mv[:, j, :], st[:, j, :])
                ins.then_inc(n_aggr, 1)
                if free:
                    free()
                dve.wait_ge(n_rstd, v)
                for j in range(PPG):
                    if mean:
                        ins = dve.tensor_scalar(dst(j), src(j), mv[:, j, 0:1], rstd[:, j:j + 1], ALU.subtract, ALU.mult)
                    else:
                        ins = dve.tensor_scalar(dst(j), src(j), rstd[:, j:j + 1], None, ALU.mult)
                ins.then_inc(n_done, 1)
                dve.wait_ge(n_done, v)

            def group(T, g):
                return T[:, :, :].rearrange("p (g j) d -> p g j d", j=PPG)[:, g]

            def add_group(k, g, u):
                dve.wait_ge(ot_ps, u)
                dve.tensor_tensor(group(X, g), group(X, g), PS[:, 5, :].rearrange("p (j d) -> p j d", j=PPG),
                                  ALU.add).then_inc(x_ready, 1)

            def head_factors(u, n, dim, eps, guard):
                dve.wait_ge(sums_sb, u + 1)
                dve.tensor_scalar(ss[:, 0:n], ss[:, 0:n], 1.0 / dim, eps, ALU.mult, guard).then_inc(ss_sb, 1)
                dve.wait_ge(root_sb, u + 1)
                dve.reciprocal(rs[:, 0:n], rt[:, 0:n]).then_inc(rs_sb, 1)
                dve.wait_ge(rs_sb, 4 * u + 1)
                dve.tensor_tensor(rs[:, 0:n], rs[:, 0:n], ss[:, 0:n], ALU.mult).then_inc(rs_sb, 1)
                dve.wait_ge(rs_sb, 4 * u + 2)
                dve.scalar_tensor_tensor(rs[:, 0:n], rs[:, 0:n], 0.25, rt[:, 0:n], ALU.mult, ALU.add).then_inc(rs_sb, 1)
                dve.wait_ge(rs_sb, 4 * u + 3)
                dve.reciprocal(rs[:, 0:n], rs[:, 0:n]).then_inc(rs_sb, 1)
                dve.wait_ge(rs_sb, 4 * u + 4)

            def pairs(k):
                a = ATT[k]
                L3 = k == L3A
                nh, nk = (2, 128) if L3 else (16, 64)
                nc_ = nh * nk
                hm = hm2 if L3 else hm16
                kt = KT[:, :, :] if L3 else KT64

                def spread(p, par):
                    par = p % 2 if par is None else par
                    wait(dve, sc_ps, NPAIR * a + p - 1)
                    dve.tensor_tensor(Kx[:, par, 0, 0:nc_].rearrange("p (h k) -> p h k", h=nh),
                                      kt[:, 2 * p, :].unsqueeze(1).to_broadcast([P, nh, nk]),
                                      hm[:, :].unsqueeze(2).to_broadcast([P, nh, nk]),
                                      ALU.mult).then_inc(kx_v, 1)
                    if k == L0A:
                        dve.tensor_scalar(kd[:, par, :], identb[:, :], keep[:, :].unsqueeze(2)[:, p, :], None, ALU.mult).then_inc(kd_sb, 1)

                def shift(p, par):
                    par = p % 2 if par is None else par
                    dve.wait_ge(sc_ps, NPAIR * a + p + 1)
                    s = PSf[:, 1024 * par:1024 * par + nc_].rearrange("p (h k) -> p h k", h=nh)
                    dve.tensor_reduce(mx[:, par, 0:nh], s, AX, ALU.max).then_inc(mx_sb, 1)
                    dve.wait_ge(mx_sb, NPAIR * a + p + 1)
                    wait(dve, pt_ps, 2 * (NPAIR * a + p - 1))
                    dve.tensor_tensor(PR[:, par, 0:nc_].rearrange("p (h k) -> p h k", h=nh), s,
                                      mx[:, par, 0:nh].unsqueeze(2).to_broadcast([P, nh, nk]),
                                      ALU.subtract).then_inc(sub_sb, 1)

                def sums(p, par):
                    par = p % 2 if par is None else par
                    dve.wait_ge(exp_sb, NPAIR * a + p + 1)
                    dve.tensor_reduce(sm[:, par, 0:nh], PR[:, par, 0:nc_].rearrange("p (h k) -> p h k", h=nh),
                                      AX, ALU.add).then_inc(sum_sb, 1)
                    dve.wait_ge(sum_sb, NPAIR * a + p + 1)
                    dve.reciprocal(rc[:, par, 0:nh], sm[:, par, 0:nh]).then_inc(rc_sb, 1)

                def add(p, par):
                    par = p % 2 if par is None else par
                    dve.wait_ge(o_ps, NPAIR * a + p + 1)
                    o = PS[:, 7, P * par:P * par + P]
                    if k == L2F:
                        dve.tensor_tensor(Zr[:, p, 32:D], Zr[:, p, 32:D], o[:, 32:D], ALU.add).then_inc(x_ready, 1)
                    else:
                        dve.tensor_tensor(X[:, p, :], X[:, p, :], o, ALU.add).then_inc(x_ready, 1)

                pipelined(dve, [(0, shift), (-2, spread), (0, sums), (3, add)])

            def group_work(k, g):
                src = Zr if k == L2M else X
                v = norm_no(k, g)

                t0 = before(TURNS, k)

                def y_free():
                    if k == L2F:
                        wait(dve, z_copied, g)
                    else:
                        wait(dve, t_ps, t0 + TURNS[k] * g)
                    if k == L1F:
                        wait(dve, e_ps, g)

                normalise(v, lambda j: src[:, PPG * g + j, :], lambda j: y[:, j, :], mean=k != L2M, free=y_free)
                if k == L2F:
                    normalise(norm_no(k, g, 1), lambda j: y[:, j, :], lambda j: yy[:, j, :], mean=False,
                              free=lambda: wait(dve, t_ps, t0 + g))
                if k == L3A:
                    normalise(norm_no(k, g, 1), lambda j: y[:, j, :], lambda j: yy[:, j, :],
                              free=lambda: wait(dve, t_ps, t0 + 2 * g))
                    dve.wait_ge(dma_ctx, 16)
                    normalise(norm_no(k, g, 2), lambda j: CTX[:, PPG * g + j, :], lambda j: y[:, j, :])
                if k in TOK:
                    a = ATT[k]
                    dve.wait_ge(kv_ps, NG * a + g + 1)
                    dve.tensor_copy(V[:, :, :].rearrange("p (g b) d -> p g (b d)", b=BPG)[:, g],
                                    PSf[:, 1024:2048]).then_inc(v_sb, 1)
                if k == L2F:
                    dve.wait_ge(kv_ps, NG * 3 + g + 1)
                    dve.tensor_copy(V[:, :, :].rearrange("p (g b) d -> p g (b d)", b=BPG)[:, g],
                                    PSf[:, 1024:2048]).then_inc(v_sb, 1)
                    dve.wait_ge(sq_sb, g + 1)
                    dve.tensor_reduce(ss[:, 0:128], sq[:, 0:1024].rearrange("p (n d) -> p n d", d=8),
                                      AX, ALU.add).then_inc(sums_sb, 1)
                    head_factors(g, 128, 8, RMS_EPS, ALU.add)
                    wait(dve, qk_turned, g)
                    dve.tensor_tensor(qkn[:, 0:1024].rearrange("p (n d) -> p n d", d=8),
                                      PSf[:, 0:1024].rearrange("p (n d) -> p n d", d=8),
                                      rs[:, 0:128].unsqueeze(2).to_broadcast([P, 128, 8]), ALU.mult).then_inc(qkn_sb, 1)
                if k == L3A:
                    dve.wait_ge(sq_sb, NG + g + 1)
                    dve.tensor_reduce(ss[:, 0:24], sq[:, :].rearrange("p (n d) -> p n d", d=64),
                                      AX, ALU.add).then_inc(sums_sb, 1)
                    head_factors(NG + g, 24, 64, RMS3_EPS ** 2, ALU.max)
                    dve.wait_ge(v_sb, NG * 4 + g + 1)
                    dve.wait_ge(qk_turned, NG + g)
                    for h in range(2):
                        dve.tensor_tensor(qkn[:, 0:1024].rearrange("p (b h d) -> p b h d", h=2, d=64)[:, :, h],
                                          PSf[:, 0:2048].rearrange("p (b c) -> p b c", c=256)[:, :, 64 * h:64 * h + 64],
                                          rs[:, h:16:2].unsqueeze(2).to_broadcast([P, BPG, 64]), ALU.mult)
                    dve.tensor_tensor(qkn[:, 1024:1536].rearrange("p (n d) -> p n d", d=64),
                                      PS[:, 4, :].rearrange("p (n d) -> p n d", d=64),
                                      rs[:, 16:24].unsqueeze(2).to_broadcast([P, 8, 64]), ALU.mult).then_inc(qkn_sb, 1)
                if k == L0F:
                    add_group(k, g, g + 1)
                if k == L1F:
                    dve.wait_ge(t_sb, turned(k, g))
                    wait(dve, g_ps, g)
                    yb = yT[:, :].rearrange("p (b s) -> p b s", s=S)
                    dve.tensor_copy(oddT[:, 0, :, :], yb[:, :, 2:10:2])
                    dve.tensor_copy(oddT[:, 1, :, :], yb[:, :, 10:18:2]).then_inc(odd_sb, 1)
                    dve.wait_ge(e_ps, g + 1)
                    dve.tensor_tensor(Er[:, :, :], PS[0:32, 5, 0:P].unsqueeze(1).to_broadcast([32, 4, P]),
                                      dR[0:32, :].unsqueeze(2).to_broadcast([32, 4, P]), ALU.mult)
                    for c in range(4):
                        r0 = slice(32 * c, 32 * c + 32)
                        ins = dve.tensor_tensor(
                            E2[r0, :, :],
                            PS[r0, 5, P:2 * P].rearrange("p (i c) -> p i c", c=4)[:, :, c].unsqueeze(1).to_broadcast([32, 4, 32]),
                            dR[r0, :].unsqueeze(2).to_broadcast([32, 4, 32]), ALU.mult)
                    ins.then_inc(e_sb, 1)
                    dve.wait_ge(xo_ps, g + 1)
                    dve.tensor_tensor(XO[:, :, :], PS[0:32, 6, :].rearrange("p (b s) -> p b s", s=S),
                                      dB[0:32, :].unsqueeze(2).to_broadcast([32, BPG, S]), ALU.mult).then_inc(xo_sb, 1)
                    dve.wait_ge(g_ps, g + 1)
                    dve.tensor_tensor(GM[:, :, :], PS[:, 6, :].rearrange("p (b s) -> p b s", s=S),
                                      dB[:, :].unsqueeze(2).to_broadcast([P, BPG, S]), ALU.mult).then_inc(g_sb, 1)
                    add_group(k, g, NG + g + 1)
                if k == L2M:
                    dve.wait_ge(lg_ps, g + 1)
                    q = 7 * g
                    lps = PS[:, 6, 0:16].rearrange("p (j e) -> p j e", e=4)
                    dve.tensor_copy(lg[:, :, :], lps)
                    dve.memset(lgz[:, :, :], 0.0).then_inc(gate_v, 1)
                    dve.wait_ge(gate_v, q + 1)
                    dve.tensor_tensor(fin[:, :, :], lg[:, :, :], lg[:, :, :], ALU.is_equal).then_inc(gate_v, 1)
                    dve.wait_ge(gate_v, q + 2)
                    dve.memset(spare[:, 1:2], 0.0)
                    dve.copy_predicated(lgz[:, :, :], fin[:, :, :], lg[:, :, :]).then_inc(gate_v, 1)
                    dve.wait_ge(gate_v, q + 3)
                    dve.tensor_scalar(lgz[:, :, :], lgz[:, :, :], -FLT_MAX, FLT_MAX, ALU.max, ALU.min)\
                        .then_inc(n_gate, 1)
                    dve.wait_ge(n_gate, 6 * g + 1)
                    dve.tensor_reduce(gmx[:, :], lgz[:, :, :], AX, ALU.max).then_inc(gate_v, 1)
                    dve.wait_ge(gate_v, q + 4)
                    dve.tensor_tensor(lgz[:, :, :], lgz[:, :, :], gmx[:, :].unsqueeze(2).to_broadcast([P, PPG, 4]),
                                      ALU.subtract).then_inc(gate_v, 1)
                    dve.wait_ge(gate_e, g + 1)
                    dve.tensor_reduce(gs[:, :], lgz[:, :, :], AX, ALU.add).then_inc(n_gate, 1)
                    dve.wait_ge(n_gate, 6 * g + 2)
                    dve.reciprocal(gs[:, :], gs[:, :]).then_inc(n_gate, 1)
                    dve.wait_ge(n_gate, 6 * g + 3)
                    dve.tensor_tensor(lgz[:, :, :], lgz[:, :, :], gs[:, :].unsqueeze(2).to_broadcast([P, PPG, 4]),
                                      ALU.mult).then_inc(n_gate, 1)
                    dve.wait_ge(n_gate, 6 * g + 4)
                    pe_ = lgz[:, :, :].unsqueeze(3).to_broadcast([P, PPG, 4, 4])
                    pj = lgz[:, :, :].unsqueeze(2).to_broadcast([P, PPG, 4, 4])
                    dve.tensor_tensor(cmp[:, :, :, :], pj, pe_, ALU.is_gt)
                    dve.tensor_tensor(tie[:, :, :, :], pj, pe_, ALU.is_equal).then_inc(n_gate, 1)
                    dve.wait_ge(n_gate, 6 * g + 5)
                    dve.tensor_tensor(tie[:, :, :, :], tie[:, :, :, :],
                                      low4[:, :, :].unsqueeze(1).to_broadcast([P, PPG, 4, 4]), ALU.mult).then_inc(n_gate, 1)
                    dve.wait_ge(n_gate, 6 * g + 6)
                    dve.tensor_tensor(cmp[:, :, :, :], cmp[:, :, :, :], tie[:, :, :, :], ALU.add).then_inc(gate_v, 1)
                    dve.wait_ge(gate_v, q + 6)
                    dve.tensor_reduce(rank[:, :, :], cmp[:, :, :, :], AX, ALU.add).then_inc(gate_v, 1)
                    dve.wait_ge(gate_v, q + 7)
                    dve.scalar_tensor_tensor(rank[:, :, :], rank[:, :, :], 2.0, lgz[:, :, :], ALU.is_lt, ALU.mult)\
                        .then_inc(wt_sb, 1)
                    dve.wait_ge(wt_sb, 4 * g + 1)
                    dve.tensor_reduce(gs[:, :], rank[:, :, :], AX, ALU.add).then_inc(wt_sb, 1)
                    dve.wait_ge(wt_sb, 4 * g + 2)
                    dve.tensor_scalar(gs[:, :], gs[:, :], 1e-8, None, ALU.add).then_inc(wt_sb, 1)
                    dve.wait_ge(wt_sb, 4 * g + 3)
                    dve.reciprocal(gmx[:, :], gs[:, :]).then_inc(wt_sb, 1)
                    dve.wait_ge(wt_sb, 4 * g + 4)
                    dve.tensor_tensor(rank[:, :, :], rank[:, :, :], gmx[:, :].unsqueeze(2).to_broadcast([P, PPG, 4]),
                                      ALU.mult).then_inc(w_done, 1)
                    for n, (name, c, dst) in enumerate(MOE_CHUNKS):
                        if name == "e1_w2":
                            dve.wait_ge(h_ps, H_PS[L2M] + NCH * g + n + 1)
                            dve.wait_ge(h_sb, H_SB[L2M] + NACT * g + acts_through(n))
                            dve.tensor_tensor(Hs[:, 4 + c, :], Hs[:, 4 + c, :], PS[:, n % 4, :], ALU.mult).then_inc(h_mul, 1)
                    dve.wait_ge(w_done, g + 1)
                    for n, (_, e, _, _, _) in enumerate(MOE_OUTS):
                        dve.wait_ge(oe_ps, 4 * g + n + 1)
                        for j in range(PPG):
                            o = PS[:, 4 + n % 2, P * j:P * j + P]
                            if n == 0:
                                ins = dve.tensor_scalar(moe[:, j, :], o, rank[:, j, e:e + 1], None, ALU.mult)
                            else:
                                ins = dve.scalar_tensor_tensor(moe[:, j, :], o, rank[:, j, e:e + 1], moe[:, j, :],
                                                               ALU.mult, ALU.add)
                        ins.then_inc(moe_sb, 1)
                        dve.wait_ge(moe_sb, 4 * g + n + 1)
                    dve.tensor_tensor(group(X, g), group(X, g), group(Zr, g), ALU.add).then_inc(x_part, 1)
                    dve.wait_ge(x_part, g + 1)
                    dve.tensor_tensor(group(X, g)[:, :, 32:D], group(X, g)[:, :, 32:D], moe[:, :, 32:D],
                                      ALU.add).then_inc(x_ready, 1)
                if k == L3F:
                    for n in range(NCHUNK3):
                        dve.wait_ge(h_sb, H_SB[L3F] + NCHUNK3 * g + n + 1)
                        if n >= 3:
                            dve.wait_ge(d_ps, NCHUNK3 * g + n - 2)
                        dve.tensor_tensor(Hs[:, 2 + n % 3, :], Hs[:, n % 2, :], PS[:, 2 + n % 2, :], ALU.mult).then_inc(h_mul, 1)
                    add_group(k, g, 2 * NG + g + 1)

            for k in range(9):
                if k > 0:
                    dve.wait_ge(x_ready, x_after(k - 1))
                groups(dve, lambda g, k=k: group_work(k, g))
                if k in ATT:
                    dve.wait_ge(k_sb, NG * (ATT[k] + 1))
                    if k == L2F:
                        dve.wait_ge(z_copied, NG)
                    pairs(k)

        @block.tensor
        def _(pe):
            pe.wait_ge(dma_small, SMALL)
            for n in range(4):
                ins = pe.matmul(PS[:, 0, P * n:P * n + P], LA[:, n, :], LB[:, n, :], start=True, stop=True)
            ins.then_inc(lora_ps, 1)
            pe.wait_ge(consts_v, 1)

            def norm_no(k, g, t=0):
                return before(NORMS, k) + NORMS[k] * g + t + 1

            def turn(k, g, src, v, t=0):
                pe.wait_ge(n_done, v)
                wait(pe, t_sb, before(TURNS, k) + TURNS[k] * g + t)
                for j in range(PPG):
                    ins = pe.transpose(PS[:, 7, P * j:P * j + P], src[:, j, :], ident[:, :])
                ins.then_inc(t_ps, 1)

            def turn_back(u):
                pe.wait_ge(o_sb, u)
                for j in range(PPG):
                    ins = pe.transpose(PS[:, 5, P * j:P * j + P], oT[:, P * j:P * j + P], ident[:, :])
                ins.then_inc(ot_ps, 1)

            def project(k, g):
                a = ATT[k]
                if k == L0A:
                    wq, wk, wv = w("L0_WQ"), w("L0_WK"), w("L0_WV")
                elif k == L1A:
                    wq, wk, wv = (W1m[:, n, :] for n in range(3))
                else:
                    wq, wk, wv = (BD[:, n, :, :].rearrange("p a b -> p (a b)") for n in range(3))
                pe.wait_ge(dma_ctx2, 16 * (NG * a + g + 1))
                pe.wait_ge(k_sb, NG * a + g)
                pe.wait_ge(v_sb, NG * a + g)
                pe.matmul(PS[:, 1, :], wk, ctx2[:, :, 0, :], start=True, stop=True)
                for b in range(BPG):
                    ins = pe.matmul(PSf[:, 1024 + P * b:1024 + P * b + P], ctx2[:, b, :, :].rearrange("p a s -> p (a s)"),
                                    wv, start=True, stop=True)
                ins.then_inc(kv_ps, 1)
                turn(k, g, y, norm_no(k, g))
                pe.wait_ge(t_sb, before(TURNS, k) + g + 1)
                pe.wait_ge(q_sb, NG * a + g)
                pe.matmul(PS[:, 0, :], wq, yT[:, :], start=True, stop=True).then_inc(q_ps, 1)

            def pairs(k):
                a = ATT[k]
                L3 = k == L3A
                wo = {L0A: w("L0_WO"), L1A: W1m[:, 3, :], L2A: w("L2_WoT"), L2F: w("woT"), L3A: w("L3_Wout")}[k]
                bias = {L1A: 0, L2A: 1, L3A: 2}.get(k)

                def scores(p, par):
                    par = p % 2 if par is None else par
                    pe.wait_ge(kx_v, NPAIR * a + p + 1)
                    pe.wait_ge(kx_p, NPAIR * a + p + 1)
                    pe.wait_ge(qs_sb, NPAIR * a + p + 1)
                    wait(pe, sub_sb, NPAIR * a + p - 1)
                    added = k != L1A
                    if k == L0A:
                        pe.wait_ge(kd_sb, p + 1)
                    for half in range(1 if L3 else 2):
                        n = 256 if L3 else 512
                        for b in range(2):
                            ins = pe.matmul(PS[64 * b:64 * b + 64, 2 * par + half, 0:n], Qs[:, par, 64 * b:64 * b + 64],
                                            Kx[:, par, b, n * half:n * half + n], start=True, stop=not added,
                                            tile_position=(0, 64 * b), skip_group_check=True)
                        dst = PS[:, 2 * par + half, 0:n]
                        if k in (L0A, L2F):
                            ins = pe.matmul(dst, kd[:, par, :] if k == L0A else identb[:, :],
                                            causal[:, :].unsqueeze(1).to_broadcast([P, 8, S]), start=False, stop=True,
                                            skip_group_check=True)
                        if k == L2A:
                            ins = pe.matmul(dst, identb[:, :], mqk[:, p, :].unsqueeze(1).to_broadcast([P, 8, S]),
                                            start=False, stop=True, skip_group_check=True)
                        if L3:
                            ins = pe.matmul(dst.rearrange("p (h k) -> p h k", h=2)[:, :, 0:S], sel2[:, :],
                                            mk[:, p, :].unsqueeze(1).to_broadcast([2, 2, S]),
                                            start=False, stop=True, skip_group_check=True)
                    ins.then_inc(sc_ps, 1)

                def probs(p, par):
                    par = p % 2 if par is None else par
                    n = 1 if L3 else 4
                    pe.wait_ge(pn_sb, NPAIR * a + p + 1)
                    for half in range(2):
                        wait(pe, pt_sb, 2 * (NPAIR * a + p - 1) + half + 1)
                        for i in range(n):
                            c = n * half + i
                            ins = pe.transpose(PS[:, 4 + half, P * i:P * i + P], PR[:, par, P * c:P * c + P], ident[:, :])
                        ins.then_inc(pt_ps, 1)

                def values(p, par):
                    par = p % 2 if par is None else par
                    pe.wait_ge(vz_sb, NPAIR * a + p + 1)
                    pe.wait_ge(pt_sb, 2 * (NPAIR * a + p + 1))
                    wait(pe, ct_sb, NPAIR * a + p)
                    for b in range(2):
                        dst = slice(P * par + 64 * b, P * par + 64 * b + 64)
                        if L3:
                            for h in range(2):
                                ins = pe.matmul(PS[64 * h:64 * h + 64, 6, dst], Vz[:, par, b, 64 * h:64 * h + 64],
                                                PT[:, par, h, 64 * b:64 * b + 64], start=True, stop=True,
                                                tile_position=(0, 64 * h))
                        else:
                            for t in range(2):
                                for j in range(4):
                                    n = 2 * j + t
                                    ins = pe.matmul(PS[32 * j:32 * j + 32, 6, dst],
                                                    Vz[:, par, b, 48 * n - 16 * t:48 * n - 16 * t + 32],
                                                    PT[:, par, n, 64 * b:64 * b + 64], start=t == 0, stop=t == 1,
                                                    tile_position=(0, 32 * j), skip_group_check=True)
                    ins.then_inc(pv_ps, 1)

                def output(p, par):
                    par = p % 2 if par is None else par
                    pe.wait_ge(ct_sb, NPAIR * a + p + 1)
                    wait(pe, x_ready, x_after(k) - NPAIR + p)
                    dst = PS[:, 7, P * par:P * par + P]
                    ins = pe.matmul(dst, cT[:, par, :], wo, start=True, stop=bias is None)
                    if bias is not None:
                        ins = pe.matmul(dst, ones_row[:, :], ROWS[:, D * bias:D * bias + D], start=False, stop=True)
                    ins.then_inc(o_ps, 1)

                pipelined(pe, [(2, output), (0, probs), (-2, scores), (0, values)])

            def group_work(k, g):
                t0 = before(TURNS, k)
                if k in TOK:
                    project(k, g)
                elif k == L2F:
                    turn(k, g, yy, norm_no(k, g, 1))
                    pe.wait_ge(t_sb, t0 + g + 1)
                    wait(pe, qkn_sb, g)
                    for j in range(PPG):
                        ins = pe.matmul(PSf[:, 256 * j:256 * j + 256], yT[:, P * j:P * j + P], w("wqkT"), start=True, stop=True)
                    ins.then_inc(q_ps, 1)
                    wait(pe, v_sb, NG * 3 + g)
                    for b in range(BPG):
                        ins = pe.matmul(PSf[:, 1024 + P * b:1024 + P * b + P], yT2[:, b, :, :].rearrange("p a s -> p (a s)"),
                                        w("wvT"), start=True, stop=True)
                    ins.then_inc(kv_ps, 1)
                    pe.wait_ge(qkn_sb, g + 1)
                    wait(pe, k_sb, NG * 3 + g)
                    for j in range(PPG):
                        for i in range(2):
                            ins = pe.transpose(PS[:, 5 + i, P * j:P * j + P], qkn[:, 256 * j + P * i:256 * j + P * i + P], ident[:, :])
                    ins.then_inc(qk_turned, 1)
                elif k == L3A:
                    wait(pe, q_sb, NG * 4 + g)
                    turn(k, g, yy, norm_no(k, g, 1))
                    turn(k, g, y, norm_no(k, g, 2), 1)
                    pe.wait_ge(t_sb, t0 + 2 * g + 2)
                    wait(pe, qkn_sb, NG + g)
                    wait(pe, v_sb, NG * 4 + g)
                    for b in range(BPG):
                        ins = pe.matmul(PSf[:, 256 * b:256 * b + 256], CL[:, b, :, :].rearrange("p a s -> p (a s)"),
                                        w("L3_Wkv"), start=True, stop=True)
                    for j in range(PPG):
                        ins = pe.matmul(PS[:, 4, P * j:P * j + P], yT[:, P * j:P * j + P], w("L3_Wq"), start=True, stop=True)
                    ins.then_inc(q_ps, 1)
                    pe.wait_ge(qkn_sb, NG + g + 1)
                    wait(pe, k_sb, NG * 4 + g)
                    for b in range(BPG):
                        pe.transpose(PSf[:, 2560 + P * b:2560 + P * b + P], qkn[:, P * b:P * b + P], ident[:, :])
                    for j in range(PPG):
                        ins = pe.transpose(PS[:, 7, P * j:P * j + P], qkn[:, 1024 + P * j:1024 + P * j + P], ident[:, :])
                    ins.then_inc(qk_turned, 1)
                elif k == L0F:
                    turn(k, g, y, norm_no(k, g))
                    pe.wait_ge(t_sb, t0 + g + 1)
                    pe.matmul(PS[0:32, 0, :], w("U1"), yT[:, :], start=True, stop=True).then_inc(h_ps, 1)
                    u = 6 * g
                    pe.wait_ge(h_sb, u + 1)
                    for c in range(4):
                        pe.matmul(PS[:, (1 + c) % 4, :], w("V1", c, rows_=32), Hs[0:32, 0, :], start=True, stop=True).then_inc(h_ps, 1)
                    for c in range(4):
                        pe.wait_ge(h_sb, u + 2 + c)
                        ins = pe.matmul(PS[0:32, 5, :], w("U2", c, 32), Hs[:, 1 + c, :], start=c == 0, stop=c == 3)
                    ins.then_inc(h_ps, 1)
                    pe.wait_ge(h_sb, u + 6)
                    pe.matmul(PS[:, 4, :], w("V2", rows_=32), Hs[0:32, 5, :], start=True, stop=True).then_inc(acc_ps, 1)
                    turn_back(g + 1)
                    pe.wait_ge(x_ready, x_after(k - 1) + g + 1)
                elif k == L1F:
                    turn(k, g, y, norm_no(k, g))
                    for j in range(PPG):
                        pe.matmul(PS[0:32, 5, 0:P], Sel1[:, j, :, :].rearrange("p b r -> p (b r)"), y[:, j, :], start=j == 0, stop=j == 3)
                    for j in range(PPG):
                        ins = pe.matmul(PS[:, 5, P:2 * P], Sel2[:, j, :, :].rearrange("p c r -> p (c r)"), y[:, j, :], start=j == 0, stop=j == 3)
                    ins.then_inc(e_ps, 1)
                    pe.wait_ge(odd_sb, g + 1)
                    pe.matmul(PS[0:32, 6, :], oddT[:, 0, :, :].rearrange("p b r -> p (b r)"), yT[:, :], start=True, stop=True).then_inc(xo_ps, 1)
                    for c in range(4):
                        pe.matmul(PS[:, c, :], w("W1T", c), yT[:, :], start=True, stop=False)
                    pe.wait_ge(e_sb, g + 1)
                    pe.wait_ge(xo_sb, g + 1)
                    for c in range(4):
                        pe.matmul(PS[:, c, :], Er[:, c, :], XO[:, :, :].rearrange("p b s -> p (b s)"), start=False, stop=True).then_inc(h_ps, 1)
                    u = H_SB[L1F] + 4 * g
                    for c in range(4):
                        pe.wait_ge(h_sb, u + 1 + c)
                        ins = pe.matmul(PS[32 * c:32 * c + 32, 6, :], oddT[:, 1, :, :].rearrange("p b r -> p (b r)"), Hs[:, c, :],
                                        start=True, stop=True, tile_position=(0, 32 * c))
                    ins.then_inc(g_ps, 1)
                    for c in range(4):
                        pe.matmul(PS[:, 4, :], w("W2T", c), Hs[:, c, :], start=c == 0, stop=False)
                    pe.wait_ge(g_sb, g + 1)
                    pe.matmul(PS[:, 4, :], E2[:, :, :].rearrange("p r i -> p (r i)"), GM[:, :, :].rearrange("p b s -> p (b s)"),
                              start=False, stop=True).then_inc(acc_ps, 1)
                    turn_back(NG + g + 1)
                    pe.wait_ge(x_ready, x_after(k - 1) + g + 1)
                elif k == L2M:
                    turn(k, g, y, norm_no(k, g))
                    pe.wait_ge(t_sb, t0 + g + 1)
                    pe.wait_ge(x_ready, x_after(k - 1) + g)
                    for j in range(PPG):
                        ins = pe.matmul(PS[:, 6, 4 * j:4 * j + 4], yT[:, P * j:P * j + P], w("gateT"), start=True, stop=True)
                    ins.then_inc(lg_ps, 1)
                    for n, (name, c, _) in enumerate(MOE_CHUNKS):
                        if n >= 4:
                            if MOE_CHUNKS[n - 4][2] is None:
                                pe.wait_ge(h_mul, H_MUL[L2M] + 2 * g + 1 + MOE_CHUNKS[n - 4][1])
                            else:
                                pe.wait_ge(h_sb, H_SB[L2M] + NACT * g + acts_through(n - 4))
                        if name in MOE_IN:
                            ins_, last = MOE_IN[name]
                            pe.wait_ge(h_sb, H_SB[L2M] + NACT * g + acts_through(last))
                            for i, hsrc in enumerate(ins_):
                                ins = pe.matmul(PS[:, n % 4, :], w(name, 2 * i + c), Hs[:, hsrc, :], start=i == 0,
                                                stop=i == len(ins_) - 1)
                        else:
                            ins = pe.matmul(PS[:, n % 4, :], w(name, c), yT[:, :], start=True, stop=True)
                        ins.then_inc(h_ps, 1)
                        for m, (after, e, wname, hs, last) in enumerate(MOE_OUTS):
                            if after != n:
                                continue
                            if m >= 2:
                                pe.wait_ge(moe_sb, 4 * g + m - 1)
                            if e == 1:
                                pe.wait_ge(h_mul, H_MUL[L2M] + 2 * g + 2)
                            pe.wait_ge(h_sb, H_SB[L2M] + NACT * g + acts_through(last))
                            for j in range(PPG):
                                for i in range(2):
                                    ins = pe.matmul(PS[:, 4 + m % 2, P * j:P * j + P], Hs[:, hs[i], P * j:P * j + P],
                                                    w(wname, i), start=i == 0, stop=i == 1)
                            ins.then_inc(oe_ps, 1)
                else:
                    pe.wait_ge(dma_moe, 32)
                    turn(k, g, y, norm_no(k, g))
                    pe.wait_ge(t_sb, t0 + g + 1)

                    def downs(n):
                        pe.wait_ge(h_mul, H_MUL[L3F] + NCHUNK3 * g + n + 1)
                        ins = pe.matmul(PS[:, 4, :], WD[:, n // 4, n % 4, :], Hs[:, 2 + n % 3, :], start=n == 0, stop=n == NCHUNK3 - 1)
                        ins.then_inc(d_ps, 1)

                    for n in range(NCHUNK3):
                        if n >= 2:
                            pe.wait_ge(h_mul, H_MUL[L3F] + NCHUNK3 * g + n - 1)
                        e, c = n // 4, n % 4
                        pe.matmul(PS[:, n % 2, :], WGU[:, e, 0, P * c:P * c + P], yT[:, :], start=True, stop=True)
                        pe.matmul(PS[:, 2 + n % 2, :], WGU[:, e, 1, P * c:P * c + P], yT[:, :], start=True, stop=True).then_inc(h_ps, 1)
                        if n >= 2:
                            downs(n - 2)
                    downs(NCHUNK3 - 2)
                    downs(NCHUNK3 - 1)
                    turn_back(2 * NG + g + 1)
                    pe.wait_ge(x_ready, x_after(k - 1) + g + 1)

            for k in range(9):
                if k > 0:
                    pe.wait_ge(x_ready, x_after(k - 1))
                groups(pe, lambda g, k=k: group_work(k, g))
                if k in ATT:
                    pairs(k)


def kernel(**inputs):
    import numpy as np
    import concourse.bacc as bacc
    from concourse import mybir as mb
    from concourse.bass_utils import run_bass_kernel_spmd

    a = {k: np.asarray(v) for k, v in inputs.items()}
    f = np.float32

    def chunks(m):
        return m.reshape(-1, 128, m.shape[1]).transpose(1, 0, 2).reshape(128, -1)

    def low(m):
        return np.concatenate([m, np.zeros((128 - m.shape[0], m.shape[1]), f)])

    def col(v):
        return v.reshape(-1, 128).T

    cols = {
        "L0_WQ": a["L0_xattn_WQ"], "L0_WK": a["L0_xattn_WK"], "L0_WV": a["L0_xattn_WV"], "L0_WO": a["L0_xattn_WO"],
        "U1": a["L0_ffn_U1"], "V1": low(a["L0_ffn_V1"]), "U2": chunks(a["L0_ffn_U2"]), "V2": low(a["L0_ffn_V2"]),
        "L1_Wq": a["L1_xattn_Wq"], "L1_Wk": a["L1_xattn_Wk"], "L1_Wv": a["L1_xattn_Wv"], "L1_Wo": a["L1_xattn_Wo"],
        "W1T": a["L1_ffn_W1"].T, "W2T": chunks(a["L1_ffn_W2"].T),
        "L2_q": np.tile(a["L2_xattn_Wq"].T, (16, 1)), "L2_k": np.tile(a["L2_xattn_Wk"].T, (16, 1)),
        "L2_v": np.tile(a["L2_xattn_Wv"].T, (16, 1)), "L2_WoT": a["L2_xattn_Wo"].T,
        "wqkT": np.concatenate([a["L2_ffn_wq"].T, a["L2_ffn_wk"].T], 1), "wvT": a["L2_ffn_wv"].T,
        "woT": a["L2_ffn_wo"].T, "gateT": a["L2_ffn_gate_w"].T,
        "e0_up": a["L2_ffn_e0_up"].T, "e0_down": chunks(a["L2_ffn_e0_down"].T),
        "e1_w1": a["L2_ffn_e1_w1"].T, "e1_w2": a["L2_ffn_e1_w2"].T, "e1_down": chunks(a["L2_ffn_e1_down"].T),
        "e2_l1": a["L2_ffn_e2_l1"].T, "e2_l2": chunks(a["L2_ffn_e2_l2"].T), "e2_l3": chunks(a["L2_ffn_e2_l3"].T),
        "e2_l4": chunks(a["L2_ffn_e2_l4"].T),
        "e3_down": a["L2_ffn_e3_down"].T, "e3_up": a["L2_ffn_e3_up"].T, "e3_out": chunks(a["L2_ffn_e3_out"].T),
        "L3_Wq": a["L3_xattn_W_q"], "L3_Wkv": a["L3_xattn_W_kv"], "L3_Wout": a["L3_xattn_W_out"],
        "c_L0b1": col(a["L0_ffn_b1"]), "c_L0b2": col(a["L0_ffn_b2"]),
        "c_bq": col(a["L1_xattn_bq"]), "c_bk": col(a["L1_xattn_bk"]), "c_bv": col(a["L1_xattn_bv"]),
        "c_L1b1": col(a["L1_ffn_b1"]), "c_L1b2": col(a["L1_ffn_b2"]),
        "c_n1": col(a["L2_ffn_n1_w"]), "c_n2": col(a["L2_ffn_n2_w"]),
        "c_qn": col(np.tile(a["L2_ffn_qn_w"], 16)), "c_kn": col(np.tile(a["L2_ffn_kn_w"], 16)),
        "c_lxg": col(a["L3_xattn_ln_x_g"]), "c_lxb": col(a["L3_xattn_ln_x_b"]),
        "c_llg": col(a["L3_xattn_ln_l_g"]), "c_llb": col(a["L3_xattn_ln_l_b"]),
        "c_qg": col(np.tile(a["L3_xattn_q_gamma"], 2)), "c_kg": col(np.tile(a["L3_xattn_k_gamma"], 2)),
        "c_scale": np.tile(a["L1_ffn_scale"].reshape(1, 1), (128, 1)),
    }
    ctx = a["ctx_1024"]
    bools = np.zeros((B, S, 4), np.uint8)
    bools[:, :, 0] = a["mask_BxS2_bk0"].view(np.uint8)
    ctx_T = ctx.transpose(2, 0, 1).reshape(128, NG, BPG, 1, S)
    arrays = {
        "x": a["x"].reshape(NPAIR, P, D).transpose(1, 0, 2),
        "ctx_tok": ctx.reshape(NPAIR, P, D).transpose(1, 0, 2),
        "ctx_T2": np.concatenate([ctx_T, ctx_T], 3),
        "mask_q": a["mask_BxS2_ik0"].reshape(NPAIR, P).T,
        "mask_qk": a["mask_Bx1xSxS2_if1"].reshape(NPAIR, P, S).transpose(1, 0, 2),
        "mask_key": bools.view(np.int32).reshape(NPAIR, 2, S).transpose(1, 0, 2),
        "pack": np.concatenate([cols[n] for n, _ in PACK], 1),
        "rows": np.concatenate([a["L1_xattn_bo"], a["L2_xattn_bo"], a["L3_xattn_b_out"]]).reshape(1, 384),
        "lora_A": np.stack([a["L1_xattn_A" + n].T for n in "qkvo"], 1),
        "lora_B": np.stack([a["L1_xattn_B" + n] for n in "qkvo"], 1),
        "gate_up": np.stack([a["L3_ffn_Wg"].transpose(1, 0, 2), a["L3_ffn_Wu"].transpose(1, 0, 2)], 2),
        "down": a["L3_ffn_Wd"].reshape(8, 4, 128, 128).transpose(2, 0, 1, 3),
    }
    nc = bacc.Bacc("TRN2", target_bir_lowering=False, num_devices=1)
    feed, args = {}, {}
    for name, v in arrays.items():
        v = np.ascontiguousarray(v)
        feed[name + "_dram"] = v
        args[name] = nc.dram_tensor(name + "_dram", v.shape, mb.dt.from_np(v.dtype), kind="ExternalInput").ap()
    args["out"] = nc.dram_tensor("out_dram", (P, NPAIR, D), mb.dt.from_np(np.dtype("float32")), kind="ExternalOutput").ap()
    build_program(nc, **args)
    r = run_bass_kernel_spmd(nc, [feed], core_ids=[0])
    got = r.results[0]["out_dram"]
    return got.transpose(1, 0, 2).reshape(B, S, D)
```

```python
from contextlib import ExitStack

import concourse.bass as bass
from concourse import mybir

P = 128
B, S, D = 32, 64, 128
NPAIR = B * S // P
NG = 4
PPG = NPAIR // NG
BPG = B // NG
GT = PPG * P
F32 = mybir.dt.float32
BF16 = mybir.dt.bfloat16
F32R = mybir.dt.float32r
ALU = mybir.AluOpType
ACT = mybir.ActivationFunctionType
AX = mybir.AxisListType.X

LN_EPS, RMS_EPS, RMS3_EPS = 1e-5, 1.1920929e-07, 1e-8
FLT_MAX = 3.4028234e38

L0A, L0F, L1A, L1F, L2A, L2F, L2M, L3A, L3F = range(9)
ATT = {L0A: 0, L1A: 1, L2A: 2, L2F: 3, L3A: 4}
NORMS = [1, 1, 1, 1, 1, 2, 1, 3, 1]
TURNS = [1, 1, 1, 1, 1, 1, 1, 2, 1]


def before(counts, k):
    return NG * sum(counts[:k])


X_UPS = [NPAIR if k in ATT else NG for k in range(9)]


def x_after(k):
    return sum(X_UPS[:k + 1])


PACK = [("L0_WQ", 128), ("L0_WK", 128), ("L0_WV", 128), ("L0_WO", 128),
        ("U1", 32), ("V1", 512), ("U2", 128), ("V2", 128),
        ("L1_Wq", 128), ("L1_Wk", 128), ("L1_Wv", 128), ("L1_Wo", 128),
        ("W1T", 512), ("W2T", 512),
        ("L2_q", 8), ("L2_k", 8), ("L2_v", 8), ("L2_WoT", 128),
        ("wqkT", 256), ("wvT", 128), ("woT", 128), ("gateT", 4),
        ("e0_up", 256), ("e0_down", 256), ("e1_w1", 256), ("e1_w2", 256), ("e1_down", 256),
        ("e2_l1", 256), ("e2_l2", 512), ("e2_l3", 512), ("e2_l4", 256),
        ("e3_down", 128), ("e3_up", 256), ("e3_out", 256),
        ("L3_Wq", 128), ("L3_Wkv", 256), ("L3_Wout", 128),
        ("c_L0b1", 4), ("c_L0b2", 1), ("c_bq", 1), ("c_bk", 1), ("c_bv", 1),
        ("c_L1b1", 4), ("c_L1b2", 1), ("c_n1", 1), ("c_n2", 1), ("c_qn", 1), ("c_kn", 1),
        ("c_lxg", 1), ("c_lxb", 1), ("c_llg", 1), ("c_llb", 1), ("c_qg", 1), ("c_kg", 1),
        ("c_scale", 1)]
OFF = {}
_at = 0
for _n, _w in PACK:
    OFF[_n] = (_at, _w)
    _at += _w
NPACK = _at


MOE_CHUNKS = [("e2_l1", 0, 0), ("e2_l1", 1, 1), ("e3_down", 0, 2), ("e0_up", 0, 8), ("e0_up", 1, 9),
              ("e2_l2", 0, 6), ("e2_l2", 1, 7), ("e3_up", 0, 10), ("e3_up", 1, 11),
              ("e2_l3", 0, 0), ("e2_l3", 1, 1),
              ("e1_w1", 0, 4), ("e1_w2", 0, None), ("e1_w1", 1, 5), ("e1_w2", 1, None)]
MOE_IN = {"e2_l2": ([0, 1], 1), "e2_l3": ([6, 7], 6), "e3_up": ([2], 2)}
MOE_OUTS = [(6, 0, "e0_down", (8, 9), 4), (12, 3, "e3_out", (10, 11), 8),
            (14, 2, "e2_l4", (0, 1), 10), (14, 1, "e1_down", (4, 5), 13)]
NCH = len(MOE_CHUNKS)


def acts_through(n):
    return sum(dst is not None for _, _, dst in MOE_CHUNKS[:n + 1])


NACT = acts_through(NCH - 1)
H_PS = {L0F: 0, L1F: NG * 6, L2M: NG * 10, L3F: NG * (10 + NCH)}
H_SB = {L0F: 0, L1F: NG * 6, L2M: NG * 10, L3F: NG * (10 + NACT)}
H_MUL = {L2M: 0, L3F: NG * 2}
NCH3 = 32
LAG3 = 2


def chunked(eng, body):
    for par in range(2):
        body(0, par, par == 0, False)
    with eng.Fori(1, NCH3 // 2 - 1) as j:
        for par in range(2):
            body(j, par, False, False)
    for par in range(2):
        body(NCH3 // 2 - 1, par, False, par == 1)


def groups(eng, body):
    body(0)
    with eng.Fori(1, NG) as g:
        body(g)


def wait(eng, sem, value):
    if isinstance(value, int) and value <= 0:
        return
    eng.wait_ge(sem, value)


KX_DVE = 4


def pipelined(eng, steps, unit=2):
    lo = min(lag for lag, _ in steps)
    hi = max(lag for lag, _ in steps)
    first = hi + hi % 2 + 2
    last = NPAIR + min(lo, 0)
    last -= (last - first) % 2

    def turn(t, static):
        for lag, step in steps:
            p = t - lag
            if static and not 0 <= p < NPAIR:
                continue
            step(p, None)

    for t in range(lo, first):
        turn(t, True)
    with eng.Fori(0, (last - first) // 2) as j:
        for half in range(2):
            for lag, step in steps:
                step(2 * j + (first + half - lag), (first + half - lag) % 2)
    for t in range(last, NPAIR + hi):
        turn(t, True)


def build_program(nc, x, ctx_tok, ctx_T2, mask_q, mask_qk, mask_key, pack, rows, lora_A, lora_B,
                  experts, out):
    es = ExitStack()
    with es:
        def sb(name, shape, dt=F32):
            return es.enter_context(nc.sbuf_tensor(name, shape, dt))

        def sem(name):
            return es.enter_context(nc.semaphore(name))

        X = sb("X", [P, NPAIR, D])
        Zr = sb("Zr", [P, NPAIR, D])
        CTX = Zr
        arena = sb("arena", [P, 12 * GT])
        W = sb("W", [P, NPACK])
        ROWS = sb("ROWS", [1, 3 * D])
        XH = sb("XH", [P, NG, GT], F32R)
        XL = sb("XL", [P, NG, GT], F32R)
        EW = sb("EW", [P, 2, 3 * P])
        EH = sb("EH", [P, 2, 3 * P], F32R)
        EL = sb("EL", [P, 2, 3 * P], F32R)
        HH = sb("HH", [P, NG, GT], F32R)
        HL = sb("HL", [P, NG, GT], F32R)
        QT = sb("QT", [P, NPAIR, P])
        KT = sb("KT", [P, B, P])
        KT64 = KT[:, 0:B // 2, :].rearrange("p a (b k) -> p (a b) k", k=S)
        V = sb("V", [P, B, D])
        ctx2 = sb("ctx2", [P, BPG, 2, S])
        yT2 = CL = ctx2
        LA = arena[0:16, 0:512].rearrange("p (n d) -> p n d", n=4)
        LB = arena[0:16, 512:1024].rearrange("p (n d) -> p n d", n=4)
        Kx = arena[:, 0:4096].rearrange("p (r b c) -> p r b c", r=2, b=2)
        Qs = sb("Qs", [P, 2, P])
        PR = arena[:, 4096:6144].rearrange("p (r c) -> p r c", r=2)
        arena2 = sb("arena2", [P, 4 * GT])
        PT = arena2[:, :].rearrange("p (r n q) -> p r n q", r=2, n=8)
        Vz = sb("Vz", [P, 2, 2, 384])
        cT = sb("cT", [P, 2, P])
        mx = sb("mx", [P, 2, 16])
        Oz = sb("Oz", [P, 384])
        rcT = sb("rcT", [P, P])
        kd = sb("kd", [P, 2, P], BF16)
        st = sb("st", [P, PPG, 6])
        spare = sb("spare", [P, 2])
        mv = sb("mv", [P, PPG, 2])
        ve = sb("ve", [P, PPG])
        rstd = sb("rstd", [P, PPG])
        y = arena2[:, 0:GT].rearrange("p (j d) -> p j d", d=D)
        yy = arena2[:, GT:2 * GT].rearrange("p (j d) -> p j d", d=D)
        yT = arena2[:, 2 * GT:3 * GT]
        Hs = arena[:, :].rearrange("p (n t) -> p n t", n=12)
        oT = arena2[:, 3 * GT:4 * GT]
        sG = arena[:, 0:2 * GT].rearrange("p (n t) -> p n t", n=2)
        Hf = arena[:, 2 * GT:4 * GT].rearrange("p (n t) -> p n t", n=2)
        oT3 = arena[:, 4 * GT:8 * GT].rearrange("p (n t) -> p n t", n=4)
        sq = arena[:, 2048:3584]
        ss = sb("ss", [P, 128])
        rs = sb("rs", [P, 128])
        rt = sb("rt", [P, 128])
        qkn = arena[:, 0:1536]
        oddT = sb("oddT", [P, 2, BPG, 4])
        Er = sb("Er", [32, 4, D])
        E2 = sb("E2", [P, 4, 32])
        XO = sb("XO", [32, BPG, S])
        part = sb("part", [P, GT])
        GM = part[:, :].rearrange("p (b s) -> p b s", s=S)
        lg = sb("lg", [P, PPG, 4])
        fin = sb("fin", [P, PPG, 4], mybir.dt.uint32)
        lgz = sb("lgz", [P, PPG, 4])
        gmx = sb("gmx", [P, PPG])
        gs = sb("gs", [P, PPG])
        cmp = sb("cmp", [P, PPG, 4, 4])
        tie = sb("tie", [P, PPG, 4, 4])
        rank = sb("rank", [P, PPG, 4])
        moe = part[:, :].rearrange("p (j d) -> p j d", d=D)
        zero = arena2[:, 0:512]
        ident = sb("ident", [P, P])
        identb = sb("identb", [P, P], BF16)
        hm16a = sb("hm16a", [P, 16])
        hm16 = sb("hm16", [P, 16])
        hm2 = sb("hm2", [P, 2])
        causal = sb("causal", [P, S], BF16)
        causalf = sb("causalf", [P, S])
        ones = sb("ones", [P, P])
        sel2f = sb("sel2f", [2, 2, S])
        sel2 = sb("sel2", [2, P], BF16)
        low4 = sb("low4", [P, 4, 4])
        eps_c = sb("eps_c", [P, 3])
        mhalf = sb("mhalf", [P, 32])
        Sel1 = sb("Sel1", [P, PPG, BPG, 4])
        Sel2 = sb("Sel2", [P, PPG, 4, 32])
        mB = sb("mB", [P, 4, BPG])
        dB = sb("dB", [P, BPG])
        mR = sb("mR", [P, 32, 4])
        dR = sb("dR", [P, 4])
        mq_i = sb("mq_i", [P, NPAIR], mybir.dt.int32)
        keep = sb("keep", [P, NPAIR])
        mqk_i = arena[:, 4096:5120].bitcast(mybir.dt.int32).rearrange("p (n k) -> p n k", k=S)
        mqk = sb("mqk", [P, NPAIR, S], BF16)
        mk_i = arena[0:2, 5120:6144].bitcast(mybir.dt.int32).rearrange("p (n k) -> p n k", k=S)
        mk = sb("mk", [2, NPAIR, S], BF16)
        W1m = sb("W1m", [P, 4, D])
        BD = sb("BD", [P, 3, 16, 8])

        PS = es.enter_context(nc.psum_tensor("PS", [P, 8, 512], F32))
        PSf = PS[:, :, :].rearrange("p a b -> p (a b)")

        def w(name, i=None, n=128, rows_=P):
            o, size = OFF[name]
            if i is None:
                return W[0:rows_, o:o + size]
            return W[0:rows_, o + i * n:o + (i + 1) * n]

        def col(name, i=0):
            o = OFF[name][0] + i
            return W[:, o:o + 1]

        dma_x, dma_ctx, dma_pack, dma_small, dma_ctx2, dma_out = (
            sem(n) for n in ("dma_x", "dma_ctx", "dma_pack", "dma_small", "dma_ctx2", "dma_out"))
        consts, consts_v, lora_ps, x_ready = (sem(n) for n in ("consts", "consts_v", "lora_ps", "x_ready"))
        n_stats, n_aggr, n_ve, n_rstd, n_done = (sem("n_" + n) for n in ("stats", "aggr", "ve", "rstd", "done"))
        t_ps, t_sb, z_copied = (sem(n) for n in ("t_ps", "t_sb", "z_copied"))
        kv_ps, q_ps, k_sb, v_sb, q_sb = (sem("p_" + n) for n in ("kv_ps", "q_ps", "k_sb", "v_sb", "q_sb"))
        sq_sb, ss_sb, rs_sb, qkn_sb, qk_turned = (sem("r_" + n) for n in ("sq", "ss", "rs", "qkn", "turned"))
        kx_v, kx_p, qs_sb, sc_ps, mx_sb, sub_sb, exp_sb, rc_sb, row_sb = (
            sem("a_" + n) for n in ("kx_v", "kx_p", "qs", "sc", "mx", "sub", "exp", "rc", "row"))
        pt_ps, pt_sb, vz_sb, pv_ps, ct_sb, o_ps, kd_sb = (
            sem("a_" + n) for n in ("pt_ps", "pt_sb", "vz", "pv", "ct", "o", "kd"))
        h_ps, h_sb, h_mul, acc_ps, o_sb, ot_ps = (sem("f_" + n) for n in ("h_ps", "h_sb", "h_mul", "acc", "o_sb", "ot"))
        e_ps, e_sb, odd_sb, xo_ps, xo_sb, g_ps, g_sb = (
            sem("l_" + n) for n in ("e_ps", "e_sb", "odd", "xo_ps", "xo_sb", "g_ps", "g_sb"))
        lg_ps, gate_v, gate_e, wt_sb, oe_ps, derived = (
            sem("m_" + n) for n in ("lg", "gate_v", "gate_e", "wt", "oe", "derived"))
        sums_sb, root_sb, n_gate, w_done, moe_sb, x_part, n_ms, n_kp = (
            sem(n) for n in ("r_sums", "r_root", "m_gate2", "m_w", "m_sum", "m_x", "n_ms", "n_kp"))

        dma_moe = [sem(f"dma_moe{m}") for m in range(2)]
        xh_sb, eh_sb, el_sb, sg_sb, hf_sb, hh_sb, hl_sb, gu_ps, d_ps = (
            sem("e_" + n) for n in ("xh", "eh", "el", "sg", "hf", "hh", "hl", "gu", "down"))

        SMALL = 16 * 6
        TOK = [L0A, L1A, L2A]

        block = es.enter_context(nc.Block())

        @block.sync
        def _(sp):
            sp.dma_start(X[:, :, :], x).then_inc(dma_x, 16)
            sp.dma_start(W[:, 0:NPACK // 2], pack[:, 0:NPACK // 2]).then_inc(dma_pack, 16)
            sp.dma_start(W[:, NPACK // 2:NPACK], pack[:, NPACK // 2:NPACK]).then_inc(dma_pack, 16)
            sp.dma_start(ctx2[:, :, :, :], ctx_T2[:, 0, :, :, :]).then_inc(dma_ctx2, 16)
            for a in range(3):
                with sp.Fori(int(a == 0), NG) as g:
                    sp.wait_ge(kv_ps, NG * a + g)
                    sp.dma_start(ctx2[:, :, :, :], ctx_T2[:, g, :, :, :]).then_inc(dma_ctx2, 16)
            sp.wait_ge(x_ready, x_after(L2M))
            sp.dma_start(CTX[:, :, :], ctx_tok).then_inc(dma_ctx, 16)
            for par in range(2):
                sp.dma_start(EW[:, par, :], experts[:, par, :]).then_inc(dma_moe[par], 16)
            with sp.Fori(1, NCH3 // 2) as j:
                for par in range(2):
                    sp.wait_ge(el_sb, 2 * j + par - 1)
                    sp.dma_start(EW[:, par, :], experts[:, 2 * j + par, :]).then_inc(dma_moe[par], 16)
            for g in range(NG):
                sp.wait_ge(x_ready, x_after(L3A) + g + 1)
                sp.dma_start(out[:, PPG * g:PPG * (g + 1), :], X[:, PPG * g:PPG * (g + 1), :]).then_inc(dma_out, 16)
            sp.wait_ge(dma_out, 16 * NG)

        @block.gpsimd
        def _(pool):
            pool.memset(zero[:, :], 0.0).then_inc(consts, 1)
            pool.memset(ones[:, :], 1.0).then_inc(consts, 1)
            pool.memset(mhalf[:, :], -0.5).then_inc(consts, 1)
            pool.memset(eps_c[:, 0:1], LN_EPS).then_inc(consts, 1)
            pool.memset(eps_c[:, 1:2], RMS_EPS).then_inc(consts, 1)
            pool.memset(eps_c[:, 2:3], 0.0).then_inc(consts, 1)
            pool.memset(causalf[:, :], 0.0).then_inc(consts, 1)
            pool.memset(Vz[:, :, :, :], 0.0).then_inc(consts, 1)
            pool.memset(Oz[:, :], 0.0).then_inc(consts, 1)
            pool.wait_ge(consts, 9)

            def pick(o, src, pattern, base, cm, op=ALU.not_equal, fill=1.0):
                pool.affine_select(out=o, in_=src, compare_op=op, fill=fill, base=base, pattern=pattern,
                                   channel_multiplier=cm).then_inc(consts, 1)

            pick(ident[:, :], zero[:, 0:P], [[-1, P]], 0, 1)
            pick(hm16a[:, :], mhalf[:, 0:16], [[-8, 16]], 0, 1, ALU.is_ge, 0.0)
            pick(mB[:, :, :], mhalf[:, 0:32].rearrange("p (c b) -> p c b", c=4), [[-32, 4], [-4, 8]], 0, 1, ALU.is_ge, 0.0)
            pick(mR[:, :, :], zero[:, 0:128].rearrange("p (m r) -> p m r", r=4), [[-4, 32], [-1, 4]], 0, 1)
            pick(Sel1[:, :, :, :], zero[:, 0:128].rearrange("p (j b r) -> p j b r", j=4, b=8),
                 [[128, 4], [-64, 8], [-2, 4]], -1, 1)
            pick(Sel2[:, :, :, :].rearrange("p j c (b r) -> p j c b r", b=8),
                 zero[:, 0:512].rearrange("p (j c b r) -> p j c b r", j=4, c=4, b=8),
                 [[128, 4], [0, 4], [-64, 8], [-2, 4]], -9, 1)
            pool.wait_ge(consts, 15)
            pick(hm16[:, :], hm16a[:, :], [[8, 16]], 7, -1, ALU.is_ge, 0.0)
            pick(mB[:, :, :], mB[:, :, :], [[32, 4], [4, 8]], 3, -1, ALU.is_ge, 0.0)
            pick(hm2[:, :], mhalf[:, 0:2], [[-64, 2]], 0, 1, ALU.is_ge, 0.0)
            pick(low4[:, :, :], zero[:, 0:16].rearrange("p (e j) -> p e j", e=4), [[-1, 4], [1, 4]], 0, 0, ALU.is_ge, 1.0)
            pool.wait_ge(consts, 19)
            pick(hm2[:, :], hm2[:, :], [[64, 2]], 63, -1, ALU.is_ge, 0.0)
            pool.wait_ge(consts, 20)
            pick(sel2f[:, :, :], zero[0:2, 0:P].rearrange("p (b q) -> p b q", b=2), [[-1, 2], [0, S]], 0, 1)
            pool.wait_ge(consts, 21)
            pick(causalf[0:64, :], causalf[0:64, :], [[-1, S]], 0, 1, ALU.is_ge, -1e9)
            pool.wait_ge(consts, 22)
            pick(causalf[64:128, :], causalf[64:128, :], [[-1, S]], 0, 1, ALU.is_ge, -1e9)
            for h in range(2):
                pool.memset(Oz[64 * h:64 * h + 64, :].rearrange("p (n c) -> p n c", c=48)[:, :, 8 * h:8 * h + 8],
                            1.0).then_inc(consts, 1)

            def rstd_of(v, eps, ms=None, kp=None):
                pool.wait_ge(n_aggr, v)
                var, mu = mv[:, :, 1], mv[:, :, 0]
                if ms is not None:
                    pool.tensor_tensor(rstd[:, :], mu, mu, ALU.mult).then_inc(n_ms, 1)
                    pool.wait_ge(n_ms, 2 * ms + 1)
                    pool.tensor_tensor(rstd[:, :], var, rstd[:, :], ALU.add).then_inc(n_ms, 1)
                    pool.wait_ge(n_ms, 2 * ms + 2)
                    var = rstd[:, :]
                pool.tensor_tensor(ve[:, :], var, eps_c[:, eps:eps + 1].to_broadcast([P, PPG]), ALU.add).then_inc(n_ve, 1)
                pool.wait_ge(n_ve, v)
                if kp is None:
                    pool.tensor_tensor(rstd[:, :], ve[:, :], mhalf[:, 0:PPG], ALU.pow).then_inc(n_rstd, 1)
                else:
                    pool.tensor_tensor(ve[:, :], ve[:, :], mhalf[:, 0:PPG], ALU.pow).then_inc(n_kp, 1)
                    pool.wait_ge(n_kp, v)
                    pool.tensor_tensor(rstd[:, :], ve[:, :], kp, ALU.mult).then_inc(n_rstd, 1)

            def norms(k, g, t=0):
                return before(NORMS, k) + NORMS[k] * g + t + 1

            def pairs(a, nh, nk):
                hm = hm16 if nh == 16 else hm2
                nc_ = nh * nk
                kt = KT64 if nk == S else KT[:, :, :]

                def spread(p, par):
                    par = p % 2 if par is None else par
                    wait(pool, sc_ps, NPAIR * a + p - 1)
                    for b in range(2):
                        h0 = (nh if nh == 2 else KX_DVE) if b == 0 else 0
                        if h0 < nh:
                            ins = pool.tensor_tensor(Kx[:, par, b, h0 * nk:nc_].rearrange("p (h k) -> p h k", k=nk),
                                                     kt[:, 2 * p + b, :].unsqueeze(1).to_broadcast([P, nh - h0, nk]),
                                                     hm[:, h0:nh].unsqueeze(2).to_broadcast([P, nh - h0, nk]),
                                                     ALU.mult)
                    ins.then_inc(kx_p, 1)

                pool.wait_ge(k_sb, NG * (a + 1))
                pipelined(pool, [(-1, spread)])

            pool.wait_ge(consts_v, 1)
            def group_norms(k, g):
                if k == L0A:
                    rstd_of(norms(k, g), 0, kp=keep[:, :].rearrange("p (g j) -> p g j", j=PPG)[:, g, :])
                elif k == L2M:
                    rstd_of(norms(k, g), 1, ms=NG + g)
                else:
                    rstd_of(norms(k, g), 0)
                if k == L2F:
                    pool.wait_ge(n_done, norms(k, g))
                    pool.tensor_copy(Zr[:, :, :].rearrange("p (g j) d -> p g j d", j=PPG)[:, g], y[:, :, :])\
                        .then_inc(z_copied, 1)
                    rstd_of(norms(k, g, 1), 1, ms=g)
                if k == L3A:
                    rstd_of(norms(k, g, 1), 0)
                    rstd_of(norms(k, g, 2), 0)
            for k in range(9):
                groups(pool, lambda g, k=k: group_norms(k, g))
                if k in ATT:
                    pairs(ATT[k], *((2, 128) if k == L3A else (16, 64)))

        @block.scalar
        def _(act):
            act.dma_start(ROWS[:, :], rows).then_inc(dma_small, 16)
            act.dma_start(LA[:, :, :], lora_A).then_inc(dma_small, 16)
            act.dma_start(LB[:, :, :], lora_B).then_inc(dma_small, 16)
            act.dma_start(mq_i[:, :], mask_q).then_inc(dma_small, 16)
            act.dma_start(mqk_i[:, :, :], mask_qk).then_inc(dma_small, 16)
            act.dma_start(mk_i[:, :, :], mask_key).then_inc(dma_small, 16)
            act.wait_ge(consts_v, 1)

            def turned(k, g, t=0):
                return before(TURNS, k) + TURNS[k] * g + t + 1

            def turn_out(k, g, t, outs, scale=None, bias=None):
                act.wait_ge(t_ps, turned(k, g, t))
                for n, o in enumerate(outs):
                    src = PS[:, 7, :]
                    if len(o.shape) == 3:
                        src = src.rearrange("p (b s) -> p b s", s=S)
                    if scale is None:
                        ins = act.activation(o, src, ACT.Copy)
                    else:
                        ins = act.activation(o, src, ACT.Identity, bias=bias if bias is not None else 0.0, scale=scale)
                ins.then_inc(t_sb, 1)

            def pairs(k):
                a = ATT[k]
                L3 = k == L3A
                nc_ = 256 if L3 else 1024
                scale = {L0A: 8 ** -0.5, L1A: 8 ** -0.5, L2A: 128 ** -0.5, L2F: 8 ** -0.5, L3A: 64 ** -0.5}[k]

                def exps(p, par):
                    par = p % 2 if par is None else par
                    act.wait_ge(sub_sb, NPAIR * a + p + 1)
                    act.activation(PR[:, par, 0:nc_], PR[:, par, 0:nc_], ACT.Exp, scale=scale).then_inc(exp_sb, 1)

                def query(p, par):
                    par = p % 2 if par is None else par
                    wait(act, sc_ps, NPAIR * a + p - 1)
                    act.activation(Qs[:, par, :], QT[:, p, :], ACT.Copy).then_inc(qs_sb, 1)

                def values(p, par):
                    par = p % 2 if par is None else par
                    wait(act, pv_ps, NPAIR * a + p - 1)
                    if L3:
                        ins = act.activation(Vz[:, par, :, 0:P], V3p(p), ACT.Copy)
                    else:
                        for h in range(2):
                            dst = Vz[64 * h:64 * h + 64, par, :, :].rearrange("p b (n c) -> p b n c", c=48)[:, :, :, 8 * h:8 * h + 8]
                            src = V3p(p)[64 * h:64 * h + 64].rearrange("p b (n c) -> p b n c", c=16)[:, :, :, 8 * h:8 * h + 8]
                            ins = act.activation(dst, src, ACT.Copy)
                    ins.then_inc(vz_sb, 1)

                def V3p(p):
                    return V[:, :, :].rearrange("p (a b) d -> p a b d", b=2)[:, p]

                def probs_out(p, par):
                    par = p % 2 if par is None else par
                    n = nc_ // P // 2
                    wait(act, pv_ps, NPAIR * a + p - 1)
                    for half in range(2):
                        act.wait_ge(pt_ps, 2 * (NPAIR * a + p) + half + 1)
                        act.activation(PT[:, par, n * half:n * (half + 1), :],
                                       PS[:, 4 + half, 0:n * P].rearrange("p (n q) -> p n q", n=n),
                                       ACT.Copy).then_inc(pt_sb, 1)

                pipelined(act, [(-1, query), (0, values), (1, probs_out), (0, exps)])

            def half_root(u, n):
                act.wait_ge(ss_sb, u + 1)
                act.activation(rt[:, 0:n], ss[:, 0:n], ACT.Sqrt, scale=0.25).then_inc(root_sb, 1)

            def group_work(k, g):
                if k in TOK:
                    a = ATT[k]
                    act.wait_ge(kv_ps, NG * a + g + 1)
                    kdst = KT64.rearrange("p (g b) s -> p g (b s)", b=BPG)[:, g]
                    if k == L1A:
                        act.activation(kdst, PS[:, 1, :], ACT.Identity, bias=col("c_bk")).then_inc(k_sb, 1)
                    else:
                        act.activation(kdst, PS[:, 1, :], ACT.Copy).then_inc(k_sb, 1)
                    turn_out(k, g, 0, [yT[:, :]])
                    act.wait_ge(q_ps, NG * a + g + 1)
                    qdst = QT[:, :, :].rearrange("p (g j) q -> p g (j q)", j=PPG)[:, g]
                    if k == L1A:
                        act.activation(qdst, PS[:, 0, :], ACT.Identity, bias=col("c_bq")).then_inc(q_sb, 1)
                    else:
                        act.activation(qdst, PS[:, 0, :], ACT.Copy).then_inc(q_sb, 1)
                elif k == L2F:
                    turn_out(k, g, 0, [yT2[:, :, 0, :], yT2[:, :, 1, :], yT[:, :]], scale=col("c_n1"))
                    act.wait_ge(q_ps, NG * 3 + g + 1)
                    act.activation(sq[:, 0:1024], PSf[:, 0:1024], ACT.Square).then_inc(sq_sb, 1)
                    half_root(g, 128)
                    act.wait_ge(qk_turned, g + 1)
                    act.activation(QT[:, :, :].rearrange("p (g j) q -> p g (j q)", j=PPG)[:, g], PS[:, 5, :],
                                   ACT.Identity, scale=col("c_qn")).then_inc(q_sb, 1)
                    act.activation(KT64.rearrange("p (g b) s -> p g (b s)", b=BPG)[:, g], PS[:, 6, :],
                                   ACT.Identity, scale=col("c_kn")).then_inc(k_sb, 1)
                elif k == L3A:
                    turn_out(k, g, 0, [CL[:, :, 1, :], yT[:, :]], scale=col("c_llg"), bias=col("c_llb"))
                    turn_out(k, g, 1, [CL[:, :, 0, :]], scale=col("c_lxg"), bias=col("c_lxb"))
                    act.wait_ge(q_ps, NG * 4 + g + 1)
                    kps = PSf[:, 0:2048].rearrange("p (b c) -> p b c", c=256)
                    act.activation(sq[:, 0:1024].rearrange("p (b c) -> p b c", c=P), kps[:, :, 0:P], ACT.Square)
                    act.activation(sq[:, 1024:1536], PS[:, 4, :], ACT.Square).then_inc(sq_sb, 1)
                    act.activation(V[:, :, :].rearrange("p (g b) d -> p g b d", b=BPG)[:, g], kps[:, :, P:256],
                                   ACT.Copy).then_inc(v_sb, 1)
                    half_root(NG + g, 24)
                    act.wait_ge(qk_turned, NG + g + 1)
                    act.activation(KT[:, :, :].rearrange("p (g b) s -> p g (b s)", b=BPG)[:, g], PSf[:, 2560:3584],
                                   ACT.Identity, scale=col("c_kg")).then_inc(k_sb, 1)
                    act.activation(QT[:, :, :].rearrange("p (g j) q -> p g (j q)", j=PPG)[:, g], PS[:, 7, :],
                                   ACT.Identity, scale=col("c_qg")).then_inc(q_sb, 1)
                elif k == L0F:
                    turn_out(k, g, 0, [yT[:, :]])
                    u = H_PS[L0F] + 6 * g
                    act.wait_ge(h_ps, u + 1)
                    act.activation(Hs[0:32, 0, :], PS[0:32, 0, :], ACT.Copy).then_inc(h_sb, 1)
                    for c in range(4):
                        act.wait_ge(h_ps, u + 2 + c)
                        act.activation(Hs[:, 1 + c, :], PS[:, (1 + c) % 4, :], ACT.Gelu_apprx_tanh,
                                       bias=col("c_L0b1", c)).then_inc(h_sb, 1)
                    act.wait_ge(h_ps, u + 6)
                    act.activation(Hs[0:32, 5, :], PS[0:32, 5, :], ACT.Copy).then_inc(h_sb, 1)
                    act.wait_ge(acc_ps, g + 1)
                    act.activation(oT[:, :], PS[:, 4, :], ACT.Identity, bias=col("c_L0b2")).then_inc(o_sb, 1)
                elif k == L1F:
                    turn_out(k, g, 0, [yT[:, :]])
                    u = H_PS[L1F] + 4 * g
                    for c in range(4):
                        act.wait_ge(h_ps, u + 1 + c)
                        act.activation(Hs[:, c, :], PS[:, c, :], ACT.Gelu, bias=col("c_L1b1", c)).then_inc(h_sb, 1)
                    act.wait_ge(acc_ps, NG + g + 1)
                    act.activation(oT[:, :], PS[:, 4, :], ACT.Identity, bias=col("c_L1b2")).then_inc(o_sb, 1)
                elif k == L2M:
                    turn_out(k, g, 0, [yT[:, :]], scale=col("c_n2"))
                    act.wait_ge(gate_v, 7 * g + 5)
                    act.activation(lgz[:, :, :], lgz[:, :, :], ACT.Exp).then_inc(gate_e, 1)
                    for n, (name, c, dst) in enumerate(MOE_CHUNKS):
                        if dst is None:
                            continue
                        act.wait_ge(h_ps, H_PS[L2M] + NCH * g + n + 1)
                        act.activation(Hs[:, dst, :], PS[:, n % 4, :],
                                       ACT.Silu if name == "e1_w1" else ACT.Gelu).then_inc(h_sb, 1)
                else:
                    act.wait_ge(t_ps, turned(k, g))
                    act.activation(XH[:, g, :], PS[:, 7, :], ACT.Copy).then_inc(xh_sb, 1)

            def experts_work():
                def high(j, par):
                    act.wait_ge(dma_moe[par], 16 * j + 16)
                    wait(act, d_ps, NG * (2 * j + par - 1))
                    act.activation(EH[:, par, :], EW[:, par, :], ACT.Copy).then_inc(eh_sb, 1)

                def chunk(j, par, first, last):
                    for g in range(NG):
                        u = NG * (2 * j + par) + g
                        act.wait_ge(gu_ps, 2 * u + 1)
                        if g >= 2 or not first:
                            act.wait_ge(hf_sb, u - 1)
                        act.activation(sG[:, g % 2, :], PS[:, g % 2, :], ACT.Silu).then_inc(sg_sb, 1)
                        act.wait_ge(hf_sb, u + 1)
                        if not first:
                            act.wait_ge(d_ps, u - NG + 1)
                        act.activation(HH[:, g, :], Hf[:, g % 2, :], ACT.Copy).then_inc(hh_sb, 1)
                        if g == 2 and not first and not last:
                            high(j + par, 1 - par)

                for par in range(2):
                    high(0, par)
                chunked(act, chunk)
                for g in range(NG):
                    act.wait_ge(d_ps, NG * (NCH3 - 1) + g + 1)
                    act.activation(oT3[:, g, :], PS[:, 4 + g, :], ACT.Copy).then_inc(o_sb, 1)

            for k in range(9):
                if k > 0:
                    act.wait_ge(x_ready, x_after(k - 1))
                groups(act, lambda g, k=k: group_work(k, g))
                if k in ATT:
                    pairs(k)
            experts_work()

        @block.vector
        def _(dve):
            dve.wait_ge(consts, 25)
            dve.wait_ge(dma_small, SMALL)
            dve.wait_ge(dma_pack, 32)
            cv = [0]

            def made(ins):
                cv[0] += 1
                ins.then_inc(derived, 1)

            def settle():
                dve.wait_ge(derived, cv[0])

            made(dve.tensor_copy(identb[:, :], ident[:, :]))
            made(dve.tensor_scalar(hm16[:, :], hm16[:, :], -2.0, None, ALU.mult))
            made(dve.tensor_scalar(hm2[:, :], hm2[:, :], -2.0, None, ALU.mult))
            made(dve.tensor_copy(causal[:, :], causalf[:, :]))
            made(dve.tensor_copy(sel2[:, :], sel2f[:, :, :].rearrange("p b q -> p (b q)")))
            made(dve.tensor_scalar(keep[:, :], mq_i[:, :], 0.0, None, ALU.is_equal))
            made(dve.tensor_scalar(mqk[:, :, :], mqk_i[:, :, :], 0.0, -1e20, ALU.is_equal, ALU.mult))
            made(dve.tensor_scalar(mk[:, :, :], mk_i[:, :, :], 0.0, -1e30, ALU.is_equal, ALU.mult))
            made(dve.tensor_reduce(dB[:, :], mB[:, :, :].rearrange("p c b -> p b c"), AX, ALU.add))
            made(dve.tensor_reduce(dR[:, :], mR[:, :, :].rearrange("p m r -> p r m"), AX, ALU.add))
            settle()
            made(dve.tensor_scalar(dB[:, :], dB[:, :], -2.0, col("c_scale"), ALU.mult, ALU.mult))
            for n, name in enumerate(("L2_q", "L2_k", "L2_v")):
                made(dve.tensor_tensor(BD[:, n, :, :], w(name).unsqueeze(1).to_broadcast([P, 16, 8]),
                                       hm16[:, :].unsqueeze(2).to_broadcast([P, 16, 8]), ALU.mult))
            dve.wait_ge(lora_ps, 1)
            settle()
            for n, name in enumerate(("L1_Wq", "L1_Wk", "L1_Wv", "L1_Wo")):
                ins = dve.scalar_tensor_tensor(W1m[:, n, :], PS[:, 0, P * n:P * n + P], 2.0, w(name), ALU.mult, ALU.add)
            ins.then_inc(consts_v, 1)
            dve.wait_ge(lora_ps, 2)
            dve.tensor_tensor(ROWS[:, 0:D], ROWS[:, 0:D], PS[0:1, 6, 0:D], ALU.add).then_inc(row_sb, 1)
            dve.wait_ge(dma_x, 16)

            def norm_no(k, g, t=0):
                return before(NORMS, k) + NORMS[k] * g + t + 1

            def turned(k, g, t=0):
                return before(TURNS, k) + TURNS[k] * g + t + 1

            def normalise(v, src, dst, mean=True, free=None):
                for j in range(PPG):
                    ins = dve.bn_stats(st[:, j, :], src(j))
                ins.then_inc(n_stats, 1)
                dve.wait_ge(n_stats, v)
                dve.memset(spare[:, 0:1], 0.0)
                for j in range(PPG):
                    ins = dve.bn_aggr(mv[:, j, :], st[:, j, :])
                ins.then_inc(n_aggr, 1)
                if free:
                    free()
                dve.wait_ge(n_rstd, v)
                for j in range(PPG):
                    if mean:
                        ins = dve.tensor_scalar(dst(j), src(j), mv[:, j, 0:1], rstd[:, j:j + 1], ALU.subtract, ALU.mult)
                    else:
                        ins = dve.tensor_scalar(dst(j), src(j), rstd[:, j:j + 1], None, ALU.mult)
                ins.then_inc(n_done, 1)
                dve.wait_ge(n_done, v)

            def group(T, g):
                return T[:, :, :].rearrange("p (g j) d -> p g j d", j=PPG)[:, g]

            def add_group(k, g, u):
                dve.wait_ge(ot_ps, u)
                dve.tensor_tensor(group(X, g), group(X, g), PS[:, 5, :].rearrange("p (j d) -> p j d", j=PPG),
                                  ALU.add).then_inc(x_ready, 1)

            def head_factors(u, n, dim, eps, guard):
                dve.wait_ge(sums_sb, u + 1)
                dve.tensor_scalar(ss[:, 0:n], ss[:, 0:n], 1.0 / dim, eps, ALU.mult, guard).then_inc(ss_sb, 1)
                dve.wait_ge(root_sb, u + 1)
                dve.reciprocal(rs[:, 0:n], rt[:, 0:n]).then_inc(rs_sb, 1)
                dve.wait_ge(rs_sb, 4 * u + 1)
                dve.tensor_tensor(rs[:, 0:n], rs[:, 0:n], ss[:, 0:n], ALU.mult).then_inc(rs_sb, 1)
                dve.wait_ge(rs_sb, 4 * u + 2)
                dve.scalar_tensor_tensor(rs[:, 0:n], rs[:, 0:n], 0.25, rt[:, 0:n], ALU.mult, ALU.add).then_inc(rs_sb, 1)
                dve.wait_ge(rs_sb, 4 * u + 3)
                dve.reciprocal(rs[:, 0:n], rs[:, 0:n]).then_inc(rs_sb, 1)
                dve.wait_ge(rs_sb, 4 * u + 4)

            def pairs(k):
                a = ATT[k]
                L3 = k == L3A
                nh, nk = (2, 128) if L3 else (16, 64)
                nc_ = nh * nk
                hm = hm2 if L3 else hm16
                kt = KT[:, :, :] if L3 else KT64

                def spread(p, par):
                    par = p % 2 if par is None else par
                    wait(dve, sc_ps, NPAIR * a + p - 1)
                    n = min(nh, KX_DVE)
                    dve.tensor_tensor(Kx[:, par, 0, 0:n * nk].rearrange("p (h k) -> p h k", h=n),
                                      kt[:, 2 * p, :].unsqueeze(1).to_broadcast([P, n, nk]),
                                      hm[:, 0:n].unsqueeze(2).to_broadcast([P, n, nk]),
                                      ALU.mult).then_inc(kx_v, 1)
                    if k == L0A:
                        dve.tensor_scalar(kd[:, par, :], identb[:, :], keep[:, :].unsqueeze(2)[:, p, :], None, ALU.mult).then_inc(kd_sb, 1)

                def shift(p, par):
                    par = p % 2 if par is None else par
                    dve.wait_ge(sc_ps, NPAIR * a + p + 1)
                    s = PSf[:, 1024 * par:1024 * par + nc_].rearrange("p (h k) -> p h k", h=nh)
                    dve.tensor_reduce(mx[:, par, 0:nh], s, AX, ALU.max).then_inc(mx_sb, 1)
                    dve.wait_ge(mx_sb, NPAIR * a + p + 1)
                    wait(dve, pt_ps, 2 * (NPAIR * a + p - 1))
                    dve.tensor_tensor(PR[:, par, 0:nc_].rearrange("p (h k) -> p h k", h=nh), s,
                                      mx[:, par, 0:nh].unsqueeze(2).to_broadcast([P, nh, nk]),
                                      ALU.subtract).then_inc(sub_sb, 1)

                def context(p, par):
                    par = p % 2 if par is None else par
                    dve.wait_ge(pv_ps, NPAIR * a + p + 1)
                    dve.reciprocal(rcT[:, :], PS[:, 6, 256 + P * par:256 + P * par + P]).then_inc(rc_sb, 1)
                    dve.wait_ge(rc_sb, NPAIR * a + p + 1)
                    wait(dve, o_ps, NPAIR * a + p - 1)
                    dve.tensor_tensor(cT[:, par, :], PS[:, 6, P * par:P * par + P], rcT[:, :], ALU.mult).then_inc(ct_sb, 1)

                def add(p, par):
                    par = p % 2 if par is None else par
                    dve.wait_ge(o_ps, NPAIR * a + p + 1)
                    o = PS[:, 7, P * par:P * par + P]
                    if k == L2F:
                        dve.tensor_tensor(Zr[:, p, 32:D], Zr[:, p, 32:D], o[:, 32:D], ALU.add).then_inc(x_ready, 1)
                    else:
                        dve.tensor_tensor(X[:, p, :], X[:, p, :], o, ALU.add).then_inc(x_ready, 1)

                pipelined(dve, [(-1, spread), (2, context), (3, add), (0, shift)])

            def group_work(k, g):
                src = Zr if k == L2M else X
                v = norm_no(k, g)

                t0 = before(TURNS, k)

                def y_free():
                    if k == L2F:
                        wait(dve, z_copied, g)
                    else:
                        wait(dve, t_ps, t0 + TURNS[k] * g)
                    if k == L1F:
                        wait(dve, e_ps, g)

                normalise(v, lambda j: src[:, PPG * g + j, :], lambda j: y[:, j, :], mean=k != L2M, free=y_free)
                if k == L2F:
                    normalise(norm_no(k, g, 1), lambda j: y[:, j, :], lambda j: yy[:, j, :], mean=False,
                              free=lambda: wait(dve, t_ps, t0 + g))
                if k == L3A:
                    normalise(norm_no(k, g, 1), lambda j: y[:, j, :], lambda j: yy[:, j, :],
                              free=lambda: wait(dve, t_ps, t0 + 2 * g))
                    dve.wait_ge(dma_ctx, 16)
                    normalise(norm_no(k, g, 2), lambda j: CTX[:, PPG * g + j, :], lambda j: y[:, j, :])
                if k in TOK:
                    a = ATT[k]
                    dve.wait_ge(kv_ps, NG * a + g + 1)
                    dve.tensor_copy(V[:, :, :].rearrange("p (g b) d -> p g (b d)", b=BPG)[:, g],
                                    PSf[:, 1024:2048]).then_inc(v_sb, 1)
                if k == L2F:
                    dve.wait_ge(kv_ps, NG * 3 + g + 1)
                    dve.tensor_copy(V[:, :, :].rearrange("p (g b) d -> p g (b d)", b=BPG)[:, g],
                                    PSf[:, 1024:2048]).then_inc(v_sb, 1)
                    dve.wait_ge(sq_sb, g + 1)
                    dve.tensor_reduce(ss[:, 0:128], sq[:, 0:1024].rearrange("p (n d) -> p n d", d=8),
                                      AX, ALU.add).then_inc(sums_sb, 1)
                    head_factors(g, 128, 8, RMS_EPS, ALU.add)
                    wait(dve, qk_turned, g)
                    dve.tensor_tensor(qkn[:, 0:1024].rearrange("p (n d) -> p n d", d=8),
                                      PSf[:, 0:1024].rearrange("p (n d) -> p n d", d=8),
                                      rs[:, 0:128].unsqueeze(2).to_broadcast([P, 128, 8]), ALU.mult).then_inc(qkn_sb, 1)
                if k == L3A:
                    dve.wait_ge(sq_sb, NG + g + 1)
                    dve.tensor_reduce(ss[:, 0:24], sq[:, :].rearrange("p (n d) -> p n d", d=64),
                                      AX, ALU.add).then_inc(sums_sb, 1)
                    head_factors(NG + g, 24, 64, RMS3_EPS ** 2, ALU.max)
                    dve.wait_ge(v_sb, NG * 4 + g + 1)
                    dve.wait_ge(qk_turned, NG + g)
                    for h in range(2):
                        dve.tensor_tensor(qkn[:, 0:1024].rearrange("p (b h d) -> p b h d", h=2, d=64)[:, :, h],
                                          PSf[:, 0:2048].rearrange("p (b c) -> p b c", c=256)[:, :, 64 * h:64 * h + 64],
                                          rs[:, h:16:2].unsqueeze(2).to_broadcast([P, BPG, 64]), ALU.mult)
                    dve.tensor_tensor(qkn[:, 1024:1536].rearrange("p (n d) -> p n d", d=64),
                                      PS[:, 4, :].rearrange("p (n d) -> p n d", d=64),
                                      rs[:, 16:24].unsqueeze(2).to_broadcast([P, 8, 64]), ALU.mult).then_inc(qkn_sb, 1)
                if k == L0F:
                    add_group(k, g, g + 1)
                if k == L1F:
                    dve.wait_ge(t_sb, turned(k, g))
                    wait(dve, g_ps, g)
                    yb = yT[:, :].rearrange("p (b s) -> p b s", s=S)
                    dve.tensor_copy(oddT[:, 0, :, :], yb[:, :, 2:10:2])
                    dve.tensor_copy(oddT[:, 1, :, :], yb[:, :, 10:18:2]).then_inc(odd_sb, 1)
                    dve.wait_ge(e_ps, g + 1)
                    dve.tensor_tensor(Er[:, :, :], PS[0:32, 5, 0:P].unsqueeze(1).to_broadcast([32, 4, P]),
                                      dR[0:32, :].unsqueeze(2).to_broadcast([32, 4, P]), ALU.mult)
                    for c in range(4):
                        r0 = slice(32 * c, 32 * c + 32)
                        ins = dve.tensor_tensor(
                            E2[r0, :, :],
                            PS[r0, 5, P:2 * P].rearrange("p (i c) -> p i c", c=4)[:, :, c].unsqueeze(1).to_broadcast([32, 4, 32]),
                            dR[r0, :].unsqueeze(2).to_broadcast([32, 4, 32]), ALU.mult)
                    ins.then_inc(e_sb, 1)
                    dve.wait_ge(xo_ps, g + 1)
                    dve.tensor_tensor(XO[:, :, :], PS[0:32, 6, :].rearrange("p (b s) -> p b s", s=S),
                                      dB[0:32, :].unsqueeze(2).to_broadcast([32, BPG, S]), ALU.mult).then_inc(xo_sb, 1)
                    dve.wait_ge(g_ps, g + 1)
                    dve.tensor_tensor(GM[:, :, :], PS[:, 6, :].rearrange("p (b s) -> p b s", s=S),
                                      dB[:, :].unsqueeze(2).to_broadcast([P, BPG, S]), ALU.mult).then_inc(g_sb, 1)
                    add_group(k, g, NG + g + 1)
                if k == L2M:
                    dve.wait_ge(lg_ps, g + 1)
                    q = 7 * g
                    lps = PS[:, 6, 0:16].rearrange("p (j e) -> p j e", e=4)
                    dve.tensor_copy(lg[:, :, :], lps)
                    dve.memset(lgz[:, :, :], 0.0).then_inc(gate_v, 1)
                    dve.wait_ge(gate_v, q + 1)
                    dve.tensor_tensor(fin[:, :, :], lg[:, :, :], lg[:, :, :], ALU.is_equal).then_inc(gate_v, 1)
                    dve.wait_ge(gate_v, q + 2)
                    dve.memset(spare[:, 1:2], 0.0)
                    dve.copy_predicated(lgz[:, :, :], fin[:, :, :], lg[:, :, :]).then_inc(gate_v, 1)
                    dve.wait_ge(gate_v, q + 3)
                    dve.tensor_scalar(lgz[:, :, :], lgz[:, :, :], -FLT_MAX, FLT_MAX, ALU.max, ALU.min)\
                        .then_inc(n_gate, 1)
                    dve.wait_ge(n_gate, 6 * g + 1)
                    dve.tensor_reduce(gmx[:, :], lgz[:, :, :], AX, ALU.max).then_inc(gate_v, 1)
                    dve.wait_ge(gate_v, q + 4)
                    dve.tensor_tensor(lgz[:, :, :], lgz[:, :, :], gmx[:, :].unsqueeze(2).to_broadcast([P, PPG, 4]),
                                      ALU.subtract).then_inc(gate_v, 1)
                    dve.wait_ge(gate_e, g + 1)
                    dve.tensor_reduce(gs[:, :], lgz[:, :, :], AX, ALU.add).then_inc(n_gate, 1)
                    dve.wait_ge(n_gate, 6 * g + 2)
                    dve.reciprocal(gs[:, :], gs[:, :]).then_inc(n_gate, 1)
                    dve.wait_ge(n_gate, 6 * g + 3)
                    dve.tensor_tensor(lgz[:, :, :], lgz[:, :, :], gs[:, :].unsqueeze(2).to_broadcast([P, PPG, 4]),
                                      ALU.mult).then_inc(n_gate, 1)
                    dve.wait_ge(n_gate, 6 * g + 4)
                    pe_ = lgz[:, :, :].unsqueeze(3).to_broadcast([P, PPG, 4, 4])
                    pj = lgz[:, :, :].unsqueeze(2).to_broadcast([P, PPG, 4, 4])
                    dve.tensor_tensor(cmp[:, :, :, :], pj, pe_, ALU.is_gt)
                    dve.tensor_tensor(tie[:, :, :, :], pj, pe_, ALU.is_equal).then_inc(n_gate, 1)
                    dve.wait_ge(n_gate, 6 * g + 5)
                    dve.tensor_tensor(tie[:, :, :, :], tie[:, :, :, :],
                                      low4[:, :, :].unsqueeze(1).to_broadcast([P, PPG, 4, 4]), ALU.mult).then_inc(n_gate, 1)
                    dve.wait_ge(n_gate, 6 * g + 6)
                    dve.tensor_tensor(cmp[:, :, :, :], cmp[:, :, :, :], tie[:, :, :, :], ALU.add).then_inc(gate_v, 1)
                    dve.wait_ge(gate_v, q + 6)
                    dve.tensor_reduce(rank[:, :, :], cmp[:, :, :, :], AX, ALU.add).then_inc(gate_v, 1)
                    dve.wait_ge(gate_v, q + 7)
                    dve.scalar_tensor_tensor(rank[:, :, :], rank[:, :, :], 2.0, lgz[:, :, :], ALU.is_lt, ALU.mult)\
                        .then_inc(wt_sb, 1)
                    dve.wait_ge(wt_sb, 4 * g + 1)
                    dve.tensor_reduce(gs[:, :], rank[:, :, :], AX, ALU.add).then_inc(wt_sb, 1)
                    dve.wait_ge(wt_sb, 4 * g + 2)
                    dve.tensor_scalar(gs[:, :], gs[:, :], 1e-8, None, ALU.add).then_inc(wt_sb, 1)
                    dve.wait_ge(wt_sb, 4 * g + 3)
                    dve.reciprocal(gmx[:, :], gs[:, :]).then_inc(wt_sb, 1)
                    dve.wait_ge(wt_sb, 4 * g + 4)
                    dve.tensor_tensor(rank[:, :, :], rank[:, :, :], gmx[:, :].unsqueeze(2).to_broadcast([P, PPG, 4]),
                                      ALU.mult).then_inc(w_done, 1)
                    for n, (name, c, dst) in enumerate(MOE_CHUNKS):
                        if name == "e1_w2":
                            dve.wait_ge(h_ps, H_PS[L2M] + NCH * g + n + 1)
                            dve.wait_ge(h_sb, H_SB[L2M] + NACT * g + acts_through(n))
                            dve.tensor_tensor(Hs[:, 4 + c, :], Hs[:, 4 + c, :], PS[:, n % 4, :], ALU.mult).then_inc(h_mul, 1)
                    dve.wait_ge(w_done, g + 1)
                    for n, (_, e, _, _, _) in enumerate(MOE_OUTS):
                        dve.wait_ge(oe_ps, 4 * g + n + 1)
                        for j in range(PPG):
                            o = PS[:, 4 + n % 2, P * j:P * j + P]
                            if n == 0:
                                ins = dve.tensor_scalar(moe[:, j, :], o, rank[:, j, e:e + 1], None, ALU.mult)
                            else:
                                ins = dve.scalar_tensor_tensor(moe[:, j, :], o, rank[:, j, e:e + 1], moe[:, j, :],
                                                               ALU.mult, ALU.add)
                        ins.then_inc(moe_sb, 1)
                        dve.wait_ge(moe_sb, 4 * g + n + 1)
                    dve.tensor_tensor(group(X, g), group(X, g), group(Zr, g), ALU.add).then_inc(x_part, 1)
                    dve.wait_ge(x_part, g + 1)
                    dve.tensor_tensor(group(X, g)[:, :, 32:D], group(X, g)[:, :, 32:D], moe[:, :, 32:D],
                                      ALU.add).then_inc(x_ready, 1)
                if k == L3F:
                    dve.wait_ge(xh_sb, g + 1)
                    dve.tensor_tensor(XL[:, g, :], PS[:, 7, :], XH[:, g, :].bitcast(F32), ALU.subtract).then_inc(t_sb, 1)

            def experts_work():
                def low(j, par):
                    dve.wait_ge(eh_sb, 2 * j + par + 1)
                    dve.tensor_tensor(EL[:, par, :], EW[:, par, :], EH[:, par, :].bitcast(F32), ALU.subtract).then_inc(el_sb, 1)

                def chunk(j, par, first, last):
                    for g in range(NG):
                        u = NG * (2 * j + par) + g
                        dve.wait_ge(sg_sb, u + 1)
                        dve.wait_ge(gu_ps, 2 * u + 2)
                        dve.tensor_tensor(Hf[:, g % 2, :], sG[:, g % 2, :], PS[:, 2 + g % 2, :], ALU.mult).then_inc(hf_sb, 1)
                        dve.wait_ge(hh_sb, u + 1)
                        dve.tensor_tensor(HL[:, g, :], Hf[:, g % 2, :], HH[:, g, :].bitcast(F32), ALU.subtract).then_inc(hl_sb, 1)
                        if g == 2 and not first and not last:
                            low(j + par, 1 - par)

                for par in range(2):
                    low(0, par)
                chunked(dve, chunk)
                for g in range(NG):
                    dve.wait_ge(ot_ps, 2 * NG + g + 1)
                    dve.tensor_tensor(group(X, g), group(X, g), PS[:, g, :].rearrange("p (j d) -> p j d", j=PPG),
                                      ALU.add).then_inc(x_ready, 1)

            for k in range(9):
                if k > 0:
                    dve.wait_ge(x_ready, x_after(k - 1))
                groups(dve, lambda g, k=k: group_work(k, g))
                if k in ATT:
                    dve.wait_ge(k_sb, NG * (ATT[k] + 1))
                    if k == L2F:
                        dve.wait_ge(z_copied, NG)
                    pairs(k)
            experts_work()

        @block.tensor
        def _(pe):
            pe.wait_ge(dma_small, SMALL)
            for n in range(4):
                ins = pe.matmul(PS[:, 0, P * n:P * n + P], LA[:, n, :], LB[:, n, :], start=True, stop=True)
            ins.then_inc(lora_ps, 1)
            pe.wait_ge(consts_v, 1)
            pe.matmul(PS[0:1, 6, 0:D], col("c_bv"), W1m[:, 3, :], start=True, stop=True).then_inc(lora_ps, 1)

            def norm_no(k, g, t=0):
                return before(NORMS, k) + NORMS[k] * g + t + 1

            def turn(k, g, src, v, t=0):
                pe.wait_ge(n_done, v)
                wait(pe, t_sb, before(TURNS, k) + TURNS[k] * g + t)
                for j in range(PPG):
                    ins = pe.transpose(PS[:, 7, P * j:P * j + P], src[:, j, :], ident[:, :])
                ins.then_inc(t_ps, 1)

            def turn_back(u):
                pe.wait_ge(o_sb, u)
                for j in range(PPG):
                    ins = pe.transpose(PS[:, 5, P * j:P * j + P], oT[:, P * j:P * j + P], ident[:, :])
                ins.then_inc(ot_ps, 1)

            def project(k, g):
                a = ATT[k]
                if k == L0A:
                    wq, wk, wv = w("L0_WQ"), w("L0_WK"), w("L0_WV")
                elif k == L1A:
                    wq, wk, wv = (W1m[:, n, :] for n in range(3))
                else:
                    wq, wk, wv = (BD[:, n, :, :].rearrange("p a b -> p (a b)") for n in range(3))
                pe.wait_ge(dma_ctx2, 16 * (NG * a + g + 1))
                pe.wait_ge(k_sb, NG * a + g)
                pe.wait_ge(v_sb, NG * a + g)
                pe.matmul(PS[:, 1, :], wk, ctx2[:, :, 0, :], start=True, stop=True)
                for b in range(BPG):
                    ins = pe.matmul(PSf[:, 1024 + P * b:1024 + P * b + P], ctx2[:, b, :, :].rearrange("p a s -> p (a s)"),
                                    wv, start=True, stop=True)
                ins.then_inc(kv_ps, 1)
                turn(k, g, y, norm_no(k, g))
                pe.wait_ge(t_sb, before(TURNS, k) + g + 1)
                pe.wait_ge(q_sb, NG * a + g)
                pe.matmul(PS[:, 0, :], wq, yT[:, :], start=True, stop=True).then_inc(q_ps, 1)

            def pairs(k):
                a = ATT[k]
                L3 = k == L3A
                wo = {L0A: w("L0_WO"), L1A: W1m[:, 3, :], L2A: w("L2_WoT"), L2F: w("woT"), L3A: w("L3_Wout")}[k]
                bias = {L1A: 0, L2A: 1, L3A: 2}.get(k)

                def scores(p, par):
                    par = p % 2 if par is None else par
                    pe.wait_ge(kx_v, NPAIR * a + p + 1)
                    pe.wait_ge(kx_p, NPAIR * a + p + 1)
                    pe.wait_ge(qs_sb, NPAIR * a + p + 1)
                    wait(pe, sub_sb, NPAIR * a + p - 1)
                    added = k != L1A
                    if k == L0A:
                        pe.wait_ge(kd_sb, p + 1)
                    for half in range(1 if L3 else 2):
                        n = 256 if L3 else 512
                        for b in range(2):
                            ins = pe.matmul(PS[64 * b:64 * b + 64, 2 * par + half, 0:n], Qs[:, par, 64 * b:64 * b + 64],
                                            Kx[:, par, b, n * half:n * half + n], start=True, stop=not added,
                                            tile_position=(0, 64 * b), skip_group_check=True)
                        dst = PS[:, 2 * par + half, 0:n]
                        if k in (L0A, L2F):
                            ins = pe.matmul(dst, kd[:, par, :] if k == L0A else identb[:, :],
                                            causal[:, :].unsqueeze(1).to_broadcast([P, 8, S]), start=False, stop=True,
                                            skip_group_check=True)
                        if k == L2A:
                            ins = pe.matmul(dst, identb[:, :], mqk[:, p, :].unsqueeze(1).to_broadcast([P, 8, S]),
                                            start=False, stop=True, skip_group_check=True)
                        if L3:
                            ins = pe.matmul(dst.rearrange("p (h k) -> p h k", h=2)[:, :, 0:S], sel2[:, :],
                                            mk[:, p, :].unsqueeze(1).to_broadcast([2, 2, S]),
                                            start=False, stop=True, skip_group_check=True)
                    ins.then_inc(sc_ps, 1)

                def probs(p, par):
                    par = p % 2 if par is None else par
                    n = 1 if L3 else 4
                    pe.wait_ge(exp_sb, NPAIR * a + p + 1)
                    for half in range(2):
                        wait(pe, pt_sb, 2 * (NPAIR * a + p - 1) + half + 1)
                        for i in range(n):
                            c = n * half + i
                            ins = pe.transpose(PS[:, 4 + half, P * i:P * i + P], PR[:, par, P * c:P * c + P], ident[:, :])
                        ins.then_inc(pt_ps, 1)

                def values(p, par):
                    par = p % 2 if par is None else par
                    pe.wait_ge(vz_sb, NPAIR * a + p + 1)
                    pe.wait_ge(pt_sb, 2 * (NPAIR * a + p + 1))
                    wait(pe, ct_sb, NPAIR * a + p)
                    for b in range(2):
                        dst = slice(P * par + 64 * b, P * par + 64 * b + 64)
                        if L3:
                            for h in range(2):
                                ins = pe.matmul(PS[64 * h:64 * h + 64, 6, dst], Vz[:, par, b, 64 * h:64 * h + 64],
                                                PT[:, par, h, 64 * b:64 * b + 64], start=True, stop=True,
                                                tile_position=(0, 64 * h))
                        else:
                            for t in range(2):
                                for j in range(4):
                                    n = 2 * j + t
                                    ins = pe.matmul(PS[32 * j:32 * j + 32, 6, dst],
                                                    Vz[:, par, b, 48 * n - 16 * t:48 * n - 16 * t + 32],
                                                    PT[:, par, n, 64 * b:64 * b + 64], start=t == 0, stop=t == 1,
                                                    tile_position=(0, 32 * j), skip_group_check=True)
                    dst = slice(256 + P * par, 256 + P * par + P)
                    if L3:
                        for h in range(2):
                            ins = pe.matmul(PS[64 * h:64 * h + 64, 6, dst], ones[:, 0:64], PT[:, par, h, :], start=True,
                                            stop=True, tile_position=(0, 64 * h))
                    else:
                        for t in range(2):
                            for j in range(4):
                                n = 2 * j + t
                                ins = pe.matmul(PS[32 * j:32 * j + 32, 6, dst], Oz[:, 48 * n - 16 * t:48 * n - 16 * t + 32],
                                                PT[:, par, n, :], start=t == 0, stop=t == 1,
                                                tile_position=(0, 32 * j), skip_group_check=True)
                    ins.then_inc(pv_ps, 1)

                def output(p, par):
                    par = p % 2 if par is None else par
                    pe.wait_ge(ct_sb, NPAIR * a + p + 1)
                    wait(pe, x_ready, x_after(k) - NPAIR + p)
                    dst = PS[:, 7, P * par:P * par + P]
                    ins = pe.matmul(dst, cT[:, par, :], wo, start=True, stop=bias is None)
                    if bias is not None:
                        ins = pe.matmul(dst, ones[0:1, :], ROWS[:, D * bias:D * bias + D], start=False, stop=True)
                    ins.then_inc(o_ps, 1)

                if k == L0A:
                    pe.wait_ge(row_sb, 1)
                pipelined(pe, [(0, scores), (1, probs), (2, output), (1, values)])

            def group_work(k, g):
                t0 = before(TURNS, k)
                if k in TOK:
                    project(k, g)
                elif k == L2F:
                    turn(k, g, yy, norm_no(k, g, 1))
                    pe.wait_ge(t_sb, t0 + g + 1)
                    wait(pe, qkn_sb, g)
                    for j in range(PPG):
                        ins = pe.matmul(PSf[:, 256 * j:256 * j + 256], yT[:, P * j:P * j + P], w("wqkT"), start=True, stop=True)
                    ins.then_inc(q_ps, 1)
                    wait(pe, v_sb, NG * 3 + g)
                    for b in range(BPG):
                        ins = pe.matmul(PSf[:, 1024 + P * b:1024 + P * b + P], yT2[:, b, :, :].rearrange("p a s -> p (a s)"),
                                        w("wvT"), start=True, stop=True)
                    ins.then_inc(kv_ps, 1)
                    pe.wait_ge(qkn_sb, g + 1)
                    wait(pe, k_sb, NG * 3 + g)
                    for j in range(PPG):
                        for i in range(2):
                            ins = pe.transpose(PS[:, 5 + i, P * j:P * j + P], qkn[:, 256 * j + P * i:256 * j + P * i + P], ident[:, :])
                    ins.then_inc(qk_turned, 1)
                elif k == L3A:
                    wait(pe, q_sb, NG * 4 + g)
                    turn(k, g, yy, norm_no(k, g, 1))
                    turn(k, g, y, norm_no(k, g, 2), 1)
                    pe.wait_ge(t_sb, t0 + 2 * g + 2)
                    wait(pe, qkn_sb, NG + g)
                    wait(pe, v_sb, NG * 4 + g)
                    for b in range(BPG):
                        ins = pe.matmul(PSf[:, 256 * b:256 * b + 256], CL[:, b, :, :].rearrange("p a s -> p (a s)"),
                                        w("L3_Wkv"), start=True, stop=True)
                    for j in range(PPG):
                        ins = pe.matmul(PS[:, 4, P * j:P * j + P], yT[:, P * j:P * j + P], w("L3_Wq"), start=True, stop=True)
                    ins.then_inc(q_ps, 1)
                    pe.wait_ge(qkn_sb, NG + g + 1)
                    wait(pe, k_sb, NG * 4 + g)
                    for b in range(BPG):
                        pe.transpose(PSf[:, 2560 + P * b:2560 + P * b + P], qkn[:, P * b:P * b + P], ident[:, :])
                    for j in range(PPG):
                        ins = pe.transpose(PS[:, 7, P * j:P * j + P], qkn[:, 1024 + P * j:1024 + P * j + P], ident[:, :])
                    ins.then_inc(qk_turned, 1)
                elif k == L0F:
                    turn(k, g, y, norm_no(k, g))
                    pe.wait_ge(t_sb, t0 + g + 1)
                    pe.matmul(PS[0:32, 0, :], w("U1"), yT[:, :], start=True, stop=True).then_inc(h_ps, 1)
                    u = 6 * g
                    pe.wait_ge(h_sb, u + 1)
                    for c in range(4):
                        pe.matmul(PS[:, (1 + c) % 4, :], w("V1", c, rows_=32), Hs[0:32, 0, :], start=True, stop=True).then_inc(h_ps, 1)
                    for c in range(4):
                        pe.wait_ge(h_sb, u + 2 + c)
                        ins = pe.matmul(PS[0:32, 5, :], w("U2", c, 32), Hs[:, 1 + c, :], start=c == 0, stop=c == 3)
                    ins.then_inc(h_ps, 1)
                    pe.wait_ge(h_sb, u + 6)
                    pe.matmul(PS[:, 4, :], w("V2", rows_=32), Hs[0:32, 5, :], start=True, stop=True).then_inc(acc_ps, 1)
                    turn_back(g + 1)
                    pe.wait_ge(x_ready, x_after(k - 1) + g + 1)
                elif k == L1F:
                    turn(k, g, y, norm_no(k, g))
                    for j in range(PPG):
                        pe.matmul(PS[0:32, 5, 0:P], Sel1[:, j, :, :].rearrange("p b r -> p (b r)"), y[:, j, :], start=j == 0, stop=j == 3)
                    for j in range(PPG):
                        ins = pe.matmul(PS[:, 5, P:2 * P], Sel2[:, j, :, :].rearrange("p c r -> p (c r)"), y[:, j, :], start=j == 0, stop=j == 3)
                    ins.then_inc(e_ps, 1)
                    pe.wait_ge(odd_sb, g + 1)
                    pe.matmul(PS[0:32, 6, :], oddT[:, 0, :, :].rearrange("p b r -> p (b r)"), yT[:, :], start=True, stop=True).then_inc(xo_ps, 1)
                    for c in range(4):
                        pe.matmul(PS[:, c, :], w("W1T", c), yT[:, :], start=True, stop=False)
                    pe.wait_ge(e_sb, g + 1)
                    pe.wait_ge(xo_sb, g + 1)
                    for c in range(4):
                        pe.matmul(PS[:, c, :], Er[:, c, :], XO[:, :, :].rearrange("p b s -> p (b s)"), start=False, stop=True).then_inc(h_ps, 1)
                    u = H_SB[L1F] + 4 * g
                    for c in range(4):
                        pe.wait_ge(h_sb, u + 1 + c)
                        ins = pe.matmul(PS[32 * c:32 * c + 32, 6, :], oddT[:, 1, :, :].rearrange("p b r -> p (b r)"), Hs[:, c, :],
                                        start=True, stop=True, tile_position=(0, 32 * c))
                    ins.then_inc(g_ps, 1)
                    for c in range(4):
                        pe.matmul(PS[:, 4, :], w("W2T", c), Hs[:, c, :], start=c == 0, stop=False)
                    pe.wait_ge(g_sb, g + 1)
                    pe.matmul(PS[:, 4, :], E2[:, :, :].rearrange("p r i -> p (r i)"), GM[:, :, :].rearrange("p b s -> p (b s)"),
                              start=False, stop=True).then_inc(acc_ps, 1)
                    turn_back(NG + g + 1)
                    pe.wait_ge(x_ready, x_after(k - 1) + g + 1)
                elif k == L2M:
                    turn(k, g, y, norm_no(k, g))
                    pe.wait_ge(t_sb, t0 + g + 1)
                    pe.wait_ge(x_ready, x_after(k - 1) + g)
                    for j in range(PPG):
                        ins = pe.matmul(PS[:, 6, 4 * j:4 * j + 4], yT[:, P * j:P * j + P], w("gateT"), start=True, stop=True)
                    ins.then_inc(lg_ps, 1)
                    for n, (name, c, _) in enumerate(MOE_CHUNKS):
                        if n >= 4:
                            if MOE_CHUNKS[n - 4][2] is None:
                                pe.wait_ge(h_mul, H_MUL[L2M] + 2 * g + 1 + MOE_CHUNKS[n - 4][1])
                            else:
                                pe.wait_ge(h_sb, H_SB[L2M] + NACT * g + acts_through(n - 4))
                        if name in MOE_IN:
                            ins_, last = MOE_IN[name]
                            pe.wait_ge(h_sb, H_SB[L2M] + NACT * g + acts_through(last))
                            for i, hsrc in enumerate(ins_):
                                ins = pe.matmul(PS[:, n % 4, :], w(name, 2 * i + c), Hs[:, hsrc, :], start=i == 0,
                                                stop=i == len(ins_) - 1)
                        else:
                            ins = pe.matmul(PS[:, n % 4, :], w(name, c), yT[:, :], start=True, stop=True)
                        ins.then_inc(h_ps, 1)
                        for m, (after, e, wname, hs, last) in enumerate(MOE_OUTS):
                            if after != n:
                                continue
                            if m >= 2:
                                pe.wait_ge(moe_sb, 4 * g + m - 1)
                            if e == 1:
                                pe.wait_ge(h_mul, H_MUL[L2M] + 2 * g + 2)
                            pe.wait_ge(h_sb, H_SB[L2M] + NACT * g + acts_through(last))
                            for j in range(PPG):
                                for i in range(2):
                                    ins = pe.matmul(PS[:, 4 + m % 2, P * j:P * j + P], Hs[:, hs[i], P * j:P * j + P],
                                                    w(wname, i), start=i == 0, stop=i == 1)
                            ins.then_inc(oe_ps, 1)
                else:
                    turn(k, g, y, norm_no(k, g))

            def experts_work():
                def product(dst, n, par, hi, lo, start, stop):
                    wh, wl = EH[:, par, P * n:P * n + P], EL[:, par, P * n:P * n + P]
                    pe.matmul(dst, wh, hi, start=start, stop=False)
                    pe.matmul(dst, wh, lo, start=False, stop=False)
                    return pe.matmul(dst, wl, hi, start=False, stop=stop)

                def downs(v, par, g, start, stop):
                    pe.wait_ge(hl_sb, v + 1)
                    product(PS[:, 4 + g, :], 2, par, HH[:, g, :], HL[:, g, :], start, stop).then_inc(d_ps, 1)

                def chunk(j, par, first, last):
                    pe.wait_ge(el_sb, 2 * j + par + 1)
                    for g in range(NG):
                        u = NG * (2 * j + par) + g
                        if g >= 2 or not first:
                            pe.wait_ge(hf_sb, u - 1)
                        product(PS[:, g % 2, :], 0, par, XH[:, g, :], XL[:, g, :], True, True).then_inc(gu_ps, 1)
                        product(PS[:, 2 + g % 2, :], 1, par, XH[:, g, :], XL[:, g, :], True, True).then_inc(gu_ps, 1)
                        if g >= LAG3:
                            downs(u - LAG3, par, g - LAG3, first, last)
                        elif not first:
                            downs(u - LAG3, 1 - par, g + NG - LAG3, isinstance(j, int) and 2 * j + par == 1, False)

                pe.wait_ge(t_sb, before(TURNS, L3F) + NG)
                chunked(pe, chunk)
                for g in range(NG - LAG3, NG):
                    downs(NG * (NCH3 - 1) + g, 1, g, False, True)
                pe.wait_ge(hf_sb, NG * NCH3)
                for g in range(NG):
                    pe.wait_ge(o_sb, 2 * NG + g + 1)
                    for i in range(PPG):
                        ins = pe.transpose(PS[:, g, P * i:P * i + P], oT3[:, g, P * i:P * i + P], ident[:, :])
                    ins.then_inc(ot_ps, 1)

            for k in range(9):
                if k > 0:
                    pe.wait_ge(x_ready, x_after(k - 1))
                groups(pe, lambda g, k=k: group_work(k, g))
                if k in ATT:
                    pairs(k)
            experts_work()


def kernel(**inputs):
    import numpy as np
    import concourse.bacc as bacc
    from concourse import mybir as mb
    from concourse.bass_utils import run_bass_kernel_spmd

    a = {k: np.asarray(v) for k, v in inputs.items()}
    f = np.float32

    def chunks(m):
        return m.reshape(-1, 128, m.shape[1]).transpose(1, 0, 2).reshape(128, -1)

    def low(m):
        return np.concatenate([m, np.zeros((128 - m.shape[0], m.shape[1]), f)])

    def col(v):
        return v.reshape(-1, 128).T

    cols = {
        "L0_WQ": a["L0_xattn_WQ"], "L0_WK": a["L0_xattn_WK"], "L0_WV": a["L0_xattn_WV"], "L0_WO": a["L0_xattn_WO"],
        "U1": a["L0_ffn_U1"], "V1": low(a["L0_ffn_V1"]), "U2": chunks(a["L0_ffn_U2"]), "V2": low(a["L0_ffn_V2"]),
        "L1_Wq": a["L1_xattn_Wq"], "L1_Wk": a["L1_xattn_Wk"], "L1_Wv": a["L1_xattn_Wv"], "L1_Wo": a["L1_xattn_Wo"],
        "W1T": a["L1_ffn_W1"].T, "W2T": chunks(a["L1_ffn_W2"].T),
        "L2_q": np.tile(a["L2_xattn_Wq"].T, (16, 1)), "L2_k": np.tile(a["L2_xattn_Wk"].T, (16, 1)),
        "L2_v": np.tile(a["L2_xattn_Wv"].T, (16, 1)), "L2_WoT": a["L2_xattn_Wo"].T,
        "wqkT": np.concatenate([a["L2_ffn_wq"].T, a["L2_ffn_wk"].T], 1), "wvT": a["L2_ffn_wv"].T,
        "woT": a["L2_ffn_wo"].T, "gateT": a["L2_ffn_gate_w"].T,
        "e0_up": a["L2_ffn_e0_up"].T, "e0_down": chunks(a["L2_ffn_e0_down"].T),
        "e1_w1": a["L2_ffn_e1_w1"].T, "e1_w2": a["L2_ffn_e1_w2"].T, "e1_down": chunks(a["L2_ffn_e1_down"].T),
        "e2_l1": a["L2_ffn_e2_l1"].T, "e2_l2": chunks(a["L2_ffn_e2_l2"].T), "e2_l3": chunks(a["L2_ffn_e2_l3"].T),
        "e2_l4": chunks(a["L2_ffn_e2_l4"].T),
        "e3_down": a["L2_ffn_e3_down"].T, "e3_up": a["L2_ffn_e3_up"].T, "e3_out": chunks(a["L2_ffn_e3_out"].T),
        "L3_Wq": a["L3_xattn_W_q"], "L3_Wkv": a["L3_xattn_W_kv"], "L3_Wout": a["L3_xattn_W_out"],
        "c_L0b1": col(a["L0_ffn_b1"]), "c_L0b2": col(a["L0_ffn_b2"]),
        "c_bq": col(a["L1_xattn_bq"]), "c_bk": col(a["L1_xattn_bk"]), "c_bv": col(a["L1_xattn_bv"]),
        "c_L1b1": col(a["L1_ffn_b1"]), "c_L1b2": col(a["L1_ffn_b2"]),
        "c_n1": col(a["L2_ffn_n1_w"]), "c_n2": col(a["L2_ffn_n2_w"]),
        "c_qn": col(np.tile(a["L2_ffn_qn_w"], 16)), "c_kn": col(np.tile(a["L2_ffn_kn_w"], 16)),
        "c_lxg": col(a["L3_xattn_ln_x_g"]), "c_lxb": col(a["L3_xattn_ln_x_b"]),
        "c_llg": col(a["L3_xattn_ln_l_g"]), "c_llb": col(a["L3_xattn_ln_l_b"]),
        "c_qg": col(np.tile(a["L3_xattn_q_gamma"], 2)), "c_kg": col(np.tile(a["L3_xattn_k_gamma"], 2)),
        "c_scale": np.tile(a["L1_ffn_scale"].reshape(1, 1), (128, 1)),
    }
    ctx = a["ctx_1024"]
    bools = np.zeros((B, S, 4), np.uint8)
    bools[:, :, 0] = a["mask_BxS2_bk0"].view(np.uint8)
    ctx_T = ctx.transpose(2, 0, 1).reshape(128, NG, BPG, 1, S)
    arrays = {
        "x": a["x"].reshape(NPAIR, P, D).transpose(1, 0, 2),
        "ctx_tok": ctx.reshape(NPAIR, P, D).transpose(1, 0, 2),
        "ctx_T2": np.concatenate([ctx_T, ctx_T], 3),
        "mask_q": a["mask_BxS2_ik0"].reshape(NPAIR, P).T,
        "mask_qk": a["mask_Bx1xSxS2_if1"].reshape(NPAIR, P, S).transpose(1, 0, 2),
        "mask_key": bools.view(np.int32).reshape(NPAIR, 2, S).transpose(1, 0, 2),
        "pack": np.concatenate([cols[n] for n, _ in PACK], 1),
        "rows": np.concatenate([a["L1_xattn_bo"], a["L2_xattn_bo"], a["L3_xattn_b_out"]]).reshape(1, 384),
        "lora_A": np.stack([a["L1_xattn_A" + n].T for n in "qkvo"], 1),
        "lora_B": np.stack([a["L1_xattn_B" + n] for n in "qkvo"], 1),
        "experts": np.stack([a["L3_ffn_Wg"].reshape(8, P, 4, P).transpose(1, 0, 2, 3).reshape(P, NCH3, P),
                             a["L3_ffn_Wu"].reshape(8, P, 4, P).transpose(1, 0, 2, 3).reshape(P, NCH3, P),
                             a["L3_ffn_Wd"].reshape(NCH3, P, P).transpose(1, 0, 2)], 2).reshape(P, NCH3, 3 * P),
    }
    nc = bacc.Bacc("TRN2", target_bir_lowering=False, num_devices=1)
    feed, args = {}, {}
    for name, v in arrays.items():
        v = np.ascontiguousarray(v)
        feed[name + "_dram"] = v
        args[name] = nc.dram_tensor(name + "_dram", v.shape, mb.dt.from_np(v.dtype), kind="ExternalInput").ap()
    args["out"] = nc.dram_tensor("out_dram", (P, NPAIR, D), mb.dt.from_np(np.dtype("float32")), kind="ExternalOutput").ap()
    build_program(nc, **args)
    r = run_bass_kernel_spmd(nc, [feed], core_ids=[0])
    got = r.results[0]["out_dram"]
    return got.transpose(1, 0, 2).reshape(B, S, D)
```

```python
from contextlib import ExitStack

import concourse.bass as bass
from concourse import mybir

P = 128
B, S, D = 32, 64, 128
NPAIR = B * S // P
NG = 4
PPG = NPAIR // NG
BPG = B // NG
GT = PPG * P
F32 = mybir.dt.float32
BF16 = mybir.dt.bfloat16
F32R = mybir.dt.float32r
ALU = mybir.AluOpType
ACT = mybir.ActivationFunctionType
AX = mybir.AxisListType.X

LN_EPS, RMS_EPS, RMS3_EPS = 1e-5, 1.1920929e-07, 1e-8
FLT_MAX = 3.4028234e38

L0A, L0F, L1A, L1F, L2A, L2F, L2M, L3A, L3F = range(9)
ATT = {L0A: 0, L1A: 1, L2A: 2, L2F: 3, L3A: 4}
NORMS = [1, 1, 1, 1, 1, 2, 1, 3, 1]
TURNS = [1, 1, 1, 1, 1, 1, 1, 2, 1]


def before(counts, k):
    return NG * sum(counts[:k])


X_UPS = [NPAIR if k in ATT else NG for k in range(9)]


def x_after(k):
    return sum(X_UPS[:k + 1])


PACK_FIRST = [("L0_WQ", 128), ("L0_WK", 128), ("L0_WV", 128), ("L0_WO", 128),
              ("L1_Wq", 128), ("L1_Wk", 128), ("L1_Wv", 128), ("L1_Wo", 128),
              ("L2_q", 8), ("L2_k", 8), ("L2_v", 8),
              ("c_L0b1", 4), ("c_L0b2", 1), ("c_bq", 1), ("c_bk", 1), ("c_bv", 1),
              ("c_L1b1", 4), ("c_L1b2", 1), ("c_n1", 1), ("c_n2", 1), ("c_qn", 1), ("c_kn", 1),
              ("c_lxg", 1), ("c_lxb", 1), ("c_llg", 1), ("c_llb", 1), ("c_qg", 1), ("c_kg", 1),
              ("c_scale", 1)]
PACK = PACK_FIRST + [
    ("U1", 32), ("V1", 512), ("U2", 128), ("V2", 128),
    ("W1T", 512), ("W2T", 512), ("L2_WoT", 128),
    ("wqkT", 256), ("wvT", 128), ("woT", 128), ("gateT", 4),
    ("e0_up", 256), ("e0_down", 256), ("e1_w1", 256), ("e1_w2", 256), ("e1_down", 256),
    ("e2_l1", 256), ("e2_l2", 512), ("e2_l3", 512), ("e2_l4", 256),
    ("e3_down", 128), ("e3_up", 256), ("e3_out", 256),
    ("L3_Wq", 128), ("L3_Wkv", 256), ("L3_Wout", 128)]
NFIRST = sum(_w for _, _w in PACK_FIRST)
OFF = {}
_at = 0
for _n, _w in PACK:
    OFF[_n] = (_at, _w)
    _at += _w
NPACK = _at


MOE_CHUNKS = [("e2_l1", 0, 0), ("e2_l1", 1, 1), ("e3_down", 0, 2), ("e0_up", 0, 8), ("e0_up", 1, 9),
              ("e2_l2", 0, 6), ("e2_l2", 1, 7), ("e3_up", 0, 10), ("e3_up", 1, 11),
              ("e2_l3", 0, 0), ("e2_l3", 1, 1),
              ("e1_w1", 0, 4), ("e1_w2", 0, None), ("e1_w1", 1, 5), ("e1_w2", 1, None)]
MOE_IN = {"e2_l2": ([0, 1], 1), "e2_l3": ([6, 7], 6), "e3_up": ([2], 2)}
MOE_OUTS = [(6, 0, "e0_down", (8, 9), 4), (12, 3, "e3_out", (10, 11), 8),
            (14, 2, "e2_l4", (0, 1), 10), (14, 1, "e1_down", (4, 5), 13)]
NCH = len(MOE_CHUNKS)


def acts_through(n):
    return sum(dst is not None for _, _, dst in MOE_CHUNKS[:n + 1])


NACT = acts_through(NCH - 1)
H_PS = {L0F: 0, L1F: NG * 6, L2M: NG * 10}
H_SB = {L0F: 0, L1F: NG * 6, L2M: NG * 10}
NCH3 = 32
PART = (slice(0, 2 * P), slice(2 * P, 3 * P))
LAG3 = 3


def chunked(eng, body):
    for par in range(2):
        body(0, par, par == 0, False)
    with eng.Fori(1, NCH3 // 2 - 1) as j:
        for par in range(2):
            body(j, par, False, False)
    for par in range(2):
        body(NCH3 // 2 - 1, par, False, par == 1)


def groups(eng, body):
    body(0, True)
    with eng.Fori(1, NG - 1) as g:
        body(g, True)
    body(NG - 1, False)


def norm_no(k, g, t=0):
    return before(NORMS, k) + NG * t + g + 1


def done_no(k, g, t=0):
    return before(NORMS, k) + (g + 1 if t == 0 else NG + (NORMS[k] - 1) * g + t)


def turned(k, g, t=0):
    return before(TURNS, k) + TURNS[k] * g + t + 1


def wait(eng, sem, value):
    if isinstance(value, int) and value <= 0:
        return
    eng.wait_ge(sem, value)


KX_DVE = 4


def pipelined(eng, steps):
    lo = min(lag for lag, _ in steps)
    hi = max(lag for lag, _ in steps)
    first = hi + hi % 2 + 2
    last = NPAIR + min(lo, 0)
    last -= (last - first) % 2

    def turn(t):
        for lag, step in steps:
            if 0 <= t - lag < NPAIR:
                step(t - lag, None)

    for t in range(lo, first):
        turn(t)
    with eng.Fori(0, (last - first) // 2) as j:
        for half in range(2):
            for lag, step in steps:
                step(2 * j + (first + half - lag), (first + half - lag) % 2)
    for t in range(last, NPAIR + hi):
        turn(t)


def build_program(nc, x, ctx_tok, ctx_T2, mask_q, mask_qk, mask_key, pack, rows, lora_A, lora_B,
                  experts, out):
    es = ExitStack()
    with es:
        def sb(name, shape, dt=F32):
            return es.enter_context(nc.sbuf_tensor(name, shape, dt))

        def sem(name):
            return es.enter_context(nc.semaphore(name))

        X = sb("X", [P, NPAIR, D])
        Zr = sb("Zr", [P, NPAIR, D])
        CTX = Zr
        arena = sb("arena", [P, 12 * GT])
        W = sb("W", [P, NPACK])
        ROWS = sb("ROWS", [1, 3 * D])
        XH = sb("XH", [P, NG, GT], F32R)
        XL = sb("XL", [P, NG, GT], F32R)
        EW = sb("EW", [P, 2, 3 * P])
        EH = sb("EH", [P, 2, 3 * P], F32R)
        EL = sb("EL", [P, 2, 3 * P], F32R)
        HH = sb("HH", [P, NG, GT], F32R)
        HL = sb("HL", [P, NG, GT], F32R)
        QT = sb("QT", [P, NPAIR, P])
        KT = sb("KT", [P, B, P])
        KT64 = KT[:, 0:B // 2, :].rearrange("p a (b k) -> p (a b) k", k=S)
        V = sb("V", [P, B, D])
        ctx2 = sb("ctx2", [P, 2, BPG, 2, S])
        yT2 = CL = ctx2[:, 0, :, :, :]
        LA = arena[0:16, 0:512].rearrange("p (n d) -> p n d", n=4)
        LB = arena[0:16, 512:1024].rearrange("p (n d) -> p n d", n=4)
        Kx = arena[:, 0:4096].rearrange("p (r b c) -> p r b c", r=2, b=2)
        Qs = sb("Qs", [P, 2, P])
        PR = arena[:, 4096:6144].rearrange("p (r c) -> p r c", r=2)
        arena2 = sb("arena2", [P, 4 * GT])
        PT = arena2[:, :].rearrange("p (r n q) -> p r n q", r=2, n=8)
        Vz = sb("Vz", [P, 2, 2, 384])
        cT = sb("cT", [P, 2, P])
        mx = sb("mx", [P, 2, 16])
        Oz = sb("Oz", [P, 384])
        rcT = sb("rcT", [P, P])
        kd = sb("kd", [P, 2, P], BF16)
        st = sb("st", [P, 2, NPAIR, 6])
        spare = sb("spare", [P, 3 * NG + 1])
        mv = sb("mv", [P, 2, NG, PPG, 2])
        ve = sb("ve", [P, 2, NG, PPG])
        rstd = sb("rstd", [P, 2, NG, PPG])
        y = arena2[:, 0:GT].rearrange("p (j d) -> p j d", d=D)
        yy = arena2[:, GT:2 * GT].rearrange("p (j d) -> p j d", d=D)
        y3 = arena[:, 4096:6144].rearrange("p (n d) -> p n d", d=D)
        yT = arena2[:, 2 * GT:3 * GT]
        Hs = arena[:, :].rearrange("p (n t) -> p n t", n=12)
        oT = arena2[:, 3 * GT:4 * GT]
        sG = arena[:, 0:2 * GT].rearrange("p (n t) -> p n t", n=2)
        Hf = arena[:, 2 * GT:6 * GT].rearrange("p (n t) -> p n t", n=4)
        oT3 = arena[:, 6 * GT:10 * GT].rearrange("p (n t) -> p n t", n=4)
        sq = arena[:, 2048:3584]
        ss = sb("ss", [P, 128])
        rs = sb("rs", [P, 128])
        rt = sb("rt", [P, 128])
        qkn = arena[:, 0:1536]
        oddT = sb("oddT", [P, 2, BPG, 4])
        Er = sb("Er", [32, 4, D])
        E2 = sb("E2", [P, 4, 32])
        XO = sb("XO", [32, BPG, S])
        part = sb("part", [P, GT])
        GM = part[:, :].rearrange("p (b s) -> p b s", s=S)
        lg = sb("lg", [P, PPG, 4])
        fin = sb("fin", [P, PPG, 4], mybir.dt.uint32)
        lgz = sb("lgz", [P, PPG, 4])
        gmx = sb("gmx", [P, PPG])
        gs = sb("gs", [P, PPG])
        cmp = sb("cmp", [P, PPG, 4, 4])
        tie = sb("tie", [P, PPG, 4, 4])
        rank = sb("rank", [P, PPG, 4])
        moe = part[:, :].rearrange("p (j d) -> p j d", d=D)
        zero = arena2[:, 0:512]
        ident = sb("ident", [P, P])
        identb = sb("identb", [P, P], BF16)
        hm16a = sb("hm16a", [P, 16])
        hm16 = sb("hm16", [P, 16])
        hm2 = sb("hm2", [P, 2])
        causal = sb("causal", [P, S], BF16)
        causalf = sb("causalf", [P, S])
        ones = sb("ones", [P, P])
        sel2f = sb("sel2f", [2, 2, S])
        sel2 = sb("sel2", [2, P], BF16)
        low4 = sb("low4", [P, 4, 4])
        eps_c = sb("eps_c", [P, 3])
        mhalf = sb("mhalf", [P, 32])
        Sel1 = sb("Sel1", [P, PPG, BPG, 4])
        Sel2 = sb("Sel2", [P, PPG, 4, 32])
        mB = sb("mB", [P, 4, BPG])
        dB = sb("dB", [P, BPG])
        mR = sb("mR", [P, 32, 4])
        dR = sb("dR", [P, 4])
        mq_i = sb("mq_i", [P, NPAIR], mybir.dt.int32)
        keep = sb("keep", [P, NPAIR])
        mqk_i = arena[:, 4096:5120].bitcast(mybir.dt.int32).rearrange("p (n k) -> p n k", k=S)
        mqk = sb("mqk", [P, NPAIR, S], BF16)
        mk_i = arena[0:2, 5120:6144].bitcast(mybir.dt.int32).rearrange("p (n k) -> p n k", k=S)
        mk = sb("mk", [2, NPAIR, S], BF16)
        W1m = sb("W1m", [P, 4, D])
        BD = sb("BD", [P, 3, 16, 8])

        PS = es.enter_context(nc.psum_tensor("PS", [P, 8, 512], F32))
        PSf = PS[:, :, :].rearrange("p a b -> p (a b)")

        def w(name, i=None, n=128, rows_=P):
            o, size = OFF[name]
            if i is None:
                return W[0:rows_, o:o + size]
            return W[0:rows_, o + i * n:o + (i + 1) * n]

        def col(name, i=0):
            o = OFF[name][0] + i
            return W[:, o:o + 1]

        dma_x, dma_ctx, dma_pack, dma_small, dma_rest, dma_out = (
            sem(n) for n in ("dma_x", "dma_ctx", "dma_pack", "dma_small", "dma_rest", "dma_out"))
        consts, consts_v, lora_ps, x_ready = (sem(n) for n in ("consts", "consts_v", "lora_ps", "x_ready"))
        n_stats, n_aggr, n_ve, n_rstd, n_done = (sem("n_" + n) for n in ("stats", "aggr", "ve", "rstd", "done"))
        t_ps, t_sb = (sem(n) for n in ("t_ps", "t_sb"))
        kv_ps, q_ps, k_sb, v_sb, q_sb = (sem("p_" + n) for n in ("kv_ps", "q_ps", "k_sb", "v_sb", "q_sb"))
        sq_sb, ss_sb, rs_sb, qkn_sb, qk_turned = (sem("r_" + n) for n in ("sq", "ss", "rs", "qkn", "turned"))
        kx_v, kx_p, qs_sb, sc_ps, mx_sb, sub_sb, exp_sb, rc_sb, row_sb = (
            sem("a_" + n) for n in ("kx_v", "kx_p", "qs", "sc", "mx", "sub", "exp", "rc", "row"))
        pt_ps, pt_sb, vz_sb, pv_ps, ct_sb, o_ps, kd_sb = (
            sem("a_" + n) for n in ("pt_ps", "pt_sb", "vz", "pv", "ct", "o", "kd"))
        h_ps, h_sb, h_mul, acc_ps, o_sb, ot_ps = (sem("f_" + n) for n in ("h_ps", "h_sb", "h_mul", "acc", "o_sb", "ot"))
        e_ps, e_sb, odd_sb, xo_ps, xo_sb, g_ps, g_sb = (
            sem("l_" + n) for n in ("e_ps", "e_sb", "odd", "xo_ps", "xo_sb", "g_ps", "g_sb"))
        lg_ps, gate_v, gate_e, wt_sb, oe_ps, derived = (
            sem("m_" + n) for n in ("lg", "gate_v", "gate_e", "wt", "oe", "derived"))
        sums_sb, root_sb, n_gate, w_done, moe_sb, x_part, n_ms, n_kp = (
            sem(n) for n in ("r_sums", "r_root", "m_gate2", "m_w", "m_sum", "m_x", "n_ms", "n_kp"))

        dma_ctx2 = [sem(f"dma_ctx2_{n}") for n in range(2)]
        dma_moe = [sem(f"dma_moe{m}") for m in range(2)]
        xh_sb, eh_sb, el_sb, sg_sb, hf_sb, hh_sb, hl_sb, gu_ps, d_ps = (
            sem("e_" + n) for n in ("xh", "eh", "el", "sg", "hf", "hh", "hl", "gu", "down"))

        SMALL = 16 * 6
        TOK = [L0A, L1A, L2A]

        block = es.enter_context(nc.Block())

        @block.sync
        def _(sp):
            sp.dma_start(W[:, 0:NFIRST], pack[:, 0:NFIRST]).then_inc(dma_pack, 16)
            sp.dma_start(X[:, :, :], x).then_inc(dma_x, 16)
            for g in range(2):
                sp.dma_start(ctx2[:, g, :, :, :], ctx_T2[:, g, :, :, :]).then_inc(dma_ctx2[g], 16)
            for a in range(3):
                with sp.Fori(int(a == 0), NG // 2) as j:
                    for par in range(2):
                        sp.wait_ge(kv_ps, NG * a + 2 * j + par - 1)
                        sp.dma_start(ctx2[:, par, :, :, :], ctx_T2[:, 2 * j + par, :, :, :]).then_inc(dma_ctx2[par], 16)
            sp.wait_ge(x_ready, x_after(L2M))
            sp.dma_start(CTX[:, :, :], ctx_tok).then_inc(dma_ctx, 16)
            for par in range(2):
                sp.dma_start(EW[:, par, :], experts[:, par, :]).then_inc(dma_moe[par], 16)
            with sp.Fori(1, NCH3 // 2) as j:
                for par in range(2):
                    sp.wait_ge(el_sb, 4 * j + 2 * par - 2)
                    sp.dma_start(EW[:, par, :], experts[:, 2 * j + par, :]).then_inc(dma_moe[par], 16)
            for g in range(NG):
                sp.wait_ge(x_ready, x_after(L3A) + g + 1)
                sp.dma_start(out[:, PPG * g:PPG * (g + 1), :], X[:, PPG * g:PPG * (g + 1), :]).then_inc(dma_out, 16)
            sp.wait_ge(dma_out, 16 * NG)

        @block.gpsimd
        def _(pool):
            pool.memset(zero[:, :], 0.0).then_inc(consts, 1)
            pool.memset(ones[:, :], 1.0).then_inc(consts, 1)
            pool.memset(mhalf[:, :], -0.5).then_inc(consts, 1)
            pool.memset(eps_c[:, 0:1], LN_EPS).then_inc(consts, 1)
            pool.memset(eps_c[:, 1:2], RMS_EPS).then_inc(consts, 1)
            pool.memset(eps_c[:, 2:3], 0.0).then_inc(consts, 1)
            pool.memset(causalf[:, :], 0.0).then_inc(consts, 1)
            pool.memset(Vz[:, :, :, :], 0.0).then_inc(consts, 1)
            pool.memset(Oz[:, :], 0.0).then_inc(consts, 1)
            pool.wait_ge(consts, 9)

            def pick(o, src, pattern, base, cm, op=ALU.not_equal, fill=1.0):
                pool.affine_select(out=o, in_=src, compare_op=op, fill=fill, base=base, pattern=pattern,
                                   channel_multiplier=cm).then_inc(consts, 1)

            pick(ident[:, :], zero[:, 0:P], [[-1, P]], 0, 1)
            pick(hm16a[:, :], mhalf[:, 0:16], [[-8, 16]], 0, 1, ALU.is_ge, 0.0)
            pick(mB[:, :, :], mhalf[:, 0:32].rearrange("p (c b) -> p c b", c=4), [[-32, 4], [-4, 8]], 0, 1, ALU.is_ge, 0.0)
            pick(mR[:, :, :], zero[:, 0:128].rearrange("p (m r) -> p m r", r=4), [[-4, 32], [-1, 4]], 0, 1)
            pick(Sel1[:, :, :, :], zero[:, 0:128].rearrange("p (j b r) -> p j b r", j=4, b=8),
                 [[128, 4], [-64, 8], [-2, 4]], -1, 1)
            pick(Sel2[:, :, :, :].rearrange("p j c (b r) -> p j c b r", b=8),
                 zero[:, 0:512].rearrange("p (j c b r) -> p j c b r", j=4, c=4, b=8),
                 [[128, 4], [0, 4], [-64, 8], [-2, 4]], -9, 1)
            pool.wait_ge(consts, 15)
            pick(hm16[:, :], hm16a[:, :], [[8, 16]], 7, -1, ALU.is_ge, 0.0)
            pick(mB[:, :, :], mB[:, :, :], [[32, 4], [4, 8]], 3, -1, ALU.is_ge, 0.0)
            pick(hm2[:, :], mhalf[:, 0:2], [[-64, 2]], 0, 1, ALU.is_ge, 0.0)
            pick(low4[:, :, :], zero[:, 0:16].rearrange("p (e j) -> p e j", e=4), [[-1, 4], [1, 4]], 0, 0, ALU.is_ge, 1.0)
            pool.wait_ge(consts, 19)
            pick(hm2[:, :], hm2[:, :], [[64, 2]], 63, -1, ALU.is_ge, 0.0)
            pool.wait_ge(consts, 20)
            pick(sel2f[:, :, :], zero[0:2, 0:P].rearrange("p (b q) -> p b q", b=2), [[-1, 2], [0, S]], 0, 1)
            pool.wait_ge(consts, 21)
            pick(causalf[0:64, :], causalf[0:64, :], [[-1, S]], 0, 1, ALU.is_ge, -1e9)
            pool.wait_ge(consts, 22)
            pick(causalf[64:128, :], causalf[64:128, :], [[-1, S]], 0, 1, ALU.is_ge, -1e9)
            for h in range(2):
                pool.memset(Oz[64 * h:64 * h + 64, :].rearrange("p (n c) -> p n c", c=48)[:, :, 8 * h:8 * h + 8],
                            1.0).then_inc(consts, 1)

            def rstd_of(k, g, eps, t=0, ms=None, kp=None):
                v, r = norm_no(k, g, t), int(t == 2)
                pool.wait_ge(n_aggr, v)
                var, mu = mv[:, r, g, :, 1], mv[:, r, g, :, 0]
                e, out_ = ve[:, r, g, :], rstd[:, r, g, :]
                if ms is not None:
                    pool.tensor_tensor(out_, mu, mu, ALU.mult).then_inc(n_ms, 1)
                    pool.wait_ge(n_ms, 2 * ms + 1)
                    pool.tensor_tensor(out_, var, out_, ALU.add).then_inc(n_ms, 1)
                    pool.wait_ge(n_ms, 2 * ms + 2)
                    var = out_
                pool.tensor_tensor(e, var, eps_c[:, eps:eps + 1].to_broadcast([P, PPG]), ALU.add).then_inc(n_ve, 1)
                pool.wait_ge(n_ve, v)
                if kp is None:
                    pool.tensor_tensor(out_, e, mhalf[:, 0:PPG], ALU.pow).then_inc(n_rstd, 1)
                else:
                    pool.tensor_tensor(e, e, mhalf[:, 0:PPG], ALU.pow).then_inc(n_kp, 1)
                    pool.wait_ge(n_kp, v)
                    pool.tensor_tensor(out_, e, kp, ALU.mult).then_inc(n_rstd, 1)

            def pairs(a, nh, nk):
                hm = hm16 if nh == 16 else hm2
                nc_ = nh * nk
                kt = KT64 if nk == S else KT[:, :, :]

                def spread(p, par):
                    par = p % 2 if par is None else par
                    early = isinstance(p, int) and a < ATT[L2F]
                    pool.wait_ge(k_sb, NG * a + p // PPG + 1 if early else NG * (a + 1))
                    wait(pool, sc_ps, NPAIR * a + p - 1)
                    for b in range(2):
                        h0 = (nh if nh == 2 else KX_DVE) if b == 0 else 0
                        if h0 < nh:
                            ins = pool.tensor_tensor(Kx[:, par, b, h0 * nk:nc_].rearrange("p (h k) -> p h k", k=nk),
                                                     kt[:, 2 * p + b, :].unsqueeze(1).to_broadcast([P, nh - h0, nk]),
                                                     hm[:, h0:nh].unsqueeze(2).to_broadcast([P, nh - h0, nk]),
                                                     ALU.mult)
                    ins.then_inc(kx_p, 1)

                pipelined(pool, [(-1, spread)])

            pool.wait_ge(consts_v, 1)
            for k in range(9):
                for t in range(NORMS[k]):
                    for g in range(NG):
                        if k == L0A:
                            rstd_of(k, g, 0, kp=keep[:, PPG * g:PPG * (g + 1)])
                        elif k == L2M:
                            rstd_of(k, g, 1, ms=NG + g)
                        elif k == L2F and t == 1:
                            rstd_of(k, g, 1, t, ms=g)
                        else:
                            rstd_of(k, g, 0, t)
                if k in ATT:
                    pairs(ATT[k], *((2, 128) if k == L3A else (16, 64)))

        @block.scalar
        def _(act):
            act.dma_start(ROWS[:, :], rows).then_inc(dma_small, 16)
            act.dma_start(LA[:, :, :], lora_A).then_inc(dma_small, 16)
            act.dma_start(LB[:, :, :], lora_B).then_inc(dma_small, 16)
            act.dma_start(mq_i[:, :], mask_q).then_inc(dma_small, 16)
            act.dma_start(mqk_i[:, :, :], mask_qk).then_inc(dma_small, 16)
            act.dma_start(mk_i[:, :, :], mask_key).then_inc(dma_small, 16)
            act.dma_start(W[:, NFIRST:NPACK], pack[:, NFIRST:NPACK]).then_inc(dma_rest, 16)
            act.wait_ge(consts_v, 1)

            def turn_out(k, g, t, outs, scale=None, bias=None):
                act.wait_ge(t_ps, turned(k, g, t))
                for n, o in enumerate(outs):
                    src = PS[:, 7, :]
                    if len(o.shape) == 3:
                        src = src.rearrange("p (b s) -> p b s", s=S)
                    if scale is None:
                        ins = act.activation(o, src, ACT.Copy)
                    else:
                        ins = act.activation(o, src, ACT.Identity, bias=bias if bias is not None else 0.0, scale=scale)
                ins.then_inc(t_sb, 1)

            def pairs(k):
                a = ATT[k]
                L3 = k == L3A
                nc_ = 256 if L3 else 1024
                scale = {L0A: 8 ** -0.5, L1A: 8 ** -0.5, L2A: 128 ** -0.5, L2F: 8 ** -0.5, L3A: 64 ** -0.5}[k]

                def exps(p, par):
                    par = p % 2 if par is None else par
                    act.wait_ge(sub_sb, NPAIR * a + p + 1)
                    act.activation(PR[:, par, 0:nc_], PR[:, par, 0:nc_], ACT.Exp, scale=scale).then_inc(exp_sb, 1)

                def query(p, par):
                    par = p % 2 if par is None else par
                    wait(act, sc_ps, NPAIR * a + p - 1)
                    act.activation(Qs[:, par, :], QT[:, p, :], ACT.Copy).then_inc(qs_sb, 1)

                def values(p, par):
                    par = p % 2 if par is None else par
                    wait(act, pv_ps, NPAIR * a + p - 1)
                    if L3:
                        ins = act.activation(Vz[:, par, :, 0:P], V3p(p), ACT.Copy)
                    else:
                        for h in range(2):
                            dst = Vz[64 * h:64 * h + 64, par, :, :].rearrange("p b (n c) -> p b n c", c=48)[:, :, :, 8 * h:8 * h + 8]
                            src = V3p(p)[64 * h:64 * h + 64].rearrange("p b (n c) -> p b n c", c=16)[:, :, :, 8 * h:8 * h + 8]
                            ins = act.activation(dst, src, ACT.Copy)
                    ins.then_inc(vz_sb, 1)

                def V3p(p):
                    return V[:, :, :].rearrange("p (a b) d -> p a b d", b=2)[:, p]

                def probs_out(p, par):
                    par = p % 2 if par is None else par
                    n = nc_ // P // 2
                    wait(act, pv_ps, NPAIR * a + p - 1)
                    for half in range(2):
                        act.wait_ge(pt_ps, 2 * (NPAIR * a + p) + half + 1)
                        act.activation(PT[:, par, n * half:n * (half + 1), :],
                                       PS[:, 4 + half, 0:n * P].rearrange("p (n q) -> p n q", n=n),
                                       ACT.Copy).then_inc(pt_sb, 1)

                pipelined(act, [(-1, query), (1, values), (1, probs_out), (0, exps)])

            def half_root(u, n):
                act.wait_ge(ss_sb, u + 1)
                act.activation(rt[:, 0:n], ss[:, 0:n], ACT.Sqrt, scale=0.25).then_inc(root_sb, 1)

            def start(k):
                if k == L2F:
                    turn_l2f(0)
                    squares_l2f(0)
                    half_root(0, 128)
                elif k == L3A:
                    turn_l3a(0)
                    squares_l3a(0)
                elif k in (L0F, L1F):
                    turn_out(k, 0, 0, [yT[:, :]])
                elif k == L2M:
                    turn_out(k, 0, 0, [yT[:, :]], scale=col("c_n2"))
                if k == L0F:
                    first_hidden(0)

            def turn_l2f(g):
                turn_out(L2F, g, 0, [yT2[:, :, 0, :], yT2[:, :, 1, :], yT[:, :]], scale=col("c_n1"))

            def turn_l3a(g):
                turn_out(L3A, g, 0, [CL[:, :, 1, :], yT[:, :]], scale=col("c_llg"), bias=col("c_llb"))
                turn_out(L3A, g, 1, [CL[:, :, 0, :]], scale=col("c_lxg"), bias=col("c_lxb"))

            def squares_l2f(g):
                act.wait_ge(q_ps, NG * 3 + g + 1)
                act.activation(sq[:, 0:1024], PSf[:, 0:1024], ACT.Square).then_inc(sq_sb, 1)

            def squares_l3a(g):
                act.wait_ge(q_ps, NG * 4 + g + 1)
                kps = PSf[:, 0:2048].rearrange("p (b c) -> p b c", c=256)
                act.activation(sq[:, 0:1024].rearrange("p (b c) -> p b c", c=P), kps[:, :, 0:P], ACT.Square)
                act.activation(sq[:, 1024:1536], PS[:, 4, :], ACT.Square).then_inc(sq_sb, 1)
                act.activation(V[:, :, :].rearrange("p (g b) d -> p g b d", b=BPG)[:, g], kps[:, :, P:256],
                               ACT.Copy).then_inc(v_sb, 1)

            def first_hidden(g):
                act.wait_ge(h_ps, H_PS[L0F] + 6 * g + 1)
                act.activation(Hs[0:32, 0, :], PS[0:32, 0, :], ACT.Copy).then_inc(h_sb, 1)

            def group_work(k, g, more):
                if k in TOK:
                    a = ATT[k]
                    if not isinstance(g, int) or g > 0:
                        turn_out(k, g, 0, [yT[:, :]])
                    act.wait_ge(kv_ps, NG * a + g + 1)
                    kdst = KT64.rearrange("p (g b) s -> p g (b s)", b=BPG)[:, g]
                    if k == L1A:
                        act.activation(kdst, PS[:, 1, :], ACT.Identity, bias=col("c_bk")).then_inc(k_sb, 1)
                    else:
                        act.activation(kdst, PS[:, 1, :], ACT.Copy).then_inc(k_sb, 1)
                    if isinstance(g, int) and g == 0:
                        turn_out(k, g, 0, [yT[:, :]])
                    act.wait_ge(q_ps, NG * a + g + 1)
                    qdst = QT[:, :, :].rearrange("p (g j) q -> p g (j q)", j=PPG)[:, g]
                    if k == L1A:
                        act.activation(qdst, PS[:, 0, :], ACT.Identity, bias=col("c_bq")).then_inc(q_sb, 1)
                    else:
                        act.activation(qdst, PS[:, 0, :], ACT.Copy).then_inc(q_sb, 1)
                elif k == L2F:
                    if more:
                        turn_l2f(g + 1)
                        squares_l2f(g + 1)
                        half_root(g + 1, 128)
                    act.wait_ge(qk_turned, g + 1)
                    act.activation(QT[:, :, :].rearrange("p (g j) q -> p g (j q)", j=PPG)[:, g], PS[:, 5, :],
                                   ACT.Identity, scale=col("c_qn")).then_inc(q_sb, 1)
                    act.activation(KT64.rearrange("p (g b) s -> p g (b s)", b=BPG)[:, g], PS[:, 6, :],
                                   ACT.Identity, scale=col("c_kn")).then_inc(k_sb, 1)
                elif k == L3A:
                    half_root(NG + g, 24)
                    if more:
                        turn_l3a(g + 1)
                        squares_l3a(g + 1)
                    act.wait_ge(qk_turned, NG + g + 1)
                    act.activation(KT[:, :, :].rearrange("p (g b) s -> p g (b s)", b=BPG)[:, g], PSf[:, 2560:3584],
                                   ACT.Identity, scale=col("c_kg")).then_inc(k_sb, 1)
                    act.activation(QT[:, :, :].rearrange("p (g j) q -> p g (j q)", j=PPG)[:, g], PS[:, 7, :],
                                   ACT.Identity, scale=col("c_qg")).then_inc(q_sb, 1)
                elif k == L0F:
                    u = H_PS[L0F] + 6 * g
                    for c in range(4):
                        act.wait_ge(h_ps, u + 2 + c)
                        act.activation(Hs[:, 1 + c, :], PS[:, (1 + c) % 4, :], ACT.Gelu_apprx_tanh,
                                       bias=col("c_L0b1", c)).then_inc(h_sb, 1)
                    if more:
                        turn_out(k, g + 1, 0, [yT[:, :]])
                    act.wait_ge(h_ps, u + 6)
                    act.activation(Hs[0:32, 5, :], PS[0:32, 5, :], ACT.Copy).then_inc(h_sb, 1)
                    if more:
                        first_hidden(g + 1)
                    act.wait_ge(acc_ps, g + 1)
                    act.activation(oT[:, :], PS[:, 4, :], ACT.Identity, bias=col("c_L0b2")).then_inc(o_sb, 1)
                elif k == L1F:
                    u = H_PS[L1F] + 4 * g
                    for c in range(4):
                        act.wait_ge(h_ps, u + 1 + c)
                        act.activation(Hs[:, c, :], PS[:, c, :], ACT.Gelu, bias=col("c_L1b1", c)).then_inc(h_sb, 1)
                    if more:
                        turn_out(k, g + 1, 0, [yT[:, :]])
                    act.wait_ge(acc_ps, NG + g + 1)
                    act.activation(oT[:, :], PS[:, 4, :], ACT.Identity, bias=col("c_L1b2")).then_inc(o_sb, 1)
                elif k == L2M:
                    wait(act, oe_ps, 4 * g)
                    for n, (name, c, dst) in enumerate(MOE_CHUNKS):
                        if dst is None:
                            continue
                        act.wait_ge(h_ps, H_PS[L2M] + NCH * g + n + 1)
                        act.activation(Hs[:, dst, :], PS[:, n % 4, :],
                                       ACT.Silu if name == "e1_w1" else ACT.Gelu).then_inc(h_sb, 1)
                        if n == 2:
                            act.wait_ge(gate_v, 7 * g + 5)
                            act.activation(lgz[:, :, :], lgz[:, :, :], ACT.Exp).then_inc(gate_e, 1)
                    if more:
                        turn_out(k, g + 1, 0, [yT[:, :]], scale=col("c_n2"))
                else:
                    act.wait_ge(t_ps, turned(k, g))
                    act.activation(XH[:, g, :], PS[:, 4:8, :][:, g, :], ACT.Copy).then_inc(xh_sb, 1)

            def high(j, par, down):
                act.wait_ge(dma_moe[par], 16 * j + 16)
                if down:
                    wait(act, d_ps, NG * (2 * j + par - 1))
                else:
                    wait(act, gu_ps, 2 * NG * (2 * j + par - 1))
                c = PART[down]
                act.activation(EH[:, par, c], EW[:, par, c], ACT.Copy).then_inc(eh_sb, 1)

            def experts_work():
                def chunk(j, par, first, last):
                    for g in range(NG):
                        u = NG * (2 * j + par) + g
                        act.wait_ge(gu_ps, 2 * u + 1)
                        if g >= 2 or not first:
                            act.wait_ge(hf_sb, u - 1)
                        act.activation(sG[:, g % 2, :], PS[:, g % 2, :], ACT.Silu).then_inc(sg_sb, 1)
                        if g % 2 == 1 and not first and not last:
                            high(j + par, 1 - par, g // 2)
                        act.wait_ge(hf_sb, u + 1)
                        if not first:
                            act.wait_ge(d_ps, u - NG + 1)
                        act.activation(HH[:, g, :], Hf[:, g, :], ACT.Copy).then_inc(hh_sb, 1)

                chunked(act, chunk)
                for g in range(NG):
                    act.wait_ge(d_ps, NG * (NCH3 - 1) + g + 1)
                    act.activation(oT3[:, g, :], PS[:, 4 + g, :], ACT.Copy).then_inc(o_sb, 1)

            for k in range(9):
                if k == L3F:
                    for par in range(2):
                        for down in range(2):
                            high(0, par, down)
                if k > 0:
                    act.wait_ge(x_ready, x_after(k - 1))
                start(k)
                groups(act, lambda g, more, k=k: group_work(k, g, more))
                if k in ATT:
                    pairs(k)
            experts_work()

        @block.vector
        def _(dve):
            dve.wait_ge(consts, 25)
            dve.wait_ge(dma_small, SMALL)
            dve.wait_ge(dma_pack, 16)
            cv = [0]

            def made(ins):
                cv[0] += 1
                ins.then_inc(derived, 1)

            def settle():
                dve.wait_ge(derived, cv[0])

            made(dve.tensor_copy(identb[:, :], ident[:, :]))
            made(dve.tensor_scalar(hm16[:, :], hm16[:, :], -2.0, None, ALU.mult))
            made(dve.tensor_scalar(hm2[:, :], hm2[:, :], -2.0, None, ALU.mult))
            made(dve.tensor_copy(causal[:, :], causalf[:, :]))
            made(dve.tensor_copy(sel2[:, :], sel2f[:, :, :].rearrange("p b q -> p (b q)")))
            made(dve.tensor_scalar(keep[:, :], mq_i[:, :], 0.0, None, ALU.is_equal))
            made(dve.tensor_scalar(mqk[:, :, :], mqk_i[:, :, :], 0.0, -1e20, ALU.is_equal, ALU.mult))
            made(dve.tensor_scalar(mk[:, :, :], mk_i[:, :, :], 0.0, -1e30, ALU.is_equal, ALU.mult))
            made(dve.tensor_reduce(dB[:, :], mB[:, :, :].rearrange("p c b -> p b c"), AX, ALU.add))
            made(dve.tensor_reduce(dR[:, :], mR[:, :, :].rearrange("p m r -> p r m"), AX, ALU.add))
            settle()
            made(dve.tensor_scalar(dB[:, :], dB[:, :], -2.0, col("c_scale"), ALU.mult, ALU.mult))
            for n, name in enumerate(("L2_q", "L2_k", "L2_v")):
                made(dve.tensor_tensor(BD[:, n, :, :], w(name).unsqueeze(1).to_broadcast([P, 16, 8]),
                                       hm16[:, :].unsqueeze(2).to_broadcast([P, 16, 8]), ALU.mult))
            dve.wait_ge(lora_ps, 1)
            settle()
            for n, name in enumerate(("L1_Wq", "L1_Wk", "L1_Wv", "L1_Wo")):
                ins = dve.scalar_tensor_tensor(W1m[:, n, :], PS[:, 0, P * n:P * n + P], 2.0, w(name), ALU.mult, ALU.add)
            ins.then_inc(consts_v, 1)
            dve.wait_ge(lora_ps, 2)
            dve.tensor_tensor(ROWS[:, 0:D], ROWS[:, 0:D], PS[0:1, 6, 0:D], ALU.add).then_inc(row_sb, 1)
            dve.wait_ge(dma_x, 16)

            def stats(src, s, r=0):
                dve.bn_stats(st[:, r, :, :][:, s], src).then_inc(n_stats, 1)

            def averages(k, g, t=0):
                r = int(t == 2)
                dve.wait_ge(n_stats, NPAIR * (sum(NORMS[:k]) + t) + PPG * (g + 1))
                dve.memset(spare[:, NG * t + g:NG * t + g + 1], 0.0)
                for j in range(PPG):
                    ins = dve.bn_aggr(mv[:, r, g, j, :], st[:, r, PPG * g + j, :])
                ins.then_inc(n_aggr, 1)

            def next_stats(k, s):
                stats((Zr if k == L2F else X)[:, s, :], s)

            def apply(k, g, src, dst, t=0, mean=True):
                r = int(t == 2)
                dve.wait_ge(n_rstd, norm_no(k, g, t))
                m, f = mv[:, r, :, :, :], rstd[:, r, :, :]
                for j in range(PPG):
                    if mean:
                        ins = dve.tensor_scalar(dst(g, j), src(g, j), m[:, g, j, 0:1], f[:, g, j:j + 1],
                                                ALU.subtract, ALU.mult)
                    else:
                        ins = dve.tensor_scalar(dst(g, j), src(g, j), f[:, g, j:j + 1], None, ALU.mult)
                ins.then_inc(n_done, 1)

            def group_stats(k, g):
                dve.wait_ge(x_ready, x_after(k - 1) + g + 1)
                for j in range(PPG):
                    next_stats(k, PPG * g + j)

            def tile_of(T):
                return lambda g, j: T[:, PPG * g + j, :]

            def y_tile(g, j):
                return y[:, j, :]

            def norm_group(k, g):
                if not isinstance(g, int) or g > 0:
                    dve.wait_ge(t_ps, turned(k, g) - 1)
                if k == L1F:
                    wait(dve, e_ps, g)
                if k == L2F:
                    apply(k, g, tile_of(Zr), y_tile, 1, mean=False)
                elif k == L3A:
                    apply(k, g, tile_of(y3), y_tile, 1)
                    apply(k, g, tile_of(CTX), lambda g, j: yy[:, j, :], 2)
                else:
                    apply(k, g, tile_of(Zr if k == L2M else X), y_tile, mean=k != L2M)

            def first_norm(k):
                if k == L2F:
                    apply(k, 0, tile_of(Zr), y_tile, 1, mean=False)
                else:
                    apply(k, 0, tile_of(y3), y_tile, 1)

            def context_norm():
                dve.wait_ge(dma_ctx, 16)
                for g in range(NG):
                    for p in range(PPG * g, PPG * (g + 1)):
                        stats(CTX[:, p, :], p, 1)
                    averages(L3A, g, 2)
                    if g == 1:
                        apply(L3A, 0, tile_of(CTX), lambda g, j: yy[:, j, :], 2)

            def start(k):
                if k == L0A:
                    for p in range(NPAIR):
                        stats(X[:, p, :], p)
                for g in range(NG):
                    averages(k, g)
                if k in (L2F, L3A):
                    z = Zr if k == L2F else y3
                    def second(g):
                        dve.wait_ge(n_done, done_no(k, g))
                        for p in range(PPG * g, PPG * (g + 1)):
                            stats(z[:, p, :], p)
                        averages(k, g, 1)

                    apply(k, 0, tile_of(X), tile_of(z))
                    for g in range(1, NG):
                        apply(k, g, tile_of(X), tile_of(z))
                        if g < 3:
                            second(g - 1)
                    first_norm(k)
                    second(2)
                    second(3)
                if k == L3A:
                    context_norm()
                elif k == L3F:
                    for par in range(2):
                        for down in range(2):
                            low(0, par, down)
                    for g in range(NG):
                        apply(k, g, tile_of(X), tile_of(y3))
                elif k != L2F:
                    norm_group(k, 0)

            def group(T, g):
                return T[:, :, :].rearrange("p (g j) d -> p g j d", j=PPG)[:, g]

            def add_group(k, g, u):
                dve.wait_ge(ot_ps, u)
                dve.tensor_tensor(group(X, g), group(X, g), PS[:, 5, :].rearrange("p (j d) -> p j d", j=PPG),
                                  ALU.add).then_inc(x_ready, 1)

            def head_factors(u, n, dim, eps, guard):
                dve.wait_ge(sums_sb, u + 1)
                dve.tensor_scalar(ss[:, 0:n], ss[:, 0:n], 1.0 / dim, eps, ALU.mult, guard).then_inc(ss_sb, 1)
                dve.wait_ge(root_sb, u + 1)
                dve.reciprocal(rs[:, 0:n], rt[:, 0:n]).then_inc(rs_sb, 1)
                dve.wait_ge(rs_sb, 4 * u + 1)
                dve.tensor_tensor(rs[:, 0:n], rs[:, 0:n], ss[:, 0:n], ALU.mult).then_inc(rs_sb, 1)
                dve.wait_ge(rs_sb, 4 * u + 2)
                dve.scalar_tensor_tensor(rs[:, 0:n], rs[:, 0:n], 0.25, rt[:, 0:n], ALU.mult, ALU.add).then_inc(rs_sb, 1)
                dve.wait_ge(rs_sb, 4 * u + 3)
                dve.reciprocal(rs[:, 0:n], rs[:, 0:n]).then_inc(rs_sb, 1)
                dve.wait_ge(rs_sb, 4 * u + 4)

            def pairs(k):
                a = ATT[k]
                L3 = k == L3A
                nh, nk = (2, 128) if L3 else (16, 64)
                nc_ = nh * nk
                hm = hm2 if L3 else hm16
                kt = KT[:, :, :] if L3 else KT64

                def spread(p, par):
                    par = p % 2 if par is None else par
                    wait(dve, sc_ps, NPAIR * a + p - 1)
                    n = nh if L3 else KX_DVE
                    dve.tensor_tensor(Kx[:, par, 0, 0:n * nk].rearrange("p (h k) -> p h k", h=n),
                                      kt[:, 2 * p, :].unsqueeze(1).to_broadcast([P, n, nk]),
                                      hm[:, 0:n].unsqueeze(2).to_broadcast([P, n, nk]),
                                      ALU.mult).then_inc(kx_v, 1)
                    if k == L0A:
                        dve.tensor_scalar(kd[:, par, :], identb[:, :], keep[:, :].unsqueeze(2)[:, p, :], None, ALU.mult).then_inc(kd_sb, 1)

                def maxima(p, par):
                    par = p % 2 if par is None else par
                    dve.wait_ge(sc_ps, NPAIR * a + p + 1)
                    s = PSf[:, 1024 * par:1024 * par + nc_].rearrange("p (h k) -> p h k", h=nh)
                    dve.tensor_reduce(mx[:, par, 0:nh], s, AX, ALU.max).then_inc(mx_sb, 1)

                def shift(p, par):
                    par = p % 2 if par is None else par
                    s = PSf[:, 1024 * par:1024 * par + nc_].rearrange("p (h k) -> p h k", h=nh)
                    dve.wait_ge(mx_sb, NPAIR * a + p + 1)
                    wait(dve, pt_ps, 2 * (NPAIR * a + p - 1))
                    dve.tensor_tensor(PR[:, par, 0:nc_].rearrange("p (h k) -> p h k", h=nh), s,
                                      mx[:, par, 0:nh].unsqueeze(2).to_broadcast([P, nh, nk]),
                                      ALU.subtract).then_inc(sub_sb, 1)

                def reciprocals(p, par):
                    par = p % 2 if par is None else par
                    dve.wait_ge(pv_ps, NPAIR * a + p + 1)
                    dve.reciprocal(rcT[:, :], PS[:, 6, 256 + P * par:256 + P * par + P]).then_inc(rc_sb, 1)

                def context(p, par):
                    par = p % 2 if par is None else par
                    dve.wait_ge(rc_sb, NPAIR * a + p + 1)
                    wait(dve, o_ps, NPAIR * a + p - 1)
                    dve.tensor_tensor(cT[:, par, :], PS[:, 6, P * par:P * par + P], rcT[:, :], ALU.mult).then_inc(ct_sb, 1)

                def add(p, par):
                    par = p % 2 if par is None else par
                    dve.wait_ge(o_ps, NPAIR * a + p + 1)
                    o = PS[:, 7, P * par:P * par + P]
                    if k == L2F:
                        dve.tensor_tensor(Zr[:, p, 32:D], Zr[:, p, 32:D], o[:, 32:D], ALU.add).then_inc(x_ready, 1)
                    else:
                        dve.tensor_tensor(X[:, p, :], X[:, p, :], o, ALU.add).then_inc(x_ready, 1)

                def after(p, par):
                    dve.wait_ge(x_ready, x_after(k) - NPAIR + p + 1)
                    next_stats(k, p)

                c = 3
                pipelined(dve, [(-1, spread), (c, reciprocals), (4, add), (c, context), (0, maxima), (5, after), (0, shift)])

            def group_work(k, g, more):
                if more and k not in (L1F, L2M, L3F):
                    norm_group(k, g + 1)
                if k in TOK:
                    a = ATT[k]
                    dve.wait_ge(kv_ps, NG * a + g + 1)
                    dve.tensor_copy(V[:, :, :].rearrange("p (g b) d -> p g (b d)", b=BPG)[:, g],
                                    PSf[:, 1024:2048]).then_inc(v_sb, 1)
                if k == L2F:
                    dve.wait_ge(sq_sb, g + 1)
                    dve.tensor_reduce(ss[:, 0:128], sq[:, 0:1024].rearrange("p (n d) -> p n d", d=8),
                                      AX, ALU.add).then_inc(sums_sb, 1)
                    head_factors(g, 128, 8, RMS_EPS, ALU.add)
                    wait(dve, qk_turned, g)
                    dve.tensor_tensor(qkn[:, 0:1024].rearrange("p (n d) -> p n d", d=8),
                                      PSf[:, 0:1024].rearrange("p (n d) -> p n d", d=8),
                                      rs[:, 0:128].unsqueeze(2).to_broadcast([P, 128, 8]), ALU.mult).then_inc(qkn_sb, 1)
                    dve.wait_ge(kv_ps, NG * 3 + g + 1)
                    dve.tensor_copy(V[:, :, :].rearrange("p (g b) d -> p g (b d)", b=BPG)[:, g],
                                    PSf[:, 1024:2048]).then_inc(v_sb, 1)
                if k == L3A:
                    dve.wait_ge(sq_sb, NG + g + 1)
                    dve.tensor_reduce(ss[:, 0:24], sq[:, :].rearrange("p (n d) -> p n d", d=64),
                                      AX, ALU.add).then_inc(sums_sb, 1)
                    head_factors(NG + g, 24, 64, RMS3_EPS ** 2, ALU.max)
                    dve.wait_ge(v_sb, NG * 4 + g + 1)
                    dve.wait_ge(qk_turned, NG + g)
                    for h in range(2):
                        dve.tensor_tensor(qkn[:, 0:1024].rearrange("p (b h d) -> p b h d", h=2, d=64)[:, :, h],
                                          PSf[:, 0:2048].rearrange("p (b c) -> p b c", c=256)[:, :, 64 * h:64 * h + 64],
                                          rs[:, h:16:2].unsqueeze(2).to_broadcast([P, BPG, 64]), ALU.mult)
                    dve.tensor_tensor(qkn[:, 1024:1536].rearrange("p (n d) -> p n d", d=64),
                                      PS[:, 4, :].rearrange("p (n d) -> p n d", d=64),
                                      rs[:, 16:24].unsqueeze(2).to_broadcast([P, 8, 64]), ALU.mult).then_inc(qkn_sb, 1)
                if k == L0F:
                    add_group(k, g, g + 1)
                    group_stats(k, g)
                if k == L1F:
                    dve.wait_ge(t_sb, turned(k, g))
                    wait(dve, g_ps, g)
                    yb = yT[:, :].rearrange("p (b s) -> p b s", s=S)
                    dve.tensor_copy(oddT[:, 0, :, :], yb[:, :, 2:10:2])
                    dve.tensor_copy(oddT[:, 1, :, :], yb[:, :, 10:18:2]).then_inc(odd_sb, 1)
                    dve.wait_ge(e_ps, g + 1)
                    dve.tensor_tensor(Er[:, :, :], PS[0:32, 5, 0:P].unsqueeze(1).to_broadcast([32, 4, P]),
                                      dR[0:32, :].unsqueeze(2).to_broadcast([32, 4, P]), ALU.mult)
                    for c in range(4):
                        r0 = slice(32 * c, 32 * c + 32)
                        ins = dve.tensor_tensor(
                            E2[r0, :, :],
                            PS[r0, 5, P:2 * P].rearrange("p (i c) -> p i c", c=4)[:, :, c].unsqueeze(1).to_broadcast([32, 4, 32]),
                            dR[r0, :].unsqueeze(2).to_broadcast([32, 4, 32]), ALU.mult)
                    ins.then_inc(e_sb, 1)
                    dve.wait_ge(xo_ps, g + 1)
                    dve.tensor_tensor(XO[:, :, :], PS[0:32, 6, :].rearrange("p (b s) -> p b s", s=S),
                                      dB[0:32, :].unsqueeze(2).to_broadcast([32, BPG, S]), ALU.mult).then_inc(xo_sb, 1)
                    if more:
                        norm_group(k, g + 1)
                    dve.wait_ge(g_ps, g + 1)
                    dve.tensor_tensor(GM[:, :, :], PS[:, 6, :].rearrange("p (b s) -> p b s", s=S),
                                      dB[:, :].unsqueeze(2).to_broadcast([P, BPG, S]), ALU.mult).then_inc(g_sb, 1)
                    add_group(k, g, NG + g + 1)
                    group_stats(k, g)
                if k == L2M:
                    dve.wait_ge(lg_ps, g + 1)
                    q = 7 * g
                    lps = PS[:, 6, 0:16].rearrange("p (j e) -> p j e", e=4)
                    dve.tensor_copy(lg[:, :, :], lps)
                    dve.memset(lgz[:, :, :], 0.0).then_inc(gate_v, 1)
                    dve.wait_ge(gate_v, q + 1)
                    dve.tensor_tensor(fin[:, :, :], lg[:, :, :], lg[:, :, :], ALU.is_equal).then_inc(gate_v, 1)
                    dve.wait_ge(gate_v, q + 2)
                    dve.memset(spare[:, 3 * NG:3 * NG + 1], 0.0)
                    dve.copy_predicated(lgz[:, :, :], fin[:, :, :], lg[:, :, :]).then_inc(gate_v, 1)
                    dve.wait_ge(gate_v, q + 3)
                    dve.tensor_scalar(lgz[:, :, :], lgz[:, :, :], -FLT_MAX, FLT_MAX, ALU.max, ALU.min)\
                        .then_inc(n_gate, 1)
                    dve.wait_ge(n_gate, 6 * g + 1)
                    dve.tensor_reduce(gmx[:, :], lgz[:, :, :], AX, ALU.max).then_inc(gate_v, 1)
                    dve.wait_ge(gate_v, q + 4)
                    dve.tensor_tensor(lgz[:, :, :], lgz[:, :, :], gmx[:, :].unsqueeze(2).to_broadcast([P, PPG, 4]),
                                      ALU.subtract).then_inc(gate_v, 1)
                    dve.wait_ge(gate_e, g + 1)
                    dve.tensor_reduce(gs[:, :], lgz[:, :, :], AX, ALU.add).then_inc(n_gate, 1)
                    dve.wait_ge(n_gate, 6 * g + 2)
                    dve.reciprocal(gs[:, :], gs[:, :]).then_inc(n_gate, 1)
                    dve.wait_ge(n_gate, 6 * g + 3)
                    dve.tensor_tensor(lgz[:, :, :], lgz[:, :, :], gs[:, :].unsqueeze(2).to_broadcast([P, PPG, 4]),
                                      ALU.mult).then_inc(n_gate, 1)
                    dve.wait_ge(n_gate, 6 * g + 4)
                    pe_ = lgz[:, :, :].unsqueeze(3).to_broadcast([P, PPG, 4, 4])
                    pj = lgz[:, :, :].unsqueeze(2).to_broadcast([P, PPG, 4, 4])
                    dve.tensor_tensor(cmp[:, :, :, :], pj, pe_, ALU.is_gt)
                    dve.tensor_tensor(tie[:, :, :, :], pj, pe_, ALU.is_equal).then_inc(n_gate, 1)
                    dve.wait_ge(n_gate, 6 * g + 5)
                    dve.tensor_tensor(tie[:, :, :, :], tie[:, :, :, :],
                                      low4[:, :, :].unsqueeze(1).to_broadcast([P, PPG, 4, 4]), ALU.mult).then_inc(n_gate, 1)
                    dve.wait_ge(n_gate, 6 * g + 6)
                    dve.tensor_tensor(cmp[:, :, :, :], cmp[:, :, :, :], tie[:, :, :, :], ALU.add).then_inc(gate_v, 1)
                    dve.wait_ge(gate_v, q + 6)
                    dve.tensor_reduce(rank[:, :, :], cmp[:, :, :, :], AX, ALU.add).then_inc(gate_v, 1)
                    dve.wait_ge(gate_v, q + 7)
                    dve.scalar_tensor_tensor(rank[:, :, :], rank[:, :, :], 2.0, lgz[:, :, :], ALU.is_lt, ALU.mult)\
                        .then_inc(wt_sb, 1)
                    dve.wait_ge(wt_sb, 4 * g + 1)
                    dve.tensor_reduce(gs[:, :], rank[:, :, :], AX, ALU.add).then_inc(wt_sb, 1)
                    dve.wait_ge(wt_sb, 4 * g + 2)
                    dve.tensor_scalar(gs[:, :], gs[:, :], 1e-8, None, ALU.add).then_inc(wt_sb, 1)
                    dve.wait_ge(wt_sb, 4 * g + 3)
                    dve.reciprocal(gmx[:, :], gs[:, :]).then_inc(wt_sb, 1)
                    dve.wait_ge(wt_sb, 4 * g + 4)
                    dve.tensor_tensor(rank[:, :, :], rank[:, :, :], gmx[:, :].unsqueeze(2).to_broadcast([P, PPG, 4]),
                                      ALU.mult).then_inc(w_done, 1)
                    if more:
                        norm_group(k, g + 1)
                    for n, (name, c, dst) in enumerate(MOE_CHUNKS):
                        if name == "e1_w2":
                            dve.wait_ge(h_ps, H_PS[L2M] + NCH * g + n + 1)
                            dve.wait_ge(h_sb, H_SB[L2M] + NACT * g + acts_through(n))
                            dve.tensor_tensor(Hs[:, 4 + c, :], Hs[:, 4 + c, :], PS[:, n % 4, :], ALU.mult).then_inc(h_mul, 1)
                    dve.wait_ge(w_done, g + 1)
                    for n, (_, e, _, _, _) in enumerate(MOE_OUTS):
                        dve.wait_ge(oe_ps, 4 * g + n + 1)
                        for j in range(PPG):
                            o = PS[:, 4 + n % 2, P * j:P * j + P]
                            if n == 0:
                                ins = dve.tensor_scalar(moe[:, j, :], o, rank[:, j, e:e + 1], None, ALU.mult)
                            else:
                                ins = dve.scalar_tensor_tensor(moe[:, j, :], o, rank[:, j, e:e + 1], moe[:, j, :],
                                                               ALU.mult, ALU.add)
                        ins.then_inc(moe_sb, 1)
                        dve.wait_ge(moe_sb, 4 * g + n + 1)
                    dve.tensor_tensor(group(X, g), group(X, g), group(Zr, g), ALU.add).then_inc(x_part, 1)
                    dve.wait_ge(x_part, g + 1)
                    dve.tensor_tensor(group(X, g)[:, :, 32:D], group(X, g)[:, :, 32:D], moe[:, :, 32:D],
                                      ALU.add).then_inc(x_ready, 1)
                    group_stats(k, g)
                if k == L3F:
                    dve.wait_ge(xh_sb, g + 1)
                    dve.tensor_tensor(XL[:, g, :], PS[:, 4:8, :][:, g, :], XH[:, g, :].bitcast(F32), ALU.subtract).then_inc(t_sb, 1)

            def low(j, par, down):
                dve.wait_ge(eh_sb, 4 * j + 2 * par + down + 1)
                c = PART[down]
                dve.tensor_tensor(EL[:, par, c], EW[:, par, c], EH[:, par, c].bitcast(F32), ALU.subtract).then_inc(el_sb, 1)

            def experts_work():
                def hidden_low(u, g):
                    dve.wait_ge(hh_sb, u + 1)
                    dve.tensor_tensor(HL[:, g, :], Hf[:, g, :], HH[:, g, :].bitcast(F32), ALU.subtract).then_inc(hl_sb, 1)

                def chunk(j, par, first, last):
                    for g in range(NG):
                        u = NG * (2 * j + par) + g
                        dve.wait_ge(sg_sb, u + 1)
                        dve.wait_ge(gu_ps, 2 * u + 2)
                        dve.tensor_tensor(Hf[:, g, :], sG[:, g % 2, :], PS[:, 2 + g % 2, :], ALU.mult).then_inc(hf_sb, 1)
                        if g > 0 or not first:
                            hidden_low(u - 1, (g - 1) % NG)
                        if g % 2 == 1 and not first and not last:
                            low(j + par, 1 - par, g // 2)

                chunked(dve, chunk)
                hidden_low(NG * NCH3 - 1, NG - 1)
                for g in range(NG):
                    dve.wait_ge(ot_ps, 2 * NG + g + 1)
                    dve.tensor_tensor(group(X, g), group(X, g), PS[:, g, :].rearrange("p (j d) -> p j d", j=PPG),
                                      ALU.add).then_inc(x_ready, 1)

            for k in range(9):
                if k > 0:
                    dve.wait_ge(x_ready, x_after(k - 1))
                start(k)
                groups(dve, lambda g, more, k=k: group_work(k, g, more))
                if k in ATT:
                    dve.wait_ge(k_sb, NG * (ATT[k] + 1))
                    pairs(k)
            experts_work()

        @block.tensor
        def _(pe):
            pe.wait_ge(dma_small, SMALL)
            for n in range(4):
                ins = pe.matmul(PS[:, 0, P * n:P * n + P], LA[:, n, :], LB[:, n, :], start=True, stop=True)
            ins.then_inc(lora_ps, 1)
            pe.wait_ge(consts_v, 1)
            pe.matmul(PS[0:1, 6, 0:D], col("c_bv"), W1m[:, 3, :], start=True, stop=True).then_inc(lora_ps, 1)

            def turn(k, g, src, t=0, bank=7):
                pe.wait_ge(n_done, done_no(k, g, min(t + 1, NORMS[k] - 1)))
                if bank == 7:
                    wait(pe, t_sb, before(TURNS, k) + TURNS[k] * g + t)
                for j in range(PPG):
                    ins = pe.transpose(PS[:, bank, P * j:P * j + P], src(j), ident[:, :])
                ins.then_inc(t_ps, 1)

            def y_tile(j):
                return y[:, j, :]

            def turn_l3a(g):
                pe.wait_ge(q_sb, NG * 4 + g - 1)
                turn(L3A, g, y_tile)
                turn(L3A, g, lambda j: yy[:, j, :], 1)

            def products_l2f(g):
                pe.wait_ge(t_sb, turned(L2F, g))
                wait(pe, qkn_sb, g)
                for j in range(PPG):
                    ins = pe.matmul(PSf[:, 256 * j:256 * j + 256], yT[:, P * j:P * j + P], w("wqkT"), start=True, stop=True)
                ins.then_inc(q_ps, 1)

            def products_l3a(g):
                pe.wait_ge(t_sb, turned(L3A, g, 1))
                wait(pe, qkn_sb, NG + g)
                wait(pe, v_sb, NG * 4 + g)
                for b in range(BPG):
                    ins = pe.matmul(PSf[:, 256 * b:256 * b + 256], CL[:, b, :, :].rearrange("p a s -> p (a s)"),
                                    w("L3_Wkv"), start=True, stop=True)
                for j in range(PPG):
                    ins = pe.matmul(PS[:, 4, P * j:P * j + P], yT[:, P * j:P * j + P], w("L3_Wq"), start=True, stop=True)
                ins.then_inc(q_ps, 1)

            def first_hidden(g):
                pe.wait_ge(t_sb, turned(L0F, g))
                pe.matmul(PS[0:32, 0, :], w("U1"), yT[:, :], start=True, stop=True).then_inc(h_ps, 1)

            def start(k):
                if k in (L2F, L0F, L1F, L2M):
                    turn(k, 0, y_tile)
                elif k == L3F:
                    for g in range(NG):
                        turn(k, g, lambda j, g=g: y3[:, PPG * g + j, :], bank=4 + g)
                elif k == L3A:
                    turn_l3a(0)
                if k == L0F:
                    first_hidden(0)
                elif k == L2F:
                    products_l2f(0)
                elif k == L3A:
                    products_l3a(0)

            def turn_back(u):
                pe.wait_ge(o_sb, u)
                for j in range(PPG):
                    ins = pe.transpose(PS[:, 5, P * j:P * j + P], oT[:, P * j:P * j + P], ident[:, :])
                ins.then_inc(ot_ps, 1)

            def project(k, g):
                a = ATT[k]
                if k == L0A:
                    wq, wk, wv = w("L0_WQ"), w("L0_WK"), w("L0_WV")
                elif k == L1A:
                    wq, wk, wv = (W1m[:, n, :] for n in range(3))
                else:
                    wq, wk, wv = (BD[:, n, :, :].rearrange("p a b -> p (a b)") for n in range(3))
                if g > 0:
                    turn(k, g, y_tile)
                pe.wait_ge(dma_ctx2[g % 2], 16 * ((NG * a + g) // 2 + 1))
                wait(pe, k_sb, NG * a + g)
                wait(pe, v_sb, NG * a + g)
                ctx = ctx2[:, g % 2, :, :, :]
                pe.matmul(PS[:, 1, :], wk, ctx[:, :, 0, :], start=True, stop=True)
                for b in range(BPG):
                    ins = pe.matmul(PSf[:, 1024 + P * b:1024 + P * b + P], ctx[:, b, :, :].rearrange("p a s -> p (a s)"),
                                    wv, start=True, stop=True)
                ins.then_inc(kv_ps, 1)
                if g == 0:
                    turn(k, g, y_tile)
                pe.wait_ge(t_sb, turned(k, g))
                wait(pe, q_sb, NG * a + g)
                pe.matmul(PS[:, 0, :], wq, yT[:, :], start=True, stop=True).then_inc(q_ps, 1)

            def pairs(k):
                a = ATT[k]
                L3 = k == L3A
                wo = {L0A: w("L0_WO"), L1A: W1m[:, 3, :], L2A: w("L2_WoT"), L2F: w("woT"), L3A: w("L3_Wout")}[k]
                bias = {L1A: 0, L2A: 1, L3A: 2}.get(k)

                def scores(p, par):
                    par = p % 2 if par is None else par
                    pe.wait_ge(kx_v, NPAIR * a + p + 1)
                    pe.wait_ge(kx_p, NPAIR * a + p + 1)
                    pe.wait_ge(qs_sb, NPAIR * a + p + 1)
                    wait(pe, sub_sb, NPAIR * a + p - 1)
                    added = k != L1A
                    if k == L0A:
                        pe.wait_ge(kd_sb, p + 1)
                    for half in range(1 if L3 else 2):
                        n = 256 if L3 else 512
                        for b in range(2):
                            ins = pe.matmul(PS[64 * b:64 * b + 64, 2 * par + half, 0:n], Qs[:, par, 64 * b:64 * b + 64],
                                            Kx[:, par, b, n * half:n * half + n], start=True, stop=not added,
                                            tile_position=(0, 64 * b), skip_group_check=True)
                        dst = PS[:, 2 * par + half, 0:n]
                        if k in (L0A, L2F):
                            ins = pe.matmul(dst, kd[:, par, :] if k == L0A else identb[:, :],
                                            causal[:, :].unsqueeze(1).to_broadcast([P, 8, S]), start=False, stop=True,
                                            skip_group_check=True)
                        if k == L2A:
                            ins = pe.matmul(dst, identb[:, :], mqk[:, p, :].unsqueeze(1).to_broadcast([P, 8, S]),
                                            start=False, stop=True, skip_group_check=True)
                        if L3:
                            ins = pe.matmul(dst.rearrange("p (h k) -> p h k", h=2)[:, :, 0:S], sel2[:, :],
                                            mk[:, p, :].unsqueeze(1).to_broadcast([2, 2, S]),
                                            start=False, stop=True, skip_group_check=True)
                    ins.then_inc(sc_ps, 1)

                def probs(p, par):
                    par = p % 2 if par is None else par
                    n = 1 if L3 else 4
                    pe.wait_ge(exp_sb, NPAIR * a + p + 1)
                    for half in range(2):
                        wait(pe, pt_sb, 2 * (NPAIR * a + p - 1) + half + 1)
                        for i in range(n):
                            c = n * half + i
                            ins = pe.transpose(PS[:, 4 + half, P * i:P * i + P], PR[:, par, P * c:P * c + P], ident[:, :])
                        ins.then_inc(pt_ps, 1)

                def values(p, par):
                    par = p % 2 if par is None else par
                    pe.wait_ge(vz_sb, NPAIR * a + p + 1)
                    pe.wait_ge(pt_sb, 2 * (NPAIR * a + p + 1))
                    wait(pe, ct_sb, NPAIR * a + p)
                    for b in range(2):
                        dst = slice(P * par + 64 * b, P * par + 64 * b + 64)
                        if L3:
                            for h in range(2):
                                ins = pe.matmul(PS[64 * h:64 * h + 64, 6, dst], Vz[:, par, b, 64 * h:64 * h + 64],
                                                PT[:, par, h, 64 * b:64 * b + 64], start=True, stop=True,
                                                tile_position=(0, 64 * h))
                        else:
                            for t in range(2):
                                for j in range(4):
                                    n = 2 * j + t
                                    ins = pe.matmul(PS[32 * j:32 * j + 32, 6, dst],
                                                    Vz[:, par, b, 48 * n - 16 * t:48 * n - 16 * t + 32],
                                                    PT[:, par, n, 64 * b:64 * b + 64], start=t == 0, stop=t == 1,
                                                    tile_position=(0, 32 * j), skip_group_check=True)
                    dst = slice(256 + P * par, 256 + P * par + P)
                    if L3:
                        for h in range(2):
                            ins = pe.matmul(PS[64 * h:64 * h + 64, 6, dst], ones[:, 0:64], PT[:, par, h, :], start=True,
                                            stop=True, tile_position=(0, 64 * h))
                    else:
                        for t in range(2):
                            for j in range(4):
                                n = 2 * j + t
                                ins = pe.matmul(PS[32 * j:32 * j + 32, 6, dst], Oz[:, 48 * n - 16 * t:48 * n - 16 * t + 32],
                                                PT[:, par, n, :], start=t == 0, stop=t == 1,
                                                tile_position=(0, 32 * j), skip_group_check=True)
                    ins.then_inc(pv_ps, 1)

                def output(p, par):
                    par = p % 2 if par is None else par
                    pe.wait_ge(ct_sb, NPAIR * a + p + 1)
                    wait(pe, x_ready, x_after(k) - NPAIR + p)
                    dst = PS[:, 7, P * par:P * par + P]
                    ins = pe.matmul(dst, cT[:, par, :], wo, start=True, stop=bias is None)
                    if bias is not None:
                        ins = pe.matmul(dst, ones[0:1, :], ROWS[:, D * bias:D * bias + D], start=False, stop=True)
                    ins.then_inc(o_ps, 1)

                if k == L0A:
                    pe.wait_ge(row_sb, 1)
                pipelined(pe, [(0, scores), (2, values), (1, probs), (3, output)])

            def group_work(k, g, more):
                if k == L2F:
                    wait(pe, v_sb, NG * 3 + g)
                    for b in range(BPG):
                        ins = pe.matmul(PSf[:, 1024 + P * b:1024 + P * b + P], yT2[:, b, :, :].rearrange("p a s -> p (a s)"),
                                        w("wvT"), start=True, stop=True)
                    ins.then_inc(kv_ps, 1)
                    if more:
                        turn(k, g + 1, y_tile)
                    pe.wait_ge(qkn_sb, g + 1)
                    if more:
                        products_l2f(g + 1)
                    wait(pe, k_sb, NG * 3 + g)
                    for j in range(PPG):
                        for i in range(2):
                            ins = pe.transpose(PS[:, 5 + i, P * j:P * j + P], qkn[:, 256 * j + P * i:256 * j + P * i + P], ident[:, :])
                    ins.then_inc(qk_turned, 1)
                elif k == L3A:
                    if more:
                        turn_l3a(g + 1)
                    pe.wait_ge(qkn_sb, NG + g + 1)
                    if more:
                        products_l3a(g + 1)
                    wait(pe, k_sb, NG * 4 + g)
                    for b in range(BPG):
                        pe.transpose(PSf[:, 2560 + P * b:2560 + P * b + P], qkn[:, P * b:P * b + P], ident[:, :])
                    for j in range(PPG):
                        ins = pe.transpose(PS[:, 7, P * j:P * j + P], qkn[:, 1024 + P * j:1024 + P * j + P], ident[:, :])
                    ins.then_inc(qk_turned, 1)
                elif k == L0F:
                    u = 6 * g
                    pe.wait_ge(h_sb, u + 1)
                    for c in range(4):
                        pe.matmul(PS[:, (1 + c) % 4, :], w("V1", c, rows_=32), Hs[0:32, 0, :], start=True, stop=True).then_inc(h_ps, 1)
                    if more:
                        turn(k, g + 1, y_tile)
                    wait(pe, x_ready, x_after(k - 1) + g)
                    for c in range(4):
                        pe.wait_ge(h_sb, u + 2 + c)
                        ins = pe.matmul(PS[0:32, 5, :], w("U2", c, 32), Hs[:, 1 + c, :], start=c == 0, stop=c == 3)
                    ins.then_inc(h_ps, 1)
                    if more:
                        first_hidden(g + 1)
                    pe.wait_ge(h_sb, u + 6)
                    pe.matmul(PS[:, 4, :], w("V2", rows_=32), Hs[0:32, 5, :], start=True, stop=True).then_inc(acc_ps, 1)
                    turn_back(g + 1)
                elif k == L1F:
                    pe.wait_ge(x_ready, x_after(k - 1) + g)
                    for j in range(PPG):
                        pe.matmul(PS[0:32, 5, 0:P], Sel1[:, j, :, :].rearrange("p b r -> p (b r)"), y[:, j, :], start=j == 0, stop=j == 3)
                    for j in range(PPG):
                        ins = pe.matmul(PS[:, 5, P:2 * P], Sel2[:, j, :, :].rearrange("p c r -> p (c r)"), y[:, j, :], start=j == 0, stop=j == 3)
                    ins.then_inc(e_ps, 1)
                    pe.wait_ge(odd_sb, g + 1)
                    pe.matmul(PS[0:32, 6, :], oddT[:, 0, :, :].rearrange("p b r -> p (b r)"), yT[:, :], start=True, stop=True).then_inc(xo_ps, 1)
                    for c in range(4):
                        pe.matmul(PS[:, c, :], w("W1T", c), yT[:, :], start=True, stop=False)
                    pe.wait_ge(e_sb, g + 1)
                    pe.wait_ge(xo_sb, g + 1)
                    for c in range(4):
                        pe.matmul(PS[:, c, :], Er[:, c, :], XO[:, :, :].rearrange("p b s -> p (b s)"), start=False, stop=True).then_inc(h_ps, 1)
                    if more:
                        turn(k, g + 1, y_tile)
                    u = H_SB[L1F] + 4 * g
                    for c in range(4):
                        pe.wait_ge(h_sb, u + 1 + c)
                        ins = pe.matmul(PS[32 * c:32 * c + 32, 6, :], oddT[:, 1, :, :].rearrange("p b r -> p (b r)"), Hs[:, c, :],
                                        start=True, stop=True, tile_position=(0, 32 * c))
                    ins.then_inc(g_ps, 1)
                    for c in range(4):
                        pe.matmul(PS[:, 4, :], w("W2T", c), Hs[:, c, :], start=c == 0, stop=False)
                    pe.wait_ge(g_sb, g + 1)
                    pe.matmul(PS[:, 4, :], E2[:, :, :].rearrange("p r i -> p (r i)"), GM[:, :, :].rearrange("p b s -> p (b s)"),
                              start=False, stop=True).then_inc(acc_ps, 1)
                    turn_back(NG + g + 1)
                elif k == L2M:
                    pe.wait_ge(t_sb, turned(k, g))
                    wait(pe, h_mul, 2 * g)
                    pe.wait_ge(h_sb, H_SB[L2M] + NACT * g)
                    for j in range(PPG):
                        ins = pe.matmul(PS[:, 6, 4 * j:4 * j + 4], yT[:, P * j:P * j + P], w("gateT"), start=True, stop=True)
                    ins.then_inc(lg_ps, 1)
                    for n, (name, c, _) in enumerate(MOE_CHUNKS):
                        if n >= 4:
                            if MOE_CHUNKS[n - 4][2] is None:
                                pe.wait_ge(h_mul, 2 * g + 1 + MOE_CHUNKS[n - 4][1])
                            else:
                                pe.wait_ge(h_sb, H_SB[L2M] + NACT * g + acts_through(n - 4))
                        if name in MOE_IN:
                            ins_, last = MOE_IN[name]
                            pe.wait_ge(h_sb, H_SB[L2M] + NACT * g + acts_through(last))
                            for i, hsrc in enumerate(ins_):
                                ins = pe.matmul(PS[:, n % 4, :], w(name, 2 * i + c), Hs[:, hsrc, :], start=i == 0,
                                                stop=i == len(ins_) - 1)
                        else:
                            ins = pe.matmul(PS[:, n % 4, :], w(name, c), yT[:, :], start=True, stop=True)
                        ins.then_inc(h_ps, 1)
                        if more and n == NCH - 1:
                            turn(k, g + 1, y_tile)
                        for m, (after, e, wname, hs, last) in enumerate(MOE_OUTS):
                            if after != n:
                                continue
                            wait(pe, moe_sb, 4 * g + m - 1)
                            if e == 1:
                                pe.wait_ge(h_mul, 2 * g + 2)
                            pe.wait_ge(h_sb, H_SB[L2M] + NACT * g + acts_through(last))
                            for j in range(PPG):
                                for i in range(2):
                                    ins = pe.matmul(PS[:, 4 + m % 2, P * j:P * j + P], Hs[:, hs[i], P * j:P * j + P],
                                                    w(wname, i), start=i == 0, stop=i == 1)
                            ins.then_inc(oe_ps, 1)

            def experts_work():
                def product(dst, n, par, hi, lo, start, stop):
                    wh, wl = EH[:, par, P * n:P * n + P], EL[:, par, P * n:P * n + P]
                    pe.matmul(dst, wh, hi, start=start, stop=False)
                    pe.matmul(dst, wh, lo, start=False, stop=False)
                    return pe.matmul(dst, wl, hi, start=False, stop=stop)

                def downs(v, par, g, start, stop):
                    pe.wait_ge(hl_sb, v + 1)
                    product(PS[:, 4 + g, :], 2, par, HH[:, g, :], HL[:, g, :], start, stop).then_inc(d_ps, 1)

                def chunk(j, par, first, last):
                    pe.wait_ge(el_sb, 4 * j + 2 * par + 1)
                    for g in range(NG):
                        u = NG * (2 * j + par) + g
                        if first:
                            pe.wait_ge(t_sb, turned(L3F, g))
                        if g >= 2 or not first:
                            pe.wait_ge(hf_sb, u - 1)
                        product(PS[:, g % 2, :], 0, par, XH[:, g, :], XL[:, g, :], True, True).then_inc(gu_ps, 1)
                        product(PS[:, 2 + g % 2, :], 1, par, XH[:, g, :], XL[:, g, :], True, True).then_inc(gu_ps, 1)
                        if g == LAG3:
                            pe.wait_ge(el_sb, 4 * j + 2 * par + 2)
                        if g >= LAG3:
                            downs(u - LAG3, par, g - LAG3, first, last)
                        elif not first:
                            downs(u - LAG3, 1 - par, g + NG - LAG3, isinstance(j, int) and 2 * j + par == 1, False)

                chunked(pe, chunk)
                for g in range(NG - LAG3, NG):
                    downs(NG * (NCH3 - 1) + g, 1, g, False, True)
                pe.wait_ge(hf_sb, NG * NCH3)
                for g in range(NG):
                    pe.wait_ge(o_sb, 2 * NG + g + 1)
                    for i in range(PPG):
                        ins = pe.transpose(PS[:, g, P * i:P * i + P], oT3[:, g, P * i:P * i + P], ident[:, :])
                    ins.then_inc(ot_ps, 1)

            for k in range(9):
                if k > 0:
                    pe.wait_ge(x_ready, x_after(k - 1))
                if k == L0F:
                    pe.wait_ge(dma_rest, 16)
                start(k)
                if k in TOK:
                    for g in range(NG):
                        project(k, g)
                elif k != L3F:
                    groups(pe, lambda g, more, k=k: group_work(k, g, more))
                if k in ATT:
                    pairs(k)
            experts_work()


def kernel(**inputs):
    import numpy as np
    import concourse.bacc as bacc
    from concourse import mybir as mb
    from concourse.bass_utils import run_bass_kernel_spmd

    a = {k: np.asarray(v) for k, v in inputs.items()}
    f = np.float32

    def chunks(m):
        return m.reshape(-1, 128, m.shape[1]).transpose(1, 0, 2).reshape(128, -1)

    def low(m):
        return np.concatenate([m, np.zeros((128 - m.shape[0], m.shape[1]), f)])

    def col(v):
        return v.reshape(-1, 128).T

    cols = {
        "L0_WQ": a["L0_xattn_WQ"], "L0_WK": a["L0_xattn_WK"], "L0_WV": a["L0_xattn_WV"], "L0_WO": a["L0_xattn_WO"],
        "U1": a["L0_ffn_U1"], "V1": low(a["L0_ffn_V1"]), "U2": chunks(a["L0_ffn_U2"]), "V2": low(a["L0_ffn_V2"]),
        "L1_Wq": a["L1_xattn_Wq"], "L1_Wk": a["L1_xattn_Wk"], "L1_Wv": a["L1_xattn_Wv"], "L1_Wo": a["L1_xattn_Wo"],
        "W1T": a["L1_ffn_W1"].T, "W2T": chunks(a["L1_ffn_W2"].T),
        "L2_q": np.tile(a["L2_xattn_Wq"].T, (16, 1)), "L2_k": np.tile(a["L2_xattn_Wk"].T, (16, 1)),
        "L2_v": np.tile(a["L2_xattn_Wv"].T, (16, 1)), "L2_WoT": a["L2_xattn_Wo"].T,
        "wqkT": np.concatenate([a["L2_ffn_wq"].T, a["L2_ffn_wk"].T], 1), "wvT": a["L2_ffn_wv"].T,
        "woT": a["L2_ffn_wo"].T, "gateT": a["L2_ffn_gate_w"].T,
        "e0_up": a["L2_ffn_e0_up"].T, "e0_down": chunks(a["L2_ffn_e0_down"].T),
        "e1_w1": a["L2_ffn_e1_w1"].T, "e1_w2": a["L2_ffn_e1_w2"].T, "e1_down": chunks(a["L2_ffn_e1_down"].T),
        "e2_l1": a["L2_ffn_e2_l1"].T, "e2_l2": chunks(a["L2_ffn_e2_l2"].T), "e2_l3": chunks(a["L2_ffn_e2_l3"].T),
        "e2_l4": chunks(a["L2_ffn_e2_l4"].T),
        "e3_down": a["L2_ffn_e3_down"].T, "e3_up": a["L2_ffn_e3_up"].T, "e3_out": chunks(a["L2_ffn_e3_out"].T),
        "L3_Wq": a["L3_xattn_W_q"], "L3_Wkv": a["L3_xattn_W_kv"], "L3_Wout": a["L3_xattn_W_out"],
        "c_L0b1": col(a["L0_ffn_b1"]), "c_L0b2": col(a["L0_ffn_b2"]),
        "c_bq": col(a["L1_xattn_bq"]), "c_bk": col(a["L1_xattn_bk"]), "c_bv": col(a["L1_xattn_bv"]),
        "c_L1b1": col(a["L1_ffn_b1"]), "c_L1b2": col(a["L1_ffn_b2"]),
        "c_n1": col(a["L2_ffn_n1_w"]), "c_n2": col(a["L2_ffn_n2_w"]),
        "c_qn": col(np.tile(a["L2_ffn_qn_w"], 16)), "c_kn": col(np.tile(a["L2_ffn_kn_w"], 16)),
        "c_lxg": col(a["L3_xattn_ln_x_g"]), "c_lxb": col(a["L3_xattn_ln_x_b"]),
        "c_llg": col(a["L3_xattn_ln_l_g"]), "c_llb": col(a["L3_xattn_ln_l_b"]),
        "c_qg": col(np.tile(a["L3_xattn_q_gamma"], 2)), "c_kg": col(np.tile(a["L3_xattn_k_gamma"], 2)),
        "c_scale": np.tile(a["L1_ffn_scale"].reshape(1, 1), (128, 1)),
    }
    ctx = a["ctx_1024"]
    bools = np.zeros((B, S, 4), np.uint8)
    bools[:, :, 0] = a["mask_BxS2_bk0"].view(np.uint8)
    ctx_T = ctx.transpose(2, 0, 1).reshape(128, NG, BPG, 1, S)
    arrays = {
        "x": a["x"].reshape(NPAIR, P, D).transpose(1, 0, 2),
        "ctx_tok": ctx.reshape(NPAIR, P, D).transpose(1, 0, 2),
        "ctx_T2": np.concatenate([ctx_T, ctx_T], 3),
        "mask_q": a["mask_BxS2_ik0"].reshape(NPAIR, P).T,
        "mask_qk": a["mask_Bx1xSxS2_if1"].reshape(NPAIR, P, S).transpose(1, 0, 2),
        "mask_key": bools.view(np.int32).reshape(NPAIR, 2, S).transpose(1, 0, 2),
        "pack": np.concatenate([cols[n] for n, _ in PACK], 1),
        "rows": np.concatenate([a["L1_xattn_bo"], a["L2_xattn_bo"], a["L3_xattn_b_out"]]).reshape(1, 384),
        "lora_A": np.stack([a["L1_xattn_A" + n].T for n in "qkvo"], 1),
        "lora_B": np.stack([a["L1_xattn_B" + n] for n in "qkvo"], 1),
        "experts": np.stack([a["L3_ffn_Wg"].reshape(8, P, 4, P).transpose(1, 0, 2, 3).reshape(P, NCH3, P),
                             a["L3_ffn_Wu"].reshape(8, P, 4, P).transpose(1, 0, 2, 3).reshape(P, NCH3, P),
                             a["L3_ffn_Wd"].reshape(NCH3, P, P).transpose(1, 0, 2)], 2).reshape(P, NCH3, 3 * P),
    }
    nc = bacc.Bacc("TRN2", target_bir_lowering=False, num_devices=1)
    feed, args = {}, {}
    for name, v in arrays.items():
        v = np.ascontiguousarray(v)
        feed[name + "_dram"] = v
        args[name] = nc.dram_tensor(name + "_dram", v.shape, mb.dt.from_np(v.dtype), kind="ExternalInput").ap()
    args["out"] = nc.dram_tensor("out_dram", (P, NPAIR, D), mb.dt.from_np(np.dtype("float32")), kind="ExternalOutput").ap()
    build_program(nc, **args)
    r = run_bass_kernel_spmd(nc, [feed], core_ids=[0])
    got = r.results[0]["out_dram"]
    return got.transpose(1, 0, 2).reshape(B, S, D)
```
